# Optimizing a Trainium2 kernel written in Bass

```python
import numpy as np
import jax
import jax.numpy as jnp

def _softmax(x, axis=-1):
    return jax.nn.softmax(x, axis=axis)

def _gelu(x):
    return jax.nn.gelu(x, approximate=True)

def _silu(x):
    return jax.nn.silu(x)

def _sigmoid(x):
    return jax.nn.sigmoid(x)

def _layernorm(x, axis=-1, eps=1e-05):
    m = jnp.mean(x, axis=axis, keepdims=True)
    v = jnp.var(x, axis=axis, keepdims=True)
    return (x - m) / jnp.sqrt(v + eps)

def _scatter_add(tgt, idx, src, axis=0):
    return tgt.at[idx].add(src)

def _segment_sum(src, seg, n):
    return jax.ops.segment_sum(src, seg, n)
kernel_name = 'mk_lm_tower_d2_tok_ids1024_r4_29f77e'

def setup_inputs(seed: int=0):
    np.random.seed(seed)
    _w = jnp.asarray

    def _rec_inputs():
        import jax
        import jax.numpy as jnp
        _rk = jax.random.key(seed)
        x = jax.random.randint(jax.random.fold_in(_rk, 1), (64, 128), 0, 28, jnp.int32)
        mask_BS_i1_0 = jnp.where(jnp.ones((64, 128), dtype=bool), 1, 0).astype(jnp.int32)
        return (x, mask_BS_i1_0)
    x, mask_BS_i1_0 = _rec_inputs()

    def _L0_tok_setup():
        import jax, jax.numpy as jnp
        import numpy as np
        WINDOW_SIZE = 3
        LN_EPS = 1e-05

        def _sliding_window_features(base_pca, mask_f):
            B, S, F = base_pca.shape
            h = WINDOW_SIZE // 2
            idx = jnp.arange(S)
            start = jnp.maximum(idx - h, 0)
            end = jnp.minimum(idx + h + 1, S)
            masked = base_pca * mask_f[..., None]
            csum = jnp.pad(jnp.cumsum(masked, axis=1), ((0, 0), (1, 0), (0, 0)))
            wsum = csum[:, end, :] - csum[:, start, :]
            mcs = jnp.pad(jnp.cumsum(mask_f, axis=1), ((0, 0), (1, 0)))
            lengths = jnp.maximum(mcs[:, end] - mcs[:, start], 1.0)
            return wsum / lengths[..., None]
        key = jax.random.key(seed)
        ks = jax.random.split(key, 8)
        B, S, V, E = (8, 1024, 28, 256)
        input_ids = jax.random.randint(ks[0], (B, S), 0, V, dtype=jnp.int64)
        attention_mask = jnp.ones((B, S), dtype=jnp.int32)
        emb = jax.random.normal(ks[1], (V, E), dtype=jnp.float32) * 0.02
        emb = emb.at[0].set(0.0)
        pca_lookup = jax.random.normal(ks[2], (V, 20), dtype=jnp.float32)
        proj_w = jax.random.normal(ks[3], (20, E), dtype=jnp.float32) * 0.2
        proj_b = jnp.zeros((E,), dtype=jnp.float32)
        fus_w = jax.random.normal(ks[4], (2 * E, E), dtype=jnp.float32) * 0.02
        fus_b = jnp.zeros((E,), dtype=jnp.float32)
        ln_g = jnp.ones((E,), dtype=jnp.float32)
        ln_b = jnp.zeros((E,), dtype=jnp.float32)
        return {'input_ids': input_ids, 'attention_mask': attention_mask, 'emb': emb, 'pca_lookup': pca_lookup, 'proj_w': proj_w, 'proj_b': proj_b, 'fus_w': fus_w, 'fus_b': fus_b, 'ln_g': ln_g, 'ln_b': ln_b}
    _L0_tok_all = _L0_tok_setup()
    _L0_tok_in = {k: v for k, v in _L0_tok_all.items() if k in ('emb', 'pca_lookup', 'proj_w', 'proj_b', 'fus_w', 'fus_b', 'ln_g', 'ln_b')}
    del _L0_tok_all

    def _L0_attn_setup():
        import jax, jax.numpy as jnp
        import numpy as np
        N_HEADS = 16
        HEAD_DIM = 64
        ROPE_THETA = 10000.0
        EPS = 1e-06

        def _rmsnorm(x, w):
            rms = jnp.sqrt(jnp.mean(jnp.square(x), axis=-1, keepdims=True) + EPS)
            return x / rms * w

        def _rope(x, cos, sin):
            x1, x2 = jnp.split(x, 2, axis=-1)
            return jnp.concatenate([x1 * cos - x2 * sin, x1 * sin + x2 * cos], axis=-1)
        key = jax.random.key(seed)
        ks = jax.random.split(key, 3)
        B, T, C = (2, 512, 256)
        x = jax.random.normal(ks[0], (B, T, C), dtype=jnp.float32)
        wqkv = jax.random.normal(ks[1], (3 * N_HEADS * HEAD_DIM, C), dtype=jnp.float32) * C ** (-0.5)
        wo = jax.random.normal(ks[2], (C, N_HEADS * HEAD_DIM), dtype=jnp.float32) * (N_HEADS * HEAD_DIM) ** (-0.5)
        q_norm_w = jnp.ones((HEAD_DIM,), dtype=jnp.float32)
        k_norm_w = jnp.ones((HEAD_DIM,), dtype=jnp.float32)
        return {'x': x, 'wqkv': wqkv, 'wo': wo, 'q_norm_w': q_norm_w, 'k_norm_w': k_norm_w}
    _L0_attn_all = _L0_attn_setup()
    _L0_attn_in = {k: v for k, v in _L0_attn_all.items() if k in ('wqkv', 'wo', 'q_norm_w', 'k_norm_w')}
    del _L0_attn_all

    def _L0_ffn_setup():
        import jax, jax.numpy as jnp
        import numpy as np
        D_MODEL = 256
        NUM_HEADS = 4
        NUM_EXPERTS = 8
        TOP_K = 2
        D_FF = 256
        EPS = 1e-06

        def _rmsnorm(x, g):
            return x * jax.lax.rsqrt(jnp.mean(x * x, axis=-1, keepdims=True) + EPS) * g

        def _swiglu(x, w1, w2, w3):
            return jax.nn.silu(x @ w1.T) * (x @ w3.T) @ w2.T
        key = jax.random.key(seed)
        ks = jax.random.split(key, 16)
        d, e, f = (D_MODEL, NUM_EXPERTS, D_FF)
        dc = d // 4
        s = 0.02
        return {'X': jax.random.normal(ks[0], (2, 256, d), dtype=jnp.float32), 'g1': jnp.ones((d,), jnp.float32), 'g2': jnp.ones((d,), jnp.float32), 'Wq': jax.random.normal(ks[1], (d, d), jnp.float32) * s, 'Wkc': jax.random.normal(ks[2], (dc, d), jnp.float32) * s, 'Wvc': jax.random.normal(ks[3], (dc, d), jnp.float32) * s, 'Wo': jax.random.normal(ks[4], (d, d), jnp.float32) * s, 'Wr': jax.random.normal(ks[5], (e, d), jnp.float32) * s, 'expert_bias': jnp.zeros((e,), jnp.float32), 'sW1': jax.random.normal(ks[6], (f, d), jnp.float32) * s, 'sW2': jax.random.normal(ks[7], (d, f), jnp.float32) * s, 'sW3': jax.random.normal(ks[8], (f, d), jnp.float32) * s, 'eW1': jax.random.normal(ks[9], (e, f, d), jnp.float32) * s, 'eW2': jax.random.normal(ks[10], (e, d, f), jnp.float32) * s, 'eW3': jax.random.normal(ks[11], (e, f, d), jnp.float32) * s}
    _L0_ffn_all = _L0_ffn_setup()
    _L0_ffn_in = {k: v for k, v in _L0_ffn_all.items() if k in ('g1', 'g2', 'Wq', 'Wkc', 'Wvc', 'Wo', 'Wr', 'expert_bias', 'sW1', 'sW2', 'sW3', 'eW1', 'eW2', 'eW3')}
    del _L0_ffn_all

    def _L1_attn_setup():
        import jax, jax.numpy as jnp
        import numpy as np
        import math
        B, S, E, H = (2, 512, 256, 8)
        Dh = E // H

        def _pos_encoding(s, e):
            pos = jnp.arange(s, dtype=jnp.float32)[:, None]
            div = jnp.exp(jnp.arange(0, e, 2, dtype=jnp.float32) * (-math.log(10000.0) / e))
            pe = jnp.zeros((s, e), jnp.float32)
            pe = pe.at[:, 0::2].set(jnp.sin(pos * div))
            pe = pe.at[:, 1::2].set(jnp.cos(pos * div))
            return pe

        def _rel_shift(ps):
            b, h, s1, s2 = ps.shape
            padded = jnp.pad(ps, ((0, 0), (0, 0), (0, 0), (1, 0)))
            return padded.reshape(b, h, s2 + 1, s1)[:, :, 1:, :].reshape(b, h, s1, s2)

        def _forward(inputs, ln_gamma, ln_beta, Wq, bq, Wk, bk, Wv, bv, Wp, u_bias, v_bias, Wo, bo):
            b, s, e = inputs.shape
            mu = inputs.mean(-1, keepdims=True)
            var = inputs.var(-1, keepdims=True)
            xn = (inputs - mu) / jnp.sqrt(var + 1e-05) * ln_gamma + ln_beta
            xh = xn.reshape(b, s, H, Dh)
            q = xh @ Wq + bq
            k = xh @ Wk + bk
            v = xh @ Wv + bv
            pe = _pos_encoding(s, e).reshape(s, H, Dh)
            p = pe @ Wp
            content = jnp.einsum('bqhd,bkhd->bhqk', q + u_bias, k)
            pos_score = jnp.einsum('bqhd,khd->bhqk', q + v_bias, p)
            pos_score = _rel_shift(pos_score)
            score = (content + pos_score) / jnp.sqrt(jnp.float32(e))
            attn = jax.nn.softmax(score, axis=-1)
            ctx = jnp.einsum('bhqk,bkhd->bqhd', attn, v).reshape(b, s, e)
            return ctx @ Wo + bo
        key = jax.random.key(seed)
        ks = jax.random.split(key, 9)
        g = lambda k, shp: jax.random.normal(k, shp, jnp.float32) * 0.02
        return {'inputs': jax.random.normal(ks[0], (B, S, E), jnp.float32), 'ln_gamma': jnp.ones((E,), jnp.float32), 'ln_beta': jnp.zeros((E,), jnp.float32), 'Wq': g(ks[1], (Dh, Dh)), 'bq': jnp.zeros((Dh,), jnp.float32), 'Wk': g(ks[2], (Dh, Dh)), 'bk': jnp.zeros((Dh,), jnp.float32), 'Wv': g(ks[3], (Dh, Dh)), 'bv': jnp.zeros((Dh,), jnp.float32), 'Wp': g(ks[4], (Dh, Dh)), 'u_bias': g(ks[5], (H, Dh)), 'v_bias': g(ks[6], (H, Dh)), 'Wo': g(ks[7], (E, E)), 'bo': jnp.zeros((E,), jnp.float32)}
    _L1_attn_all = _L1_attn_setup()
    _L1_attn_in = {k: v for k, v in _L1_attn_all.items() if k in ('ln_gamma', 'ln_beta', 'Wq', 'bq', 'Wk', 'bk', 'Wv', 'bv', 'Wp', 'u_bias', 'v_bias', 'Wo', 'bo')}
    del _L1_attn_all

    def _L1_ffn_setup():
        import jax, jax.numpy as jnp
        import numpy as np
        B, S, D_IN, D_OUT = (16, 1024, 256, 256)
        ACT_BITS = 8
        QB = float(2 ** (ACT_BITS - 1) - 1)
        key = jax.random.key(seed)
        k1, k2, k3 = jax.random.split(key, 3)
        x = jax.random.normal(k1, (B, S, D_IN), dtype=jnp.float32)
        ternary_weight = jax.random.randint(k2, (D_OUT, D_IN), 0, 3, dtype=jnp.int32)
        bias = jax.random.normal(k3, (D_OUT,), dtype=jnp.float32)
        act_scale = (jnp.max(jnp.abs(x)) / QB).astype(jnp.float32)
        return {'x': x, 'ternary_weight': ternary_weight, 'bias': bias, 'act_scale': act_scale}
    _L1_ffn_all = _L1_ffn_setup()
    _L1_ffn_in = {k: v for k, v in _L1_ffn_all.items() if k in ('ternary_weight', 'bias', 'act_scale')}
    del _L1_ffn_all
    return {'x': x, 'mask_BS_i1_0': mask_BS_i1_0, 'L0_tok_emb': _L0_tok_in['emb'], 'L0_tok_pca_lookup': _L0_tok_in['pca_lookup'], 'L0_tok_proj_w': _L0_tok_in['proj_w'], 'L0_tok_proj_b': _L0_tok_in['proj_b'], 'L0_tok_fus_w': _L0_tok_in['fus_w'], 'L0_tok_fus_b': _L0_tok_in['fus_b'], 'L0_tok_ln_g': _L0_tok_in['ln_g'], 'L0_tok_ln_b': _L0_tok_in['ln_b'], 'L0_attn_wqkv': _L0_attn_in['wqkv'], 'L0_attn_wo': _L0_attn_in['wo'], 'L0_attn_q_norm_w': _L0_attn_in['q_norm_w'], 'L0_attn_k_norm_w': _L0_attn_in['k_norm_w'], 'L0_ffn_g1': _L0_ffn_in['g1'], 'L0_ffn_g2': _L0_ffn_in['g2'], 'L0_ffn_Wq': _L0_ffn_in['Wq'], 'L0_ffn_Wkc': _L0_ffn_in['Wkc'], 'L0_ffn_Wvc': _L0_ffn_in['Wvc'], 'L0_ffn_Wo': _L0_ffn_in['Wo'], 'L0_ffn_Wr': _L0_ffn_in['Wr'], 'L0_ffn_expert_bias': _L0_ffn_in['expert_bias'], 'L0_ffn_sW1': _L0_ffn_in['sW1'], 'L0_ffn_sW2': _L0_ffn_in['sW2'], 'L0_ffn_sW3': _L0_ffn_in['sW3'], 'L0_ffn_eW1': _L0_ffn_in['eW1'], 'L0_ffn_eW2': _L0_ffn_in['eW2'], 'L0_ffn_eW3': _L0_ffn_in['eW3'], 'L1_attn_ln_gamma': _L1_attn_in['ln_gamma'], 'L1_attn_ln_beta': _L1_attn_in['ln_beta'], 'L1_attn_Wq': _L1_attn_in['Wq'], 'L1_attn_bq': _L1_attn_in['bq'], 'L1_attn_Wk': _L1_attn_in['Wk'], 'L1_attn_bk': _L1_attn_in['bk'], 'L1_attn_Wv': _L1_attn_in['Wv'], 'L1_attn_bv': _L1_attn_in['bv'], 'L1_attn_Wp': _L1_attn_in['Wp'], 'L1_attn_u_bias': _L1_attn_in['u_bias'], 'L1_attn_v_bias': _L1_attn_in['v_bias'], 'L1_attn_Wo': _L1_attn_in['Wo'], 'L1_attn_bo': _L1_attn_in['bo'], 'L1_ffn_ternary_weight': _L1_ffn_in['ternary_weight'], 'L1_ffn_bias': _L1_ffn_in['bias'], 'L1_ffn_act_scale': _L1_ffn_in['act_scale']}

def reference(x, mask_BS_i1_0, L0_tok_emb, L0_tok_pca_lookup, L0_tok_proj_w, L0_tok_proj_b, L0_tok_fus_w, L0_tok_fus_b, L0_tok_ln_g, L0_tok_ln_b, L0_attn_wqkv, L0_attn_wo, L0_attn_q_norm_w, L0_attn_k_norm_w, L0_ffn_g1, L0_ffn_g2, L0_ffn_Wq, L0_ffn_Wkc, L0_ffn_Wvc, L0_ffn_Wo, L0_ffn_Wr, L0_ffn_expert_bias, L0_ffn_sW1, L0_ffn_sW2, L0_ffn_sW3, L0_ffn_eW1, L0_ffn_eW2, L0_ffn_eW3, L1_attn_ln_gamma, L1_attn_ln_beta, L1_attn_Wq, L1_attn_bq, L1_attn_Wk, L1_attn_bk, L1_attn_Wv, L1_attn_bv, L1_attn_Wp, L1_attn_u_bias, L1_attn_v_bias, L1_attn_Wo, L1_attn_bo, L1_ffn_ternary_weight, L1_ffn_bias, L1_ffn_act_scale):
    import jax
    import jax.numpy as jnp

    def _L0_tok_ref(input_ids, attention_mask, emb, pca_lookup, proj_w, proj_b, fus_w, fus_b, ln_g, ln_b):
        import jax, jax.numpy as jnp
        import numpy as np
        WINDOW_SIZE = 3
        LN_EPS = 1e-05

        def _sliding_window_features(base_pca, mask_f):
            B, S, F = base_pca.shape
            h = WINDOW_SIZE // 2
            idx = jnp.arange(S)
            start = jnp.maximum(idx - h, 0)
            end = jnp.minimum(idx + h + 1, S)
            masked = base_pca * mask_f[..., None]
            csum = jnp.pad(jnp.cumsum(masked, axis=1), ((0, 0), (1, 0), (0, 0)))
            wsum = csum[:, end, :] - csum[:, start, :]
            mcs = jnp.pad(jnp.cumsum(mask_f, axis=1), ((0, 0), (1, 0)))
            lengths = jnp.maximum(mcs[:, end] - mcs[:, start], 1.0)
            return wsum / lengths[..., None]
        token_embeds = emb[input_ids]
        base_pca = pca_lookup[input_ids]
        pca_feat = _sliding_window_features(base_pca, attention_mask.astype(jnp.float32))
        cont = pca_feat @ proj_w + proj_b
        combined = jnp.concatenate([token_embeds, cont], axis=-1)
        fused = combined @ fus_w + fus_b
        mu = jnp.mean(fused, axis=-1, keepdims=True)
        var = jnp.mean(jnp.square(fused - mu), axis=-1, keepdims=True)
        return (fused - mu) * jax.lax.rsqrt(var + LN_EPS) * ln_g + ln_b

    def _L0_attn_ref(x, wqkv, wo, q_norm_w, k_norm_w):
        import jax, jax.numpy as jnp
        import numpy as np
        N_HEADS = 16
        HEAD_DIM = 64
        ROPE_THETA = 10000.0
        EPS = 1e-06

        def _rmsnorm(x, w):
            rms = jnp.sqrt(jnp.mean(jnp.square(x), axis=-1, keepdims=True) + EPS)
            return x / rms * w

        def _rope(x, cos, sin):
            x1, x2 = jnp.split(x, 2, axis=-1)
            return jnp.concatenate([x1 * cos - x2 * sin, x1 * sin + x2 * cos], axis=-1)
        B, T, C = x.shape
        H, D = (N_HEADS, HEAD_DIM)
        qkv = jnp.einsum('btc,oc->bto', x, wqkv)
        q, k, v = jnp.split(qkv, 3, axis=-1)

        def to_heads(t):
            return t.reshape(B, T, H, D).transpose(0, 2, 1, 3)
        q, k, v = (to_heads(q), to_heads(k), to_heads(v))
        q = _rmsnorm(q, q_norm_w)
        k = _rmsnorm(k, k_norm_w)
        inv_freq = 1.0 / ROPE_THETA ** (jnp.arange(0, D, 2, dtype=jnp.float32) / D)
        freqs = jnp.arange(T, dtype=jnp.float32)[:, None] * inv_freq
        cos, sin = (jnp.cos(freqs), jnp.sin(freqs))
        q = _rope(q, cos, sin)
        k = _rope(k, cos, sin)
        scale = D ** (-0.5)
        attn = jnp.einsum('bhtd,bhsd->bhts', q, k) * scale
        causal = jnp.tril(jnp.ones((T, T), dtype=bool))
        attn = jnp.where(causal, attn, -jnp.inf)
        attn = jax.nn.softmax(attn.astype(jnp.float32), axis=-1).astype(q.dtype)
        out = jnp.einsum('bhts,bhsd->bhtd', attn, v)
        out = out.transpose(0, 2, 1, 3).reshape(B, T, H * D)
        return jnp.einsum('bte,ce->btc', out, wo)

    def _L0_ffn_ref(X, g1, g2, Wq, Wkc, Wvc, Wo, Wr, expert_bias, sW1, sW2, sW3, eW1, eW2, eW3):
        import jax, jax.numpy as jnp
        import numpy as np
        D_MODEL = 256
        NUM_HEADS = 4
        NUM_EXPERTS = 8
        TOP_K = 2
        D_FF = 256
        EPS = 1e-06

        def _rmsnorm(x, g):
            return x * jax.lax.rsqrt(jnp.mean(x * x, axis=-1, keepdims=True) + EPS) * g

        def _swiglu(x, w1, w2, w3):
            return jax.nn.silu(x @ w1.T) * (x @ w3.T) @ w2.T
        B, S, d = X.shape
        H = NUM_HEADS
        dk = d // H
        scale = 1.0 / jnp.sqrt(jnp.float32(dk))
        nx = _rmsnorm(X, g1)
        Q = (nx @ Wq.T).reshape(B, S, H, dk).transpose(0, 2, 1, 3)
        Kc = nx @ Wkc.T
        Vc = nx @ Wvc.T
        scores = jnp.einsum('bhsd,btd->bhst', Q, Kc) * scale
        attn = jax.nn.softmax(scores, axis=-1)
        out = jnp.einsum('bhst,btd->bhsd', attn, Vc)
        out = out.transpose(0, 2, 1, 3).reshape(B, S, d) @ Wo.T
        X = X + out
        nx = _rmsnorm(X, g2)
        xf = nx.reshape(-1, d)
        logits = xf @ Wr.T + expert_bias
        rw = jax.nn.softmax(logits, axis=-1)
        topw, topi = jax.lax.top_k(rw, TOP_K)
        topw = jax.nn.softmax(topw, axis=-1)
        combine = jnp.sum(jax.nn.one_hot(topi, NUM_EXPERTS, dtype=xf.dtype) * topw[..., None], axis=1)
        shared = _swiglu(xf, sW1, sW2, sW3)
        h = jax.nn.silu(jnp.einsum('td,efd->etf', xf, eW1)) * jnp.einsum('td,efd->etf', xf, eW3)
        eo = jnp.einsum('etf,edf->etd', h, eW2)
        specialist = jnp.einsum('te,etd->td', combine, eo)
        moe_out = (shared + specialist).reshape(B, S, d)
        return X + moe_out

    def _L1_attn_ref(inputs, ln_gamma, ln_beta, Wq, bq, Wk, bk, Wv, bv, Wp, u_bias, v_bias, Wo, bo):
        import jax, jax.numpy as jnp
        import numpy as np
        import math
        B, S, E, H = (2, 512, 256, 8)
        Dh = E // H

        def _pos_encoding(s, e):
            pos = jnp.arange(s, dtype=jnp.float32)[:, None]
            div = jnp.exp(jnp.arange(0, e, 2, dtype=jnp.float32) * (-math.log(10000.0) / e))
            pe = jnp.zeros((s, e), jnp.float32)
            pe = pe.at[:, 0::2].set(jnp.sin(pos * div))
            pe = pe.at[:, 1::2].set(jnp.cos(pos * div))
            return pe

        def _rel_shift(ps):
            b, h, s1, s2 = ps.shape
            padded = jnp.pad(ps, ((0, 0), (0, 0), (0, 0), (1, 0)))
            return padded.reshape(b, h, s2 + 1, s1)[:, :, 1:, :].reshape(b, h, s1, s2)

        def _forward(inputs, ln_gamma, ln_beta, Wq, bq, Wk, bk, Wv, bv, Wp, u_bias, v_bias, Wo, bo):
            b, s, e = inputs.shape
            mu = inputs.mean(-1, keepdims=True)
            var = inputs.var(-1, keepdims=True)
            xn = (inputs - mu) / jnp.sqrt(var + 1e-05) * ln_gamma + ln_beta
            xh = xn.reshape(b, s, H, Dh)
            q = xh @ Wq + bq
            k = xh @ Wk + bk
            v = xh @ Wv + bv
            pe = _pos_encoding(s, e).reshape(s, H, Dh)
            p = pe @ Wp
            content = jnp.einsum('bqhd,bkhd->bhqk', q + u_bias, k)
            pos_score = jnp.einsum('bqhd,khd->bhqk', q + v_bias, p)
            pos_score = _rel_shift(pos_score)
            score = (content + pos_score) / jnp.sqrt(jnp.float32(e))
            attn = jax.nn.softmax(score, axis=-1)
            ctx = jnp.einsum('bhqk,bkhd->bqhd', attn, v).reshape(b, s, e)
            return ctx @ Wo + bo
        return _forward(inputs, ln_gamma, ln_beta, Wq, bq, Wk, bk, Wv, bv, Wp, u_bias, v_bias, Wo, bo)

    def _L1_ffn_ref(x, ternary_weight, bias, act_scale):
        import jax, jax.numpy as jnp
        import numpy as np
        B, S, D_IN, D_OUT = (16, 1024, 256, 256)
        ACT_BITS = 8
        QB = float(2 ** (ACT_BITS - 1) - 1)
        scale = jnp.maximum(act_scale, 1e-05)
        x_int = jnp.clip(jnp.round(x / scale), -QB, QB)
        x_dq = jnp.nan_to_num(x_int * scale, nan=0.0, posinf=10000.0, neginf=-10000.0)
        w = ternary_weight.astype(jnp.float32) - 1.0
        return jnp.einsum('bsi,oi->bso', x_dq, w) + bias
    h = _L0_tok_ref(x, mask_BS_i1_0, L0_tok_emb, L0_tok_pca_lookup, L0_tok_proj_w, L0_tok_proj_b, L0_tok_fus_w, L0_tok_fus_b, L0_tok_ln_g, L0_tok_ln_b)
    h = h + _L0_attn_ref(_layernorm(h, axis=-1), L0_attn_wqkv, L0_attn_wo, L0_attn_q_norm_w, L0_attn_k_norm_w)
    h = h + _L0_ffn_ref(_layernorm(h, axis=-1), L0_ffn_g1, L0_ffn_g2, L0_ffn_Wq, L0_ffn_Wkc, L0_ffn_Wvc, L0_ffn_Wo, L0_ffn_Wr, L0_ffn_expert_bias, L0_ffn_sW1, L0_ffn_sW2, L0_ffn_sW3, L0_ffn_eW1, L0_ffn_eW2, L0_ffn_eW3)
    h = h + _L1_attn_ref(_layernorm(h, axis=-1), L1_attn_ln_gamma, L1_attn_ln_beta, L1_attn_Wq, L1_attn_bq, L1_attn_Wk, L1_attn_bk, L1_attn_Wv, L1_attn_bv, L1_attn_Wp, L1_attn_u_bias, L1_attn_v_bias, L1_attn_Wo, L1_attn_bo)
    h = h + _L1_ffn_ref(_layernorm(h, axis=-1), L1_ffn_ternary_weight, L1_ffn_bias, L1_ffn_act_scale)
    return h

_drawn_inputs = setup_inputs


def setup_inputs(seed=0):
    import zlib

    import numpy as np

    out = dict(_drawn_inputs(seed))
    spreads = {'L0_tok_proj_b': (0.0, 0.1),
     'L0_tok_fus_b': (0.0, 0.1),
     'L0_tok_ln_g': (1.0, 0.2),
     'L0_tok_ln_b': (0.0, 0.1),
     'L0_attn_q_norm_w': (1.0, 0.2),
     'L0_attn_k_norm_w': (1.0, 0.2),
     'L0_ffn_g1': (1.0, 0.6),
     'L0_ffn_g2': (1.0, 0.6),
     'L0_ffn_expert_bias': (0.0, 0.8),
     'L1_attn_ln_gamma': (1.0, 0.6),
     'L1_attn_ln_beta': (0.0, 2.0),
     'L1_attn_bq': (0.0, 2.0),
     'L1_attn_bk': (0.0, 2.0),
     'L1_attn_bv': (0.0, 1.332),
     'L1_attn_bo': (0.0, 0.385)}
    factors = {'L0_ffn_Wq': 8.0,
     'L0_ffn_Wkc': 8.0,
     'L0_ffn_Wr': 5.538,
     'L0_ffn_sW1': 4.45,
     'L0_ffn_sW2': 4.519,
     'L0_ffn_sW3': 4.595,
     'L0_ffn_eW1': 5.091,
     'L0_ffn_eW2': 5.001,
     'L0_ffn_eW3': 5.17,
     'L1_attn_Wq': 50.749,
     'L1_attn_Wk': 48.504,
     'L1_attn_Wv': 9.262,
     'L1_attn_Wp': 64.0,
     'L1_attn_u_bias': 64.0,
     'L1_attn_v_bias': 64.0}
    for name, (base, spread) in spreads.items():
        noise = np.random.default_rng([zlib.crc32(name.encode()), seed]).standard_normal(out[name].shape)
        drawn = base * np.exp(spread * noise) if base else spread * noise
        out[name] = jnp.asarray(drawn.astype(out[name].dtype))
    for name, factor in factors.items():
        out[name] = (out[name] * factor).astype(out[name].dtype)
    return out
```

```python
from contextlib import ExitStack

import concourse.bass as bass
from concourse import mybir

P = 128
ALU = mybir.AluOpType
ACT = mybir.ActivationFunctionType
AX_X = mybir.AxisListType.X
F32 = mybir.dt.float32
BF16 = mybir.dt.bfloat16
I32 = mybir.dt.int32
U32 = mybir.dt.uint32

SEQS = 64
TOK = 128
D = 256
DC = D // P
VOCAB = 28
PCA = 20
AH, AD = 16, 64
ATTN_GROUPS = 4
QKV_CHUNKS = 6
BANK = 512


def pipeline(eng, steps, skew, body, peel=2):
    first = max(skew + skew % 2, peel)
    last = steps - steps % 2
    for it in range(first):
        body(it, it // 2, it % 2, lambda off, it=it: 0 <= it - off < steps)
    with eng.Fori(first // 2, last // 2) as j:
        for half in range(2):
            body(2 * j + half, j, half, lambda off: True)
    for it in range(last, steps + skew):
        body(it, it // 2, it % 2, lambda off, it=it: 0 <= it - off < steps)


def wait(eng, sem, value, most=None):
    if isinstance(value, int):
        if most is not None:
            value = min(value, most)
        if value <= 0:
            return
    eng.wait_ge(sem, value)


class Links:

    def __init__(self, eng, sem, per_step):
        self.eng, self.sem, self.per_step, self.k = eng, sem, per_step, 0

    def at(self, step):
        assert self.k in (0, self.per_step), (self.k, self.per_step)
        self.step, self.k = step, 0
        return self

    def __call__(self, ins):
        self.k += 1
        ins.then_inc(self.sem, 1)
        self.eng.wait_ge(self.sem, self.step * self.per_step + self.k)


def bcast(ap, n, axis):
    return ap.unsqueeze(axis).broadcast_to([*ap.shape[:axis], n, *ap.shape[axis:]])


def program(nc, dram, out):
    with ExitStack() as ctx:
        h = ctx.enter_context(nc.sbuf_tensor("h", [P, SEQS * D], F32))
        ident = ctx.enter_context(nc.sbuf_tensor("ident", [P, P], F32))
        ident16 = ctx.enter_context(nc.sbuf_tensor("ident16", [P, P], BF16))
        bank = [ctx.enter_context(nc.psum_tensor(f"bank{i}", [P, BANK], F32)) for i in range(8)]
        eps5 = ctx.enter_context(nc.sbuf_tensor("eps5", [P, AH], F32))
        eps6 = ctx.enter_context(nc.sbuf_tensor("eps6", [P, AH], F32))
        neghalf = ctx.enter_context(nc.sbuf_tensor("neghalf", [P, AH], F32))
        shared = dict(ident16=ident16, nc=nc, dram=dram, h=h, ident=ident, bank=bank, eps5=eps5, eps6=eps6, neghalf=neghalf)
        block = ctx.enter_context(nc.Block())
        with ExitStack() as local:
            done = first_attention(ctx, block, shared, local)
        with ExitStack() as local:
            done = experts(ctx, block, shared, local, done)
        with ExitStack() as local:
            second_attention(ctx, block, shared, local, done, out)


def first_attention(ctx, block, shared, local):
    nc, dram, h, ident, bank = (shared[k] for k in ("nc", "dram", "h", "ident", "bank"))
    eps5, eps6, neghalf = (shared[k] for k in ("eps5", "eps6", "neghalf"))

    def sb(name, shape, dt=F32):
        return local.enter_context(nc.sbuf_tensor(name, shape, dt))

    def sem(name):
        return ctx.enter_context(nc.semaphore(name))

    wqkv = sb("wqkv", [P, DC, 3 * AH * AD])
    wo = sb("wo", [P, AH * AD // P, D])
    table = sb("table", [64, D])
    gain, shift = sb("tok_gain", [P, D]), sb("tok_shift", [P, D])
    rope_cs = sb("rope_cs", [P, 2, AD])
    norm_w = sb("norm_w", [P, 2, AD])
    rope_c = sb("rope_c", [P, 2, AD])
    rope_s = sb("rope_s", [P, 2, AD])
    causal = sb("causal", [P, BANK], BF16)
    causal_f = sb("causal_f", [P, TOK])
    ident16 = shared["ident16"]
    emb_t = sb("emb_t", [P, DC, VOCAB])
    pca_t = sb("pca_t", [PCA, VOCAB])
    proj_w = sb("proj_w", [PCA, D])
    proj_b = sb("proj_b", [P, DC])
    fus = sb("fus", [P, 2 * DC, D])
    fus_b = sb("fus_b", [1, D])
    cont_t = sb("cont_t", [P, DC, VOCAB])
    proj_bv = sb("proj_bv", [P, DC, VOCAB])
    onesv = sb("onesv", [P, P])
    idm = sb("idm", [64, 2, 2, TOK], I32)
    vocab_id = sb("vocab_id", [64, 1])
    hot = sb("hot", [64, TOK])
    mlen = sb("mlen", [64, TOK])
    mpad = sb("mpad", [64, TOK + 2])
    hpad = sb("hpad", [64, TOK + 2])
    wsum = sb("wsum", [64, TOK])
    msum = sb("msum", [64, TOK])
    minv = sb("minv", [64, TOK])
    ohw = sb("ohw", [64, 2, TOK])
    st6, mv0, mv1 = sb("st6", [P, 2, 6]), sb("mv0", [P, 2]), sb("mv1", [P, 2])
    carrier = sb("carrier", [P, 1])
    rstd = sb("rstd", [P, 4])
    hx = sb("hx", [P, 2, D])
    xin = sb("xin", [P, D])
    xt = sb("xt", [P, 2, DC, TOK])
    sq = sb("sq", [P, 2, BANK])
    ssq = sb("ssq", [P, 4, 8])
    rsh = sb("rsh", [P, 4, 8])
    rtmp = sb("rtmp", [P, 16])
    t1, t2 = sb("t1", [P, BANK]), sb("t2", [P, BANK])
    roped = sb("roped", [P, 2, 4, BANK])
    vbuf = sb("vbuf", [P, 2, 2, BANK])
    qscale = sb("qscale", [P, 2, AH])
    qkt = sb("qkt", [P, 4, BANK])
    smax, nbias = sb("smax", [P, 4]), sb("nbias", [P, 2, 4])
    probs = sb("probs", [P, 2, 4, TOK])
    probs_t = sb("probs_t", [P, 2, 4, TOK])
    psums = sb("psums", [P, 2, AH])
    pinv = sb("pinv", [P, 8])
    obuf = sb("obuf", [P, AH * AD])
    ot = sb("ot", [P, AH * AD // P, TOK])

    s_w = sem("a_weights")
    s_const = sem("a_const")
    s_tab = sem("a_table")
    s_ropetab = sem("a_rope_tables")
    s_idm = [sem(f"a_idm{i}") for i in range(2)]
    hot_pre, len_link, len_clipped = sem("a_hot_pre"), sem("a_len_link"), sem("a_len_clipped")
    hot_ready, hot_link = sem("a_hot_ready"), sem("a_hot_link")
    f_done, ln0_read = sem("a_fused"), sem("a_fused_read")
    ln_stat, ln_rs, ln_link, pool_link = sem("a_ln_stat"), sem("a_ln_rs"), sem("a_ln_link"), sem("a_pool_link")
    xin_ready, xt_filled, xt_evac = sem("a_xin"), sem("a_xt_filled"), sem("a_xt_evac")
    qkv_filled, sq_done, ssq_done, rs_ready = sem("a_qkv"), sem("a_sq"), sem("a_ssq"), sem("a_rs")
    rope_read, rope_link, roped_done, v_evac = sem("a_rope_read"), sem("a_rope_link"), sem("a_roped"), sem("a_v")
    rs_link = sem("a_rs_link")
    qkt_filled, qkt_evac = sem("a_qkt_filled"), sem("a_qkt_evac")
    s_done, nb_ready, nb_link, exp_done = sem("a_scores"), sem("a_nbias"), sem("a_nb_link"), sem("a_exp")
    pt_filled, pt_evac, av_done = sem("a_pt_filled"), sem("a_pt_evac"), sem("a_av")
    on_link, on_done = sem("a_on_link"), sem("a_on")
    ot_filled, ot_evac, wo_done, stored = sem("a_ot_filled"), sem("a_ot_evac"), sem("a_wo"), sem("a_stored")

    LOADS = [
        (ident[:], dram["ident"]), (vocab_id[:], dram["vocab_id"]), (emb_t[:], dram["emb_t"].rearrange("(c p) v -> p c v", p=P)),
        (pca_t[:], dram["pca_t"]), (proj_w[:], dram["proj_w"]), (proj_b[:], dram["proj_b"]),
        (fus[:], dram["fus_w"].rearrange("(c p) n -> p c n", p=P)), (fus_b[:], dram["fus_b"]),
        (gain[:], dram["ln_g"].partition_broadcast(P)), (shift[:], dram["ln_b"].partition_broadcast(P)),
        (rope_cs[:], dram["rope"]), (norm_w[:], dram["qk_norm"].partition_broadcast(P)),
        (causal_f[:], dram["causal"]),
        (wqkv[:], dram["wqkv_t"].rearrange("(c p) n -> p c n", p=P)),
        (wo[:], dram["wo_t"].rearrange("(c p) n -> p c n", p=P)),
    ]
    NL = 16 * len(LOADS)

    @block.sync
    def _(sp):
        for dst, src in LOADS:
            sp.dma_start(dst, src).then_inc(s_w, 16)

        def body(it, j, half, live):
            if live(0):
                wait(sp, hot_pre, it - 1)
                sp.dma_start(idm[:, half], dram["idm"][it].partition_broadcast(64)).then_inc(s_idm[half], 16)
        pipeline(sp, SEQS, 0, body)

    @block.gpsimd
    def _(pool):
        g = nc.gpsimd
        for t, v in ((eps5, 1e-5), (eps6, 1e-6), (neghalf, -0.5), (onesv, 1.0), (mpad, 0.0), (hpad, 0.0)):
            g.memset(t[:], v).then_inc(s_const, 1)
        pool.wait_ge(s_const, 6)
        link = Links(pool, hot_link, 4)
        plink = Links(pool, pool_link, 2)
        rlink = Links(pool, rs_link, 4)

        def hot_sums(s):
            lk = link.at(s)
            pool.wait_ge(hot_pre, s + 1)
            lk(g.tensor_tensor(out=hpad[:, 1:TOK + 1], in0=hot[:], in1=mpad[:, 1:TOK + 1], op=ALU.mult))
            g.tensor_tensor(out=wsum[:], in0=hpad[:, 0:TOK], in1=hpad[:, 1:TOK + 1], op=ALU.add)
            lk(g.tensor_tensor(out=msum[:], in0=mpad[:, 0:TOK], in1=mpad[:, 1:TOK + 1], op=ALU.add))
            g.tensor_tensor(out=wsum[:], in0=wsum[:], in1=hpad[:, 2:TOK + 2], op=ALU.add)
            lk(g.tensor_tensor(out=msum[:], in0=msum[:], in1=mpad[:, 2:TOK + 2], op=ALU.add))

        def hot_mean(s, half):
            pool.wait_ge(len_clipped, s + 1)
            wait(pool, f_done, s - 1)
            link(g.tensor_tensor(out=ohw[:, half], in0=wsum[:], in1=minv[:], op=ALU.mult))
            g.tensor_tensor(out=ohw[0:32, half], in0=hot[0:32], in1=onesv[0:32, :], op=ALU.mult).then_inc(hot_ready, 1)

        def ln_rsqrt(n, src, dst):
            lk = plink.at(n)
            pool.wait_ge(ln_stat, n + 1)
            lk(g.tensor_tensor(out=rstd[:, dst + 2:dst + 3], in0=src, in1=eps5[:, 0:1], op=ALU.add))
            lk(g.tensor_tensor(out=rstd[:, dst:dst + 1], in0=rstd[:, dst + 2:dst + 3], in1=neghalf[:, 0:1], op=ALU.pow))

        def head_rsqrt(s, c):
            pool.wait_ge(ssq_done, 4 * s + c + 1)
            wait(pool, rs_ready, 4 * s + c)
            rlink_(g.tensor_tensor(out=rtmp[:, 0:8], in0=ssq[:, c], in1=eps6[:, 0:8], op=ALU.add))
            g.tensor_tensor(out=rsh[:, c], in0=rtmp[:, 0:8], in1=neghalf[:, 0:8], op=ALU.pow).then_inc(rs_ready, 1)

        def body(it, j, half, live):
            nonlocal rlink_
            if live(2):
                rlink_ = rlink.at(it - 2)
            for c in range(4):
                if live(2):
                    head_rsqrt(it - 2, c)
                if c == 1 and live(1):
                    ln_rsqrt(2 * (it - 1), mv0[:, 1:2], 0)
                if c == 2 and live(1):
                    ln_rsqrt(2 * (it - 1) + 1, mv1[:, 1:2], 1)
                if c == 0 and live(0):
                    hot_sums(it)
            if live(0):
                hot_mean(it, half)
        rlink_ = None
        pipeline(pool, SEQS, 3, body)

    @block.tensor
    def _(pe):
        t = nc.tensor
        pe.wait_ge(s_w, NL)
        for c in range(DC):
            ins = t.matmul(bank[c][:, 0:VOCAB], proj_w[:, c * P:(c + 1) * P], pca_t[:], start=True, stop=True)
        ins.then_inc(s_tab, 1)
        pe.wait_ge(s_const, 6)
        pe.wait_ge(s_tab, 4)
        for c in range(DC):
            t.matmul(bank[2][0:VOCAB, 0:D], emb_t[:, c], fus[:, c], start=(c == 0), stop=False)
            t.matmul(bank[2][0:VOCAB, 0:D], proj_bv[:, c], fus[:, DC + c], start=False, stop=False)
        t.matmul(bank[2][0:VOCAB, 0:D], onesv[0:1, 0:VOCAB], fus_b[:], start=False, stop=True).then_inc(s_tab, 1)
        for c in range(DC):
            ins = t.matmul(bank[3][32:32 + VOCAB, 0:D], cont_t[:, c], fus[:, DC + c], start=(c == 0), stop=(c == DC - 1))
        ins.then_inc(s_tab, 1)
        pe.wait_ge(s_tab, 8)
        pe.wait_ge(s_ropetab, 4)

        def fused(s, half):
            pe.wait_ge(hot_ready, s + 1)
            wait(pe, stored, s - 2)
            t.matmul(bank[7][:, 0:D], ohw[:, half], table[:], start=True, stop=True).then_inc(f_done, 1)

        def qkv(s, half, c):
            if c == 0:
                pe.wait_ge(xt_evac, s + 1)
            if c < 2:
                wait(pe, v_evac, 2 * s - 1 + c)
            else:
                pe.wait_ge(rope_read, 4 * s + c - 1)
            for d in range(DC):
                ins = t.matmul(bank[c % 2][:], xt[:, half, d], wqkv[:, d, c * BANK:(c + 1) * BANK],
                               start=(d == 0), stop=(d == DC - 1))
            ins.then_inc(qkv_filled, 1)

        def qk_transposes(s, half, g):
            if g == 0:
                wait(pe, ot_evac, 2 * s - 1)
                if isinstance(s, int) and s == 0:
                    pe.wait_ge(xt_evac, 2)
                pe.wait_ge(roped_done, 4 * s + 4)
            elif g == 1:
                wait(pe, ot_evac, 2 * s)
            else:
                pe.wait_ge(qkt_evac, 4 * s + g - 1)
            for j in range(4):
                src = roped[:, half, 2 * (g % 2) + g // 2, j * P:(j + 1) * P]
                ins = t.transpose(bank[2 + g % 2][:, j * P:(j + 1) * P], src, ident[:])
            ins.then_inc(qkt_filled, 1)

        def scores(s, u):
            pe.wait_ge(qkt_evac, 4 * s + 2 * u + 2)
            wait(pe, exp_done, 4 * s + 2 * u)
            for par in range(2):
                t.matmul(bank[4 + par][:], ident16[:], causal[:], start=True, stop=False, skip_group_check=True)
            for j in range(4):
                for par in range(2):
                    rows, cols = slice(64 * par, 64 * par + 64), slice(j * P, (j + 1) * P)
                    ins = t.matmul(bank[4 + par][:, j * TOK:(j + 1) * TOK], qkt[rows, 2 * u, cols],
                                   qkt[rows, 2 * u + 1, cols], start=False, stop=(j == 3), skip_group_check=True)
                    if j == 3:
                        ins.then_inc(s_done, 1)

        def p_transposes(s, g):
            pe.wait_ge(exp_done, 4 * s + g + 1)
            if g < 2:
                pe.wait_ge(qkt_evac, 4 * s + 3 + g)
            else:
                pe.wait_ge(pt_evac, 4 * s + g - 1)
            for j in range(4):
                ins = t.transpose(bank[2 + g % 2][:, j * P:(j + 1) * P], probs[:, g % 2, j], ident[:])
            ins.then_inc(pt_filled, 1)

        def values(s, half, g):
            pe.wait_ge(pt_evac, 4 * s + g + 1)
            if g % 2 == 0:
                wait(pe, on_done, 2 * s + g // 2)
            if g == 0:
                pe.wait_ge(v_evac, 2 * s + 2)
            for j in range(4):
                hd = 8 * (g // 2) + 2 * j + g % 2
                ins = t.matmul(bank[6][:, (hd % 8) * AD:(hd % 8 + 1) * AD], probs_t[:, g % 2, j],
                               vbuf[:, half, hd // 8, (hd % 8) * AD:(hd % 8 + 1) * AD],
                               start=True, stop=True, skip_group_check=True)
            ins.then_inc(av_done, 1)

        def x_transposes(s, last):
            pe.wait_ge(xin_ready, s + 1)
            if isinstance(s, int) and s < 2:
                wait(pe, xt_evac, s)
            wait(pe, pt_evac, 4 * (s - 2) + 3)
            for d in range(DC):
                ins = t.transpose(bank[2][:, d * P:(d + 1) * P], xin[:, d * P:(d + 1) * P], ident[:])
            ins.then_inc(xt_filled, 1)

        def o_transposes(s, u):
            pe.wait_ge(on_done, 2 * s + u + 1)
            if u == 0:
                wait(pe, xt_evac, s + 3, SEQS)
            else:
                pe.wait_ge(pt_evac, 4 * s + 4)
            for j in range(4):
                ins = t.transpose(bank[2 + u][:, j * P:(j + 1) * P], obuf[:, (4 * u + j) * P:(4 * u + j + 1) * P], ident[:])
            ins.then_inc(ot_filled, 1)

        def out_proj(s):
            wait(pe, ln0_read, s + 3, SEQS)
            for u in range(8):
                if u % 4 == 0:
                    pe.wait_ge(ot_evac, 2 * s + u // 4 + 1)
                ins = t.matmul(bank[7][:, D:2 * D], ot[:, u], wo[:, u], start=(u == 0), stop=(u == 7))
            ins.then_inc(wo_done, 1)

        def body(it, j, half, live):
            s1, s2, s3 = it - 1, it - 2, it - 3
            other = 1 - half
            A, Q, F = live(3), live(2), live(1)
            if A:
                qk_transposes(s3, other, 0)
                qk_transposes(s3, other, 1)
            if Q: qkv(s2, half, 0)
            if A:
                scores(s3, 0)
                qk_transposes(s3, other, 2)
                qk_transposes(s3, other, 3)
            if Q: qkv(s2, half, 1)
            if F: fused(s1, other)
            if A: p_transposes(s3, 0)
            if Q: qkv(s2, half, 2)
            if A:
                p_transposes(s3, 1)
                scores(s3, 1)
                values(s3, other, 0)
                values(s3, other, 1)
            if Q: qkv(s2, half, 3)
            if A:
                p_transposes(s3, 2)
            if Q: qkv(s2, half, 4)
            if A:
                p_transposes(s3, 3)
                values(s3, other, 2)
                values(s3, other, 3)
            if Q: qkv(s2, half, 5)
            if F: x_transposes(s1, it)
            if A:
                o_transposes(s3, 0)
                o_transposes(s3, 1)
                out_proj(s3)
        pipeline(pe, SEQS, 3, body)

    @block.scalar
    def _(act):
        a = nc.scalar

        def qkt_copy(s, g):
            act.wait_ge(qkt_filled, 4 * s + g + 1)
            wait(act, s_done, 4 * (s - 1) + 2 * (g // 2) + 2)
            a.activation(qkt[:, g], bank[2 + g % 2][:], ACT.Copy).then_inc(qkt_evac, 1)

        def square(s, c):
            act.wait_ge(qkv_filled, 6 * s + c + 1)
            wait(act, ssq_done, 4 * s + c - 1)
            a.activation(sq[:, c % 2], bank[c % 2][:], ACT.Square, scale=AD ** -0.5).then_inc(sq_done, 1)

        def v_copy(s, half, c):
            act.wait_ge(qkv_filled, 6 * s + 5 + c)
            wait(act, av_done, 4 * (s - 1))
            a.activation(vbuf[:, half, c], bank[c % 2][:], ACT.Copy).then_inc(v_evac, 1)

        def exps(s, half, g):
            act.wait_ge(nb_ready, 4 * s + g + 1)
            wait(act, pt_filled, 4 * s + g - 1)
            for j in range(4):
                hd = 8 * (g // 2) + 2 * j + g % 2
                ins = a.activation(probs[:, g % 2, j], bank[4 + g % 2][:, j * TOK:(j + 1) * TOK], ACT.Exp,
                                   bias=nbias[:, g % 2, j:j + 1], scale=qscale[:, half, hd:hd + 1],
                                   accum_out=psums[:, half, hd:hd + 1])
            ins.then_inc(exp_done, 1)

        def pt_copy(s, g):
            act.wait_ge(pt_filled, 4 * s + g + 1)
            wait(act, av_done, 4 * s + g - 1)
            a.activation(probs_t[:, g % 2].rearrange("p a b -> p (a b)"), bank[2 + g % 2][:], ACT.Copy).then_inc(pt_evac, 1)

        def xt_copy(s, half):
            act.wait_ge(xt_filled, s + 1)
            wait(act, qkv_filled, 6 * (s - 1))
            a.activation(xt[:, half].rearrange("p a b -> p (a b)"), bank[2][:, 0:D], ACT.Copy).then_inc(xt_evac, 1)

        def ot_copy(s, u):
            act.wait_ge(ot_filled, 2 * s + u + 1)
            wait(act, wo_done, s)
            a.activation(ot[:, 4 * u:4 * u + 4].rearrange("p a b -> p (a b)"), bank[2 + u][:], ACT.Copy).then_inc(ot_evac, 1)

        def body(it, j, half, live):
            s1, s2, s3 = it - 1, it - 2, it - 3
            other = 1 - half
            A, Q, F = live(3), live(2), live(1)
            if A:
                qkt_copy(s3, 0)
                qkt_copy(s3, 1)
            if Q: square(s2, 0)
            if A:
                qkt_copy(s3, 2)
                qkt_copy(s3, 3)
                exps(s3, other, 0)
            if Q: square(s2, 1)
            if A:
                exps(s3, other, 1)
                pt_copy(s3, 0)
            if Q: square(s2, 2)
            if A:
                pt_copy(s3, 1)
                exps(s3, other, 2)
            if Q: square(s2, 3)
            if A:
                exps(s3, other, 3)
                pt_copy(s3, 2)
                pt_copy(s3, 3)
            if Q: v_copy(s2, half, 0)
            if Q: v_copy(s2, half, 1)
            if F: xt_copy(s1, other)
            if A:
                ot_copy(s3, 0)
                ot_copy(s3, 1)
        pipeline(act, SEQS, 3, body)

    @block.vector
    def _(dve):
        v = nc.vector
        dve.wait_ge(s_w, NL)
        dve.wait_ge(s_const, 6)
        v.memset(table[:], 0.0).then_inc(s_ropetab, 1)
        dve.wait_ge(s_tab, 1)
        for c in range(DC):
            v.tensor_copy(cont_t[:, c], bank[c][:, 0:VOCAB]).then_inc(s_tab, 1)
        v.tensor_copy(proj_bv[:], bcast(proj_b[:], VOCAB, 2)).then_inc(s_tab, 1)
        v.tensor_copy(causal[:].rearrange("p (a b) -> p a b", a=4), bcast(causal_f[:], 4, 1)).then_inc(s_ropetab, 1)
        v.tensor_copy(ident16[:], ident[:]).then_inc(s_ropetab, 1)
        for i in range(2):
            v.tensor_tensor(rope_c[:, i], rope_cs[:, 0], norm_w[:, i], ALU.mult)
            for u in range(2):
                ins = v.tensor_tensor(rope_s[:, i, 32 * u:32 * u + 32], rope_cs[:, 1, 32 * u:32 * u + 32],
                                      norm_w[:, i, 32 - 32 * u:64 - 32 * u], ALU.mult)
        ins.then_inc(s_ropetab, 1)
        dve.wait_ge(s_tab, 6)
        dve.wait_ge(s_ropetab, 4)
        v.tensor_copy(table[0:VOCAB], bank[2][0:VOCAB, 0:D]).then_inc(s_tab, 1)
        v.tensor_copy(table[32:32 + VOCAB], bank[3][32:32 + VOCAB, 0:D]).then_inc(s_tab, 1)
        dve.wait_ge(s_ropetab, 4)

        lenl = Links(dve, len_link, 1)
        lnl = Links(dve, ln_link, 5)
        ropel = Links(dve, rope_link, 4)
        nbl = Links(dve, nb_link, 4)
        onl = Links(dve, on_link, 2)

        def hot_prep(s, half, j):
            dve.wait_ge(s_idm[half], 16 * j + 16)
            wait(dve, hot_ready, s)
            v.tensor_scalar(hot[:], idm[:, half, 0], vocab_id[:], None, ALU.is_equal)
            v.tensor_copy(mpad[:, 1:TOK + 1], idm[:, half, 1]).then_inc(hot_pre, 1)

        def len_clip(s):
            dve.wait_ge(hot_link, 4 * s + 3)
            lenl.at(s)(v.tensor_scalar(mlen[:], msum[:], 1.0, None, ALU.max))
            v.reciprocal(minv[:], mlen[:]).then_inc(len_clipped, 1)

        def ln_stats(s):
            dve.wait_ge(f_done, s + 1)
            lnl.at(s)(v.bn_stats(st6[:, 0], bank[7][:, 0:D]))
            v.memset(carrier[:], 0.0)
            v.bn_aggr(mv0[:], st6[:, 0]).then_inc(ln_stat, 1)

        def ln_apply(s):
            dve.wait_ge(pool_link, 4 * s + 2)
            ins = v.tensor_scalar(hx[:, 0], bank[7][:, 0:D], mv0[:, 0:1], rstd[:, 0:1], ALU.subtract, ALU.mult)
            ins.then_inc(ln0_read, 1)
            dve.wait_ge(ln0_read, s + 1)
            wait(dve, xin_ready, s)
            lnl(v.tensor_tensor(hx[:, 0], hx[:, 0], gain[:], ALU.mult))
            lnl(v.tensor_tensor(hx[:, 1], hx[:, 0], shift[:], ALU.add))
            lnl(v.bn_stats(st6[:, 1], hx[:, 1]))
            v.memset(carrier[:], 0.0)
            v.bn_aggr(mv1[:], st6[:, 1]).then_inc(ln_stat, 1)
            lnl(v.tensor_copy(h[:, bass.ds(s * D, D)], hx[:, 1]))

        def ln_xin(s):
            dve.wait_ge(pool_link, 4 * s + 4)
            wait(dve, xt_filled, s)
            v.tensor_scalar(xin[:], hx[:, 1], mv1[:, 0:1], rstd[:, 1:2], ALU.subtract, ALU.mult).then_inc(xin_ready, 1)

        def rope(s, half, c):
            i = c // 2
            dve.wait_ge(sq_done, 4 * s + c + 1)
            if c == 0:
                ropel.at(s)
                wait(dve, qkt_filled, 4 * (s - 1))
            wait(dve, roped_done, 4 * s + c)
            v.tensor_reduce(ssq[:, c], sq[:, c % 2].rearrange("p (a b) -> p a b", b=AD), AX_X, ALU.add).then_inc(ssq_done, 1)
            x = bank[c % 2][:].rearrange("p (a b) -> p a b", b=AD)
            xs = bank[c % 2][:].rearrange("p (a u b) -> p a u b", u=2, b=32)
            y1 = t1[:].rearrange("p (a b) -> p a b", b=AD)
            y2 = t2[:].rearrange("p (a u b) -> p a u b", u=2, b=32)
            v.tensor_tensor(y1, x, bcast(rope_c[:, i], 8, 1), ALU.mult)
            for u in range(2):
                ins = v.tensor_tensor(y2[:, :, u], xs[:, :, 1 - u],
                                      bcast(rope_s[:, i, 32 * u:32 * u + 32], 8, 1), ALU.mult)
            ins.then_inc(rope_read, 1)
            dve.wait_ge(rope_read, 4 * s + c + 1)
            out = roped[:, half, c]
            if i == 0:
                v.tensor_tensor(out, t1[:], t2[:], ALU.add).then_inc(roped_done, 1)
            else:
                ropel(v.tensor_tensor(t1[:], t1[:], t2[:], ALU.add))
                dve.wait_ge(rs_ready, 4 * s + c + 1)
                v.tensor_tensor(out.rearrange("p (a b) -> p a b", b=AD), y1, bcast(rsh[:, c], AD, 2), ALU.mult).then_inc(roped_done, 1)
            if c == 3:
                for cc in range(2):
                    ropel(v.tensor_scalar(qscale[:, half, 8 * cc:8 * cc + 8], rsh[:, cc], AD ** -0.5, None, ALU.mult))

        def row_max(s, half, g):
            dve.wait_ge(s_done, 4 * s + g + 1)
            if g == 0:
                nbl.at(s)
            wait(dve, nb_ready, 4 * s + g)
            nbl(v.tensor_reduce(smax[:], bank[4 + g % 2][:].rearrange("p (a b) -> p a b", b=TOK), AX_X, ALU.max))
            wait(dve, exp_done, 4 * s + g - 1)
            v.scalar_tensor_tensor(nbias[:, g % 2], smax[:], -1.0, qscale[:, half, 8 * (g // 2) + g % 2:8 * (g // 2) + 8:2], ALU.mult, ALU.mult).then_inc(nb_ready, 1)

        def o_norm(s, half, u):
            if u == 0:
                onl.at(s)
            dve.wait_ge(av_done, 4 * s + 2 * u + 2)
            wait(dve, on_done, 2 * s + u)
            onl(v.reciprocal(pinv[:], psums[:, half, 8 * u:8 * u + 8]))
            wait(dve, ot_filled, 2 * s + u - 1)
            v.tensor_tensor(obuf[:, u * BANK:(u + 1) * BANK].rearrange("p (a b) -> p a b", b=AD),
                            bank[6][:].rearrange("p (a b) -> p a b", b=AD), bcast(pinv[:], AD, 2), ALU.mult).then_inc(on_done, 1)

        def residual(s):
            dve.wait_ge(wo_done, s + 1)
            hs = h[:, bass.ds(s * D, D)]
            v.tensor_tensor(hs, hs, bank[7][:, D:2 * D], ALU.add).then_inc(stored, 1)

        def body(it, j, half, live):
            s1, s2, s3 = it - 1, it - 2, it - 3
            other = 1 - half
            A, Q, F = live(3), live(2), live(1)
            if live(0): hot_prep(it, half, j)
            if A: row_max(s3, other, 0)
            if A: row_max(s3, other, 1)
            if Q: rope(s2, half, 0)
            if Q: rope(s2, half, 1)
            if live(0): len_clip(it)
            if F: ln_stats(s1)
            if A: row_max(s3, other, 2)
            if A: row_max(s3, other, 3)
            if Q: rope(s2, half, 2)
            if F: ln_apply(s1)
            if A: o_norm(s3, other, 0)
            if Q: rope(s2, half, 3)
            if F: ln_xin(s1)
            if A: o_norm(s3, other, 1)
            if A: residual(s3)
        pipeline(dve, SEQS, 3, body)

    return stored, SEQS


G4 = 4
GROUPS = SEQS // G4
GT = G4 * TOK
EXPERTS = 8
NE = EXPERTS + 1
FF = 256
FC = FF // P
LH, LD = 4, 64
LSCALE = LD ** -0.5


def experts(ctx, block, shared, local, a_done):
    nc, dram, h, ident, bank = (shared[k] for k in ("nc", "dram", "h", "ident", "bank"))
    eps5, eps6, neghalf = (shared[k] for k in ("eps5", "eps6", "neghalf"))

    def sb(name, shape, dt=F32):
        return local.enter_context(nc.sbuf_tensor("b_" + name, shape, dt))

    def sem(name):
        return ctx.enter_context(nc.semaphore("b_" + name))

    w1 = sb("w1", [P, DC, NE * FF])
    w3 = sb("w3", [P, DC, NE * FF])
    w2 = sb("w2", [P, FC, NE, D])
    wq = sb("wq", [P, DC, D])
    wk = sb("wk", [P, DC, 2 * LD])
    wv = sb("wv", [P, DC, LD])
    wo = sb("wo", [P, DC, D])
    wr = sb("wr", [P, DC, EXPERTS])
    g1, g2 = sb("g1", [P, DC]), sb("g2", [P, DC])
    rbias = sb("rbias", [P, EXPERTS])
    iota8 = sb("iota8", [P, EXPERTS])
    carrier = sb("carrier", [P, 1])
    st = sb("st", [P, 2, G4, 6])
    mv1, mv2 = sb("mv1", [P, G4, 2]), sb("mv2", [P, G4, 2])
    ms = sb("ms", [P, G4])
    rtmp, rs = sb("rtmp", [P, G4]), sb("rs", [P, 3, G4])
    x = sb("x", [P, G4 * D])
    nx = sb("nx", [P, G4 * D])
    nxt = sb("nxt", [P, DC, GT])
    qt = sb("qt", [P, DC, GT])
    kt = sb("kt", [P, GT])
    vb = sb("vb", [P, G4 * LD])
    smax, nbias = sb("smax", [P, 4]), sb("nbias", [P, 2, 4])
    probs = sb("probs", [P, 2, LH * TOK])
    pt = sb("pt", [P, G4, LH * TOK])
    psums = sb("psums", [P, G4, LH])
    pinv = sb("pinv", [P, 2 * LH])
    ob = sb("ob", [P, G4 * D])
    otb = sb("otb", [P, DC, GT])
    xft = sb("xft", [P, 2, DC, GT])
    lg, ex, rw = (sb(n, [P, G4, EXPERTS]) for n in ("lg", "ex", "rw"))
    r4a, r4b = sb("r4a", [P, G4]), sb("r4b", [P, G4])
    top = sb("top", [P, G4, 8])
    topi = sb("topi", [P, G4, 8], U32)
    topf = sb("topf", [P, G4, 8])
    diff, ediff = sb("diff", [P, G4]), sb("ediff", [P, G4])
    tw = sb("tw", [P, 2, G4])
    comb = sb("comb", [P, G4, EXPERTS])
    th, up = sb("th", [P, 2, GT]), sb("up", [P, GT])
    hid = sb("hid", [P, 2, FC, GT])

    s_w, s_const = sem("weights"), sem("const")
    stat, rs_ready, link_ln, link_pool = sem("stat"), sem("rs"), sem("link_ln"), sem("link_pool")
    nx_ready, t_filled, t_evac = sem("nx"), sem("t_filled"), sem("t_evac")
    q_filled, q_evac = sem("q_filled"), sem("q_evac")
    s_done, nb_ready, exp_done, nb_link = sem("scores"), sem("nbias"), sem("exp"), sem("nb_link")
    pt_filled, pt_evac, av_done, on_done, on_link = sem("pt_filled"), sem("pt_evac"), sem("av"), sem("on"), sem("on_link")
    ot_filled, ot_evac, wo_done, x2_done = sem("ot_filled"), sem("ot_evac"), sem("wo"), sem("x2")
    r_done, r_shift, r_exp, r_diff, r_ediff, r_link, comb_ready = (sem(n) for n in (
        "r_logits", "r_shift", "r_exp", "r_diff", "r_ediff", "r_link", "r_comb"))
    w13_done, tanh_done, up_done, hid_done, w2_half, acc_done = (sem(n) for n in (
        "w13", "tanh", "up", "hid", "w2_half", "acc"))

    LOADS = [
        (wq[:], dram["l_wq"]), (wk[:, :, 0:LD], dram["l_wk"]), (wk[:, :, LD:2 * LD], dram["l_wk"]), (wv[:], dram["l_wv"]),
        (wo[:], dram["l_wo"]), (wr[:], dram["l_wr"]), (g1[:], dram["l_g1"]), (g2[:], dram["l_g2"]),
        (rbias[:], dram["l_rbias"].partition_broadcast(P)), (iota8[:], dram["iota8"].partition_broadcast(P)),
        (w1[:, :, 0:FF], dram["l_sw1"]), (w3[:, :, 0:FF], dram["l_sw3"]), (w2[:, :, 0], dram["l_sw2"]),
        (w1[:, :, FF:], dram["l_ew1"]), (w3[:, :, FF:], dram["l_ew3"]), (w2[:, :, 1:], dram["l_ew2"]),
    ]
    NL = 16 * len(LOADS)

    @block.sync
    def _(sp):
        sp.wait_ge(*a_done)
        for dst, src in LOADS:
            sp.dma_start(dst, src).then_inc(s_w, 16)

    @block.gpsimd
    def _(pool):
        g = nc.gpsimd
        pool.wait_ge(*a_done)
        lk = Links(pool, link_pool, 3)

        def body(it, j, half, live):
            if live(0):
                for n, src, eps in ((0, mv1[:, :, 1], eps5), (1, ms[:], eps6), (2, ms[:], eps6)):
                    if n == 0:
                        lk.at(it)
                    pool.wait_ge(stat, 3 * it + n + 1)
                    wait(pool, rs_ready, 3 * it + n)
                    lk(g.tensor_tensor(out=rtmp[:], in0=src, in1=eps[:, 0:G4], op=ALU.add))
                    g.tensor_tensor(out=rs[:, n], in0=rtmp[:], in1=neghalf[:, 0:G4], op=ALU.pow).then_inc(rs_ready, 1)
        pipeline(pool, GROUPS, 1, body)

    @block.tensor
    def _(pe):
        t = nc.tensor
        pe.wait_ge(*a_done)
        pe.wait_ge(s_w, NL)

        def transposes(src, b, dst_bank):
            for q in range(G4):
                ins = t.transpose(dst_bank[:, q * TOK:(q + 1) * TOK], src[:, q * D + b * P:q * D + (b + 1) * P], ident[:])
            return ins

        def t1(g):
            pe.wait_ge(nx_ready, 2 * g + 1)
            wait(pe, r_shift, g)
            for b in range(2):
                transposes(nx, b, bank[6 + b]).then_inc(t_filled, 1)

        def q_proj(g):
            for c in range(DC):
                pe.wait_ge(t_evac, 4 * g + 2)
                for d in range(DC):
                    ins = t.matmul(bank[6 + c][:], wq[:, d, c * P:(c + 1) * P], nxt[:, d], start=(d == 0), stop=(d == DC - 1))
                ins.then_inc(q_filled, 1)

        def kv_proj(g):
            pe.wait_ge(q_evac, 4 * g + 1)
            for d in range(DC):
                ins = t.matmul(bank[6][:], wk[:, d], nxt[:, d], start=(d == 0), stop=(d == DC - 1))
            ins.then_inc(q_filled, 1)
            pe.wait_ge(q_evac, 4 * g + 2)
            for q in range(G4):
                for d in range(DC):
                    ins = t.matmul(bank[7][:, q * LD:(q + 1) * LD], nxt[:, d, q * TOK:(q + 1) * TOK], wv[:, d],
                                   start=(d == 0), stop=(d == DC - 1), skip_group_check=True)
            ins.then_inc(q_filled, 1)

        def scores(g, u):
            if u == 0:
                pe.wait_ge(q_evac, 4 * g + 4)
            else:
                pe.wait_ge(pt_evac, 4 * g + 2)
            for q in range(2):
                for c in range(DC):
                    for par in range(2):
                        rows, seq = slice(64 * par, 64 * par + 64), 2 * u + q
                        cols = slice(seq * TOK, (seq + 1) * TOK)
                        ins = t.matmul(bank[6 + par][:, (2 * q + c) * TOK:(2 * q + c + 1) * TOK], qt[rows, c, cols],
                                       kt[rows, cols], start=True, stop=True, skip_group_check=True)
                        if q == 1 and c == 1:
                            ins.then_inc(s_done, 1)

        def p_transposes(g, u):
            pe.wait_ge(exp_done, 4 * g + 2 * u + 2)
            for q in range(2):
                for hd in range(LH):
                    col = (2 * q + hd // 2) * TOK
                    ins = t.transpose(bank[6 + q][:, hd * TOK:(hd + 1) * TOK], probs[:, hd % 2, col:col + TOK], ident[:])
                ins.then_inc(pt_filled, 1)

        def values(g):
            for u in range(2):
                pe.wait_ge(pt_evac, 4 * g + 3 + u)
                for q in range(2):
                    for hd in range(LH):
                        seq = 2 * u + q
                        if u == 0 and q == 0 and hd == 0:
                            pe.wait_ge(pt_evac, 4 * g + 4)
                        ins = t.matmul(bank[6 + u][:, q * D + hd * LD:q * D + (hd + 1) * LD], pt[:, seq, hd * TOK:(hd + 1) * TOK],
                                       vb[:, seq * LD:(seq + 1) * LD], start=True, stop=True, skip_group_check=True)
                ins.then_inc(av_done, 1)

        def o_transposes(g):
            pe.wait_ge(on_done, 2 * g + 2)
            for b in range(2):
                transposes(ob, b, bank[6 + b]).then_inc(ot_filled, 1)

        def out_proj(g):
            pe.wait_ge(ot_evac, 2 * g + 2)
            for q in range(G4):
                for c in range(DC):
                    ins = t.matmul(bank[6 + q // 2][:, (q % 2) * D:(q % 2 + 1) * D], otb[:, c, q * TOK:(q + 1) * TOK], wo[:, c],
                                   start=(c == 0), stop=(c == DC - 1), skip_group_check=True)
                if q % 2:
                    ins.then_inc(wo_done, 1)

        def t2(g):
            pe.wait_ge(nx_ready, 2 * g + 2)
            for b in range(2):
                transposes(nx, b, bank[6 + b]).then_inc(t_filled, 1)

        def logits(g, half):
            pe.wait_ge(t_evac, 4 * g + 4)
            for q in range(G4):
                for d in range(DC):
                    ins = t.matmul(bank[6][:, q * EXPERTS:(q + 1) * EXPERTS], xft[:, half, d, q * TOK:(q + 1) * TOK], wr[:, d],
                                   start=(d == 0), stop=(d == DC - 1), skip_group_check=True)
            ins.then_inc(r_done, 1)

        def up_gate(g, half, n):
            wait(pe, hid_done, 18 * g + n - 1)
            cols = slice(n * P, (n + 1) * P)
            for i, w in enumerate((w1, w3)):
                for d in range(DC):
                    ins = t.matmul(bank[2 * i + n % 2][:], w[:, d, cols], xft[:, half, d], start=(d == 0), stop=(d == DC - 1))
            ins.then_inc(w13_done, 1)

        def down(g, e):
            pe.wait_ge(hid_done, 18 * g + 2 * e + 2)
            for q in range(G4):
                if q % 2 == 0:
                    wait(pe, acc_done, 4 * (NE * g + e) - 2 + q)
                for c in range(FC):
                    ins = t.matmul(bank[4 + q // 2][:, (q % 2) * D:(q % 2 + 1) * D], hid[:, e % 2, c, q * TOK:(q + 1) * TOK],
                                   w2[:, c, e], start=(c == 0), stop=(c == FC - 1), skip_group_check=True)
                if q % 2:
                    ins.then_inc(w2_half, 1)

        def body(it, j, half, live):
            g, m, other = it, it - 1, 1 - half
            if live(1): logits(m, other)
            for n in range(2 * NE):
                if live(0):
                    if n == 3: t1(g)
                    if n == 4: q_proj(g)
                    if n == 5: kv_proj(g)
                    if n == 6: scores(g, 0)
                    if n == 8: p_transposes(g, 0)
                    if n == 9: scores(g, 1)
                    if n == 11: p_transposes(g, 1)
                    if n == 12: values(g)
                    if n == 13: o_transposes(g)
                    if n == 14: out_proj(g)
                    if n == 17: t2(g)
                if live(1):
                    up_gate(m, other, n)
                    if n >= 2 and n % 2 == 0:
                        down(m, n // 2 - 1)
            if live(1): down(m, NE - 1)
        pipeline(pe, GROUPS, 1, body)

    @block.scalar
    def _(act):
        a = nc.scalar
        act.wait_ge(*a_done)
        act.wait_ge(s_w, NL)

        def t_copy(g, half, k):
            dst, gain = (nxt, g1) if k == 0 else (xft[:, half], g2)
            for b in range(2):
                act.wait_ge(t_filled, 4 * g + 2 * k + b + 1)
                if k == 0:
                    wait(act, q_filled, 4 * g)
                else:
                    wait(act, w13_done, 18 * (g - 1))
                a.activation(dst[:, b], bank[6 + b][:], ACT.Copy, scale=gain[:, b:b + 1]).then_inc(t_evac, 1)

        def q_copy(g):
            for c in range(2):
                act.wait_ge(q_filled, 4 * g + c + 1)
                wait(act, s_done, 4 * g)
                a.activation(qt[:, c], bank[6 + c][:], ACT.Copy).then_inc(q_evac, 1)

        def kv_copy(g):
            act.wait_ge(q_filled, 4 * g + 3)
            a.activation(kt[:], bank[6][:], ACT.Copy).then_inc(q_evac, 1)
            act.wait_ge(q_filled, 4 * g + 4)
            wait(act, av_done, 2 * g)
            a.activation(vb[:], bank[7][:, 0:G4 * LD], ACT.Copy).then_inc(q_evac, 1)

        def exps(g, u):
            for par in range(2):
                act.wait_ge(nb_ready, 4 * g + 2 * u + par + 1)
                wait(act, pt_filled, 4 * g + 2 * u)
                for i in range(4):
                    ins = a.activation(probs[:, par, i * TOK:(i + 1) * TOK], bank[6 + par][:, i * TOK:(i + 1) * TOK], ACT.Exp,
                                       bias=nbias[:, par, i:i + 1], scale=LSCALE,
                                       accum_out=psums[:, 2 * u + i // 2, 2 * (i % 2) + par:2 * (i % 2) + par + 1])
                ins.then_inc(exp_done, 1)

        def pt_copy(g, u):
            for q in range(2):
                act.wait_ge(pt_filled, 4 * g + 2 * u + q + 1)
                wait(act, av_done, 2 * g)
                a.activation(pt[:, 2 * u + q], bank[6 + q][:], ACT.Copy).then_inc(pt_evac, 1)

        def ot_copy(g):
            for b in range(2):
                act.wait_ge(ot_filled, 2 * g + b + 1)
                wait(act, wo_done, 2 * g)
                a.activation(otb[:, b], bank[6 + b][:], ACT.Copy).then_inc(ot_evac, 1)

        def gate_tanh(g, n):
            act.wait_ge(w13_done, 18 * g + n + 1)
            wait(act, up_done, 18 * g + n - 1)
            a.activation(th[:, n % 2], bank[n % 2][:], ACT.Tanh, scale=0.5).then_inc(tanh_done, 1)

        def body(it, j, half, live):
            g, m, other = it, it - 1, 1 - half
            for n in range(2 * NE):
                if live(0):
                    if n == 3: t_copy(g, half, 0)
                    if n == 4: q_copy(g)
                    if n == 5: kv_copy(g)
                    if n == 6: exps(g, 0)
                    if n == 8: pt_copy(g, 0)
                    if n == 9: exps(g, 1)
                    if n == 11: pt_copy(g, 1)
                    if n == 13: ot_copy(g)
                    if n == 17: t_copy(g, half, 1)
                if live(1):
                    if n == 0:
                        act.wait_ge(r_shift, m + 1)
                        wait(act, r_diff, m)
                        a.activation(ex[:], lg[:], ACT.Exp).then_inc(r_exp, 1)
                    if n == 1:
                        act.wait_ge(r_diff, m + 1)
                        a.activation(ediff[:], diff[:], ACT.Exp).then_inc(r_ediff, 1)
                    gate_tanh(m, n)
        pipeline(act, GROUPS, 1, body)

    @block.vector
    def _(dve):
        v = nc.vector
        dve.wait_ge(*a_done)
        dve.wait_ge(s_w, NL)
        lnl = Links(dve, link_ln, 11)
        nbl, onl, rl = Links(dve, nb_link, 4), Links(dve, on_link, 2), Links(dve, r_link, 13)

        def tile_of(g, q):
            return h[:, bass.ds((G4 * g + q) * D, D)]

        def stats(src, mv, k):
            for q in range(G4):
                ins = v.bn_stats(st[:, k, q], src(q))
            lnl(ins)
            v.memset(carrier[:], 0.0)
            for q in range(G4):
                ins = v.bn_aggr(mv[:, q], st[:, k, q])
            return ins

        def mean_square():
            lnl(v.tensor_tensor(ms[:], mv2[:, :, 0], mv2[:, :, 0], ALU.mult))
            v.tensor_tensor(ms[:], ms[:], mv2[:, :, 1], ALU.add).then_inc(stat, 1)

        def ln_stats(g):
            lnl.at(g)
            wait(dve, nx_ready, 2 * g)
            lnl(v.memset(carrier[:], 0.0))
            v.memset(carrier[:], 0.0)
            stats(lambda q: tile_of(g, q), mv1, 0).then_inc(stat, 1)

        def ln_apply(g):
            dve.wait_ge(rs_ready, 3 * g + 1)
            for q in range(G4):
                ins = v.tensor_scalar(x[:, q * D:(q + 1) * D], tile_of(g, q), mv1[:, q, 0:1], rs[:, 0, q:q + 1], ALU.subtract, ALU.mult)
            lnl(ins)
            lnl(stats(lambda q: x[:, q * D:(q + 1) * D], mv2, 1))
            mean_square()

        def scale_rows(g, k):
            dve.wait_ge(rs_ready, 3 * g + 2 + k)
            wait(dve, t_filled, 4 * g + 2 * k)
            for q in range(G4):
                ins = v.tensor_scalar(nx[:, q * D:(q + 1) * D], x[:, q * D:(q + 1) * D], rs[:, 1 + k, q:q + 1], None, ALU.mult)
            ins.then_inc(nx_ready, 1)

        def row_max(g, u):
            for par in range(2):
                if u == 0 and par == 0:
                    nbl.at(g)
                dve.wait_ge(s_done, 4 * g + 2 * u + par + 1)
                wait(dve, nb_ready, 4 * g + 2 * u + par)
                nbl(v.tensor_reduce(smax[:], bank[6 + par][:].rearrange("p (a b) -> p a b", b=TOK), AX_X, ALU.max))
                wait(dve, exp_done, 4 * g + 2 * u + par - 1)
                v.tensor_scalar(nbias[:, par], smax[:], -LSCALE, None, ALU.mult).then_inc(nb_ready, 1)

        def o_norm(g):
            for u in range(2):
                if u == 0:
                    onl.at(g)
                dve.wait_ge(av_done, 2 * g + u + 1)
                wait(dve, on_done, 2 * g + u)
                onl(v.reciprocal(pinv[:], psums[:, 2 * u:2 * u + 2].rearrange("p a b -> p (a b)")))
                wait(dve, ot_filled, 2 * g)
                v.tensor_tensor(ob[:, u * 2 * D:(u + 1) * 2 * D].rearrange("p (a b) -> p a b", b=LD),
                                bank[6 + u][:].rearrange("p (a b) -> p a b", b=LD), bcast(pinv[:], LD, 2), ALU.mult).then_inc(on_done, 1)

        def residual(g):
            dve.wait_ge(wo_done, 2 * g + 2)
            dve.wait_ge(nx_ready, 2 * g + 1)
            for u in range(2):
                xs = x[:, u * 2 * D:(u + 1) * 2 * D]
                ins = v.tensor_tensor(xs, xs, bank[6 + u][:], ALU.add)
            lnl(ins)
            lnl(stats(lambda q: x[:, q * D:(q + 1) * D], mv2, 1))
            mean_square()
            hs = h[:, bass.ds(g * G4 * D, G4 * D)]
            lnl(v.tensor_tensor(hs, hs, x[:], ALU.add))

        def route_shift(m):
            dve.wait_ge(r_done, m + 1)
            rl.at(m)
            wait(dve, acc_done, 4 * NE * m)
            rl(v.tensor_tensor(lg[:], bank[6][:, 0:G4 * EXPERTS].rearrange("p (a b) -> p a b", b=EXPERTS), bcast(rbias[:], G4, 1), ALU.add))
            rl(v.tensor_reduce(r4a[:], lg[:], AX_X, ALU.max))
            v.tensor_tensor(lg[:], lg[:], bcast(r4a[:], EXPERTS, 2), ALU.subtract).then_inc(r_shift, 1)

        def route_top(m):
            dve.wait_ge(r_exp, m + 1)
            rl(v.tensor_reduce(r4a[:], ex[:], AX_X, ALU.add))
            rl(v.reciprocal(r4b[:], r4a[:]))
            rl(v.tensor_tensor(rw[:], ex[:], bcast(r4b[:], EXPERTS, 2), ALU.mult))
            v.memset(carrier[:], 0.0)
            for q in range(G4):
                ins = v.max(top[:, q], rw[:, q])
            rl(ins)
            v.memset(carrier[:], 0.0)
            for q in range(G4):
                ins = v.max_index(topi[:, q], top[:, q], rw[:, q])
            rl(ins)
            v.tensor_tensor(diff[:], top[:, :, 1], top[:, :, 0], ALU.subtract).then_inc(r_diff, 1)

        def route_weights(m):
            dve.wait_ge(r_ediff, m + 1)
            v.tensor_copy(topf[:], topi[:])
            rl(v.tensor_scalar(r4a[:], ediff[:], 1.0, None, ALU.add))
            rl(v.reciprocal(r4b[:], r4a[:]))
            rl(v.tensor_scalar(tw[:, 0], r4b[:], 0.5, None, ALU.mult))
            v.tensor_tensor(tw[:, 1], tw[:, 0], ediff[:], ALU.mult)
            io = bcast(iota8[:], G4, 1)
            v.tensor_tensor(lg[:], io, bcast(topf[:, :, 0], EXPERTS, 2), ALU.is_equal)
            rl(v.tensor_tensor(rw[:], io, bcast(topf[:, :, 1], EXPERTS, 2), ALU.is_equal))
            v.tensor_tensor(lg[:], lg[:], bcast(tw[:, 0], EXPERTS, 2), ALU.mult)
            rl(v.tensor_tensor(rw[:], rw[:], bcast(tw[:, 1], EXPERTS, 2), ALU.mult))
            rl(v.tensor_tensor(comb[:], lg[:], rw[:], ALU.add))

        def hidden(m, n):
            dve.wait_ge(tanh_done, 18 * m + n + 1)
            wait(dve, hid_done, 18 * m + n)
            v.scalar_tensor_tensor(up[:], th[:, n % 2], 1.0, bank[n % 2][:], ALU.add, ALU.mult).then_inc(up_done, 1)
            dve.wait_ge(up_done, 18 * m + n + 1)
            wait(dve, w2_half, 2 * (NE * m + n // 2 - 1))
            v.tensor_tensor(hid[:, (n // 2) % 2, n % 2], up[:], bank[2 + n % 2][:], ALU.mult).then_inc(hid_done, 1)

        def accumulate(m, e):
            for q in range(G4):
                if q % 2 == 0:
                    dve.wait_ge(w2_half, 2 * (NE * m + e) + q // 2 + 1)
                hs = tile_of(m, q)
                c = 0.5 if e == 0 else comb[:, q, e - 1:e]
                v.scalar_tensor_tensor(hs, bank[4 + q // 2][:, (q % 2) * D:(q % 2 + 1) * D], c, hs, ALU.mult, ALU.add).then_inc(acc_done, 1)

        def body(it, j, half, live):
            g, m = it, it - 1
            for n in range(2 * NE):
                if live(1):
                    if n == 0: route_shift(m)
                    if n == 1: route_top(m)
                    if n == 2: route_weights(m)
                if live(0):
                    if n == 0: ln_stats(g)
                    if n == 1: ln_apply(g)
                    if n == 2: scale_rows(g, 0)
                    if n == 6: row_max(g, 0)
                    if n == 9: row_max(g, 1)
                    if n == 12: o_norm(g)
                    if n == 14: residual(g)
                    if n == 16: scale_rows(g, 1)
                if live(1):
                    hidden(m, n)
                    if n >= 3 and n % 2 == 1:
                        accumulate(m, n // 2 - 1)
            if live(1): accumulate(m, NE - 1)
        pipeline(dve, GROUPS, 1, body)

    return acc_done, 4 * NE * GROUPS


PAIRS = SEQS // 2
HH, HD = 8, 32
RT = 4
H2 = 2 * HH
HSCALE = D ** -0.5
QB = 127.0
ROUND = 12582912.0
FLT_MAX = 3.4028235e38


def second_attention(ctx, block, shared, local, b_done, out):
    nc, dram, h, ident, bank = (shared[k] for k in ("nc", "dram", "h", "ident", "bank"))
    eps5, neghalf = shared["eps5"], shared["neghalf"]

    def sb(name, shape, dt=F32):
        return local.enter_context(nc.sbuf_tensor("c_" + name, shape, dt))

    def sem(name):
        return ctx.enter_context(nc.semaphore("c_" + name))

    W = 2 * D
    wbd = sb("wbd", [P, 4, P])
    wo = sb("wo", [P, DC, D])
    pe_t = sb("pe_t", [P, DC, TOK])
    pp = sb("pp", [P, DC, TOK])
    bq, bk, bv = sb("bq", [P, 1]), sb("bk", [P, 1]), sb("bv", [P, 1])
    ub, vb_ = sb("ub", [P, DC]), sb("vb_", [P, DC])
    bqu, bqv = sb("bqu", [P, DC]), sb("bqv", [P, DC])
    bo, bo2 = sb("bo", [1, D]), sb("bo2", [1, D])
    ones = sb("ones", [1, P])
    gamma, beta = sb("gamma", [P, DC]), sb("beta", [P, DC])
    tern_i = sb("tern_i", [P, DC, D], I32)
    tern = sb("tern", [P, DC, D], BF16)
    fbias = sb("fbias", [P, D])
    scale, scale_c, scale_i = sb("scale", [P, 1]), sb("scale_c", [P, 1]), sb("scale_i", [P, 1])
    ident16 = shared["ident16"]
    carrier = sb("carrier", [P, 1])
    st = sb("st", [P, 3, 2, 6])
    mv = sb("mv", [P, 3, 2, 2])
    rtmp, rs = sb("rtmp", [P, 3, 2]), sb("rs", [P, 3, 2])
    x, xn = sb("x", [P, W]), sb("xn", [P, W])
    xnt = sb("xnt", [P, 2, DC, 2 * TOK])
    qu, kt = sb("qu", [P, 2, DC, 2 * TOK]), sb("kt", [P, 2, DC, 2 * TOK])
    qv = sb("qv", [P, DC, 2 * TOK])
    vv = sb("vv", [P, 2, W])
    posb = sb("posb", [P, H2, TOK + 1])
    shifted = sb("shifted", [P, 2, H2 * TOK])
    sc = sb("sc", [P, H2 * TOK])
    probs, pt = sb("probs", [P, H2 * TOK]), sb("pt", [P, H2 * TOK])
    smax, nbias, psums, pinv = (sb(n, [P, H2]) for n in ("smax", "nbias", "psums", "pinv"))
    ob = sb("ob", [P, W])
    ot = sb("ot", [P, DC, 2 * TOK])
    h1 = sb("h1", [P, W])
    hb = sb("hb", [P, 2, W])
    y = sb("y", [P, W])
    yq, yt = sb("yq", [P, W], BF16), sb("yt", [P, DC, 2 * TOK], BF16)
    res = sb("res", [P, 2, W])
    scratch = nc.dram_tensor("scratch", (2, H2, TOK, TOK + 1), F32, kind="Internal").ap()

    s_w, s_z, s_pre, scale_bound = sem("weights"), sem("zero"), sem("pre"), sem("scale_bound")
    stat = [sem(f"stat{i}") for i in range(3)]
    rsr = [sem(f"rs{i}") for i in range(3)]
    pool_link = [sem(f"pool_link{i}") for i in range(3)]
    link_f, link_t, link_h, link_s, link_o = sem("link_front"), sem("link_tail"), sem("link_h1"), sem("link_s"), sem("link_o")
    xn_ready, xt_filled, xt_evac = sem("xn"), sem("xt_filled"), sem("xt_evac")
    q_filled, q_evac, k_filled, k_evac = sem("q_filled"), sem("q_evac"), sem("k_filled"), sem("k_evac")
    v_filled, v_evac = sem("v_filled"), sem("v_evac")
    pos_filled, pos_evac, c_filled, s_added = sem("pos_filled"), sem("pos_evac"), sem("c_filled"), sem("s_added")
    pos_out = [sem(f"pos_out{i}") for i in range(2)]
    shift_in = [sem(f"shift_in{i}") for i in range(2)]
    nb_ready, exp_done = sem("nb"), sem("exp")
    pt_filled, pt_evac_a, pt_evac_d, av_done, on_done = sem("pt_filled"), sem("pt_evac_act"), sem("pt_evac_dve"), sem("av"), sem("on")
    ot_filled, ot_evac, wo_done, h1_done, hb_done = sem("ot_filled"), sem("ot_evac"), sem("wo"), sem("h1"), sem("hb")
    yq_ready, yt_filled, yt_evac, f_done, res_done = sem("yq"), sem("yt_filled"), sem("yt_evac"), sem("ffn"), sem("res")
    out_sem = [sem(f"out{i}") for i in range(2)]

    LOADS = [(wbd[32 * r:32 * r + 32, i, 32 * r:32 * r + 32], dram[n])
             for i, n in enumerate(("c_wq", "c_wk", "c_wv", "c_wp")) for r in range(RT)] + [
        (wo[:], dram["c_wo"]), (pe_t[:], dram["c_pe"]), (bq[:], dram["c_bq"]), (bk[:], dram["c_bk"]), (bv[:], dram["c_bv"]),
        (ub[:], dram["c_u"]), (vb_[:], dram["c_v"]), (bo[:], dram["c_bo"]), (gamma[:], dram["c_gamma"]), (beta[:], dram["c_beta"]),
        (tern_i[:], dram["c_tern"]), (fbias[:], dram["c_fbias"].partition_broadcast(P)),
        (scale[:], dram["c_scale"].partition_broadcast(P)),
    ]
    NL = 16 * len(LOADS)

    @block.sync
    def _(sp):
        sp.wait_ge(*b_done)
        sp.wait_ge(s_z, 1)
        for dst, src in LOADS:
            sp.dma_start(dst, src).then_inc(s_w, 16)

        def body(it, j, half, live):
            s1, s4, o = it - 1, it - 4, 1 - half
            j1 = j if half else j - 1
            if live(1):
                sp.wait_ge(pos_evac, 4 * s1 + 4)
                sp.dma_start(scratch[o].rearrange("i q k -> q i k"), posb[:]).then_inc(pos_out[o], 16)
            if live(4):
                sp.wait_ge(res_done, s4 + 1)
                sp.dma_start(out[bass.ds(2 * s4, 2)].rearrange("s t d -> t s d"),
                             res[:, half].rearrange("p (s d) -> p s d", s=2)).then_inc(out_sem[half], 16)
            if live(1):
                sp.wait_ge(pos_out[o], 16 * (j1 + 1))
                wait(sp, s_added, 4 * (s1 - 1))
                src = scratch[o].rearrange("i q k -> i (q k)")[:, TOK:].rearrange("i (q k) -> q i k", k=TOK)
                dst = shifted[:, o].rearrange("p (i k) -> p i k", k=TOK)
                for q in range(2):
                    sp.dma_start(dst[:, q * HH:(q + 1) * HH], src[:, q * HH:(q + 1) * HH]).then_inc(shift_in[o], 16)
        pipeline(sp, PAIRS, 4, body)
        for i in range(2):
            sp.wait_ge(out_sem[i], 16 * PAIRS // 2)

    @block.gpsimd
    def _(pool):
        g = nc.gpsimd
        pool.wait_ge(*b_done)
        g.memset(ones[:], 1.0)
        g.memset(posb[:, :, 0:1], 0.0)
        g.memset(wbd[:], 0.0).then_inc(s_z, 1)
        lks = [Links(pool, pool_link[n], 1) for n in range(3)]

        def rsqrt(n, s):
            pool.wait_ge(stat[n], s + 1)
            wait(pool, rsr[n], s)
            lks[n].at(s)(g.tensor_tensor(out=rtmp[:, n], in0=mv[:, n, :, 1], in1=eps5[:, 0:2], op=ALU.add))
            g.tensor_tensor(out=rs[:, n], in0=rtmp[:, n], in1=neghalf[:, 0:2], op=ALU.pow).then_inc(rsr[n], 1)

        def body(it, j, half, live):
            if live(0):
                rsqrt(0, it)
                rsqrt(1, it)
            if live(3):
                s3 = it - 3
                rsqrt(2, s3)
                wait(pool, res_done, s3 - 1)
                if isinstance(s3, int) and s3 == 0:
                    pool.wait_ge(s_w, NL)
                for q in range(2):
                    ins = g.tensor_tensor(out=hb[:, 1 - half, q * D:(q + 1) * D], in0=h1[:, q * D:(q + 1) * D], in1=fbias[:], op=ALU.add)
                ins.then_inc(hb_done, 1)
        pipeline(pool, PAIRS, 4, body)

    @block.tensor
    def _(pe):
        t = nc.tensor
        pe.wait_ge(*b_done)
        pe.wait_ge(s_w, NL)
        for c in range(DC):
            t.matmul(bank[4][:, c * TOK:(c + 1) * TOK], wbd[:, 3], pe_t[:, c], start=True, stop=True, skip_group_check=True)
        for c in range(DC):
            t.matmul(bank[5][0:1, 0:D], bv[:], wo[:, c], start=(c == 0), stop=False)
        t.matmul(bank[5][0:1, 0:D], ones[0:1, 0:1], bo[:], start=False, stop=True).then_inc(s_pre, 1)
        pe.wait_ge(s_pre, 3)

        def col(q, c, n=P):
            return slice((2 * q + c) * TOK, (2 * q + c + 1) * TOK)

        def x_transposes(s):
            pe.wait_ge(xn_ready, s + 1)
            wait(pe, v_evac, s - 1)
            for c in range(DC):
                for q in range(2):
                    ins = t.transpose(bank[6][:, c * 2 * TOK + q * TOK:c * 2 * TOK + (q + 1) * TOK],
                                      xn[:, q * D + c * P:q * D + (c + 1) * P], ident[:])
            ins.then_inc(xt_filled, 1)

        def project(s, o, w, filled, waits):
            for sm, val in waits:
                pe.wait_ge(sm, val)
            t.matmul(bank[6][:], wbd[:, w], xnt[:, o].rearrange("p a b -> p (a b)"), start=True, stop=True).then_inc(filled, 1)

        def v_proj(s, half):
            wait(pe, k_evac, s + 2, PAIRS)
            for q in range(2):
                for c in range(DC):
                    ins = t.matmul(bank[6][:, q * D + c * P:q * D + (c + 1) * P], xnt[:, half, c, q * TOK:(q + 1) * TOK],
                                   wbd[:, 2], start=True, stop=True, skip_group_check=True)
            ins.then_inc(v_filled, 1)

        def position_scores(s, o):
            pe.wait_ge(q_evac, 4 * s + 4)
            wait(pe, s_added, 4 * (s - 1))
            for q in range(2):
                for c in range(DC):
                    for r in range(RT):
                        rows = slice(32 * r, 32 * r + 32)
                        ins = t.matmul(bank[r][:, col(q, c)], qv[rows, c, q * TOK:(q + 1) * TOK], pp[rows, c],
                                       start=True, stop=True, skip_group_check=True)
                        if q == 1 and c == 1:
                            ins.then_inc(pos_filled, 1)

        def content_scores(s, half):
            wait(pe, pos_evac, 4 * (s + 2), 4 * PAIRS)
            for q in range(2):
                for c in range(DC):
                    for r in range(RT):
                        rows, cols = slice(32 * r, 32 * r + 32), slice(q * TOK, (q + 1) * TOK)
                        ins = t.matmul(bank[r][:, col(q, c)], qu[rows, half, c, cols], kt[rows, half, c, cols],
                                       start=True, stop=True, skip_group_check=True)
                        if q == 1 and c == 1:
                            ins.then_inc(c_filled, 1)

        def p_transposes(s, k):
            if k == 0:
                pe.wait_ge(exp_done, s + 1)
            if k < 2:
                wait(pe, (pt_evac_a, pt_evac_d)[k], 2 * s)
            else:
                pe.wait_ge((pt_evac_a, pt_evac_d)[k - 2], 2 * s + 1)
            for i in range(4):
                hd = 4 * k + i
                ins = t.transpose(bank[4 + k % 2][:, i * TOK:(i + 1) * TOK], probs[:, hd * TOK:(hd + 1) * TOK], ident[:])
            ins.then_inc(pt_filled, 1)

        def values(s, o):
            pe.wait_ge(pt_evac_a, 2 * s + 2)
            pe.wait_ge(pt_evac_d, 2 * s + 2)
            pe.wait_ge(v_evac, s + 1)
            wait(pe, h1_done, s)
            for hd in range(H2):
                ins = t.matmul(bank[7][:, hd * HD:(hd + 1) * HD], pt[:, hd * TOK:(hd + 1) * TOK],
                               vv[:, o, hd * HD:(hd + 1) * HD], start=True, stop=True, skip_group_check=True)
            ins.then_inc(av_done, 1)

        def o_transposes(s):
            pe.wait_ge(on_done, s + 1)
            for c in range(DC):
                for q in range(2):
                    ins = t.transpose(bank[7][:, c * 2 * TOK + q * TOK:c * 2 * TOK + (q + 1) * TOK],
                                      ob[:, q * D + c * P:q * D + (c + 1) * P], ident[:])
            ins.then_inc(ot_filled, 1)

        def y_transposes(s):
            pe.wait_ge(yq_ready, s + 1)
            wait(pe, ot_evac, s + 2, PAIRS)
            b16 = bank[7][:].bitcast(BF16)
            for c in range(DC):
                for q in range(2):
                    ins = t.transpose(b16[:, c * 2 * TOK + q * TOK:c * 2 * TOK + (q + 1) * TOK],
                                      yq[:, q * D + c * P:q * D + (c + 1) * P], ident16[:])
            ins.then_inc(yt_filled, 1)

        def ffn(s):
            pe.wait_ge(yt_evac, s + 1)
            for q in range(2):
                for c in range(DC):
                    ins = t.matmul(bank[7][:, q * D:(q + 1) * D], yt[:, c, q * TOK:(q + 1) * TOK], tern[:, c],
                                   start=(c == 0), stop=(c == DC - 1), skip_group_check=True)
            ins.then_inc(f_done, 1)

        def out_proj(s):
            pe.wait_ge(ot_evac, s + 1)
            wait(pe, res_done, s)
            for q in range(2):
                for c in range(DC):
                    t.matmul(bank[7][:, q * D:(q + 1) * D], ot[:, c, q * TOK:(q + 1) * TOK], wo[:, c],
                             start=(c == 0), stop=False, skip_group_check=True)
                ins = t.matmul(bank[7][:, q * D:(q + 1) * D], ones[:], bo2[:], start=False, stop=True, skip_group_check=True)
            ins.then_inc(wo_done, 1)

        def body(it, j, half, live):
            s1, s2, s3, s4, o = it - 1, it - 2, it - 3, it - 4, 1 - half
            if live(1): x_transposes(s1)
            if live(3):
                p_transposes(s3, 0)
                p_transposes(s3, 1)
            if live(1): project(s1, o, 0, q_filled, [(xt_evac, 2 * s1 + 2)])
            if live(3):
                p_transposes(s3, 2)
                p_transposes(s3, 3)
            if live(1): project(s1, o, 1, k_filled, [(q_evac, 4 * s1 + 4)])
            if live(3): values(s3, o)
            if live(1): position_scores(s1, o)
            if live(2): v_proj(s2, half)
            if live(3): o_transposes(s3)
            if live(4):
                y_transposes(s4)
                ffn(s4)
            if live(2): content_scores(s2, half)
            if live(3): out_proj(s3)
        pipeline(pe, PAIRS, 4, body)

    @block.scalar
    def _(act):
        a = nc.scalar
        act.wait_ge(*b_done)
        act.wait_ge(s_w, NL)
        act.wait_ge(s_pre, 4)

        def xt_copy(s, o):
            for c in range(DC):
                act.wait_ge(xt_filled, s + 1)
                wait(act, v_filled, s - 1)
                a.activation(xnt[:, o, c], bank[6][:, c * 2 * TOK:(c + 1) * 2 * TOK], ACT.Identity,
                             scale=gamma[:, c:c + 1], bias=beta[:, c:c + 1]).then_inc(xt_evac, 1)

        def q_copy(s, o):
            act.wait_ge(q_filled, s + 1)
            wait(act, pos_filled, 4 * s)
            wait(act, c_filled, 4 * (s - 1))
            for dst, bias in ((qu[:, o], bqu), (qv, bqv)):
                for c in range(DC):
                    a.activation(dst[:, c], bank[6][:, c * 2 * TOK:(c + 1) * 2 * TOK], ACT.Identity,
                                 bias=bias[:, c:c + 1]).then_inc(q_evac, 1)

        def pt_copy(s, k):
            act.wait_ge(pt_filled, 4 * s + k + 1)
            wait(act, av_done, s)
            a.activation(pt[:, 4 * k * TOK:4 * (k + 1) * TOK], bank[4 + k % 2][:], ACT.Copy).then_inc(pt_evac_a, 1)

        def pos_copy(s, r):
            act.wait_ge(pos_filled, 4 * s + r + 1)
            if r == 0:
                if isinstance(s, int):
                    for i in range(2):
                        wait(act, pos_out[i], 16 * ((s + 1 - i) // 2))
                else:
                    act.wait_ge(pos_out[pos_copy.other], 16 * pos_copy.count)
            dst = posb[:].rearrange("p (a r) k -> p a r k", r=RT)[:, :, r, 1:TOK + 1]
            a.activation(dst, bank[r][:].rearrange("p (a k) -> p a k", k=TOK), ACT.Copy).then_inc(pos_evac, 1)

        def ot_copy(s):
            act.wait_ge(ot_filled, s + 1)
            wait(act, wo_done, s)
            a.activation(ot[:].rearrange("p a b -> p (a b)"), bank[7][:], ACT.Copy).then_inc(ot_evac, 1)

        def yt_copy(s):
            act.wait_ge(yt_filled, s + 1)
            wait(act, f_done, s)
            a.activation(yt[:].rearrange("p a b -> p (a b)"), bank[7][:].bitcast(BF16)[:, 0:W], ACT.Copy).then_inc(yt_evac, 1)

        def exps(s):
            act.wait_ge(nb_ready, s + 1)
            wait(act, pt_filled, 4 * s)
            for i in range(H2):
                ins = a.activation(probs[:, i * TOK:(i + 1) * TOK], sc[:, i * TOK:(i + 1) * TOK], ACT.Exp,
                                   bias=nbias[:, i:i + 1], scale=HSCALE, accum_out=psums[:, i:i + 1])
            ins.then_inc(exp_done, 1)

        def body(it, j, half, live):
            s1, s2, s3, s4, o = it - 1, it - 2, it - 3, it - 4, 1 - half
            if live(1): xt_copy(s1, o)
            if live(3): pt_copy(s3, 0)
            if live(1): q_copy(s1, o)
            if live(3): pt_copy(s3, 2)
            if live(1):
                pos_copy.other, pos_copy.count = half, (j if half == 0 else j)
                for r in range(RT):
                    pos_copy(s1, r)
            if live(3): ot_copy(s3)
            if live(4): yt_copy(s4)
            if live(2): exps(s2)
        pipeline(act, PAIRS, 4, body)

    @block.vector
    def _(dve):
        v = nc.vector
        dve.wait_ge(*b_done)
        dve.wait_ge(s_w, NL)
        v.tensor_tensor(bqu[:], ub[:], bcast(bq[:, 0], DC, 1), ALU.add)
        v.tensor_tensor(bqv[:], vb_[:], bcast(bq[:, 0], DC, 1), ALU.add)
        v.tensor_scalar(tern[:].rearrange("p a b -> p (a b)"), tern_i[:].rearrange("p a b -> p (a b)"), -1.0, None, ALU.add)
        v.tensor_scalar(scale_c[:], scale[:], 1e-5, FLT_MAX, ALU.max, ALU.min).then_inc(scale_bound, 1)
        dve.wait_ge(scale_bound, 1)
        v.reciprocal(scale_i[:], scale_c[:])
        dve.wait_ge(s_pre, 1)
        v.tensor_copy(pp[:].rearrange("p a b -> p (a b)"), bank[4][:, 0:DC * TOK]).then_inc(s_pre, 1)
        v.tensor_copy(bo2[:], bank[5][0:1, 0:D]).then_inc(s_pre, 1)
        v.memset(carrier[:], 0.0).then_inc(s_pre, 1)
        dve.wait_ge(s_pre, 4)

        lf, lh, lt = Links(dve, link_f, 6), Links(dve, link_h, 2), Links(dve, link_t, 4)
        ls, lo = Links(dve, link_s, 1), Links(dve, link_o, 1)

        def pair(s):
            return h[:, bass.ds(s * W, W)]

        def stats(link, src, n):
            for q in range(2):
                ins = v.bn_stats(st[:, n, q], src[:, q * D:(q + 1) * D])
            link(ins)
            v.memset(carrier[:], 0.0)
            for q in range(2):
                ins = v.bn_aggr(mv[:, n, q], st[:, n, q])
            ins.then_inc(stat[n], 1)

        def normalise(dst, src, n):
            for q in range(2):
                ins = v.tensor_scalar(dst[:, q * D:(q + 1) * D], src[:, q * D:(q + 1) * D], mv[:, n, q, 0:1], rs[:, n, q:q + 1],
                                      ALU.subtract, ALU.mult)
            return ins

        def front_a(s):
            lf.at(s)
            wait(dve, xn_ready, s)
            lf(v.memset(carrier[:], 0.0))
            lf(v.memset(carrier[:], 0.0))
            v.memset(carrier[:], 0.0)
            stats(lf, pair(s), 0)

        def front_b(s):
            dve.wait_ge(rsr[0], s + 1)
            lf(normalise(x, pair(s), 0))
            lf_stats_link = lf
            stats(lf_stats_link, x, 1)

        def front_c(s):
            dve.wait_ge(rsr[1], s + 1)
            wait(dve, xt_filled, s)
            lf(v.memset(carrier[:], 0.0))
            normalise(xn, x, 1).then_inc(xn_ready, 1)

        def pt_copy(s, k):
            dve.wait_ge(pt_filled, 4 * s + k + 1)
            wait(dve, av_done, s)
            v.tensor_copy(pt[:, 4 * k * TOK:4 * (k + 1) * TOK], bank[4 + k % 2][:]).then_inc(pt_evac_d, 1)

        def k_copy(s, o):
            dve.wait_ge(k_filled, s + 1)
            wait(dve, c_filled, 4 * (s - 1))
            v.tensor_scalar(kt[:, o].rearrange("p a b -> p (a b)"), bank[6][:], bk[:, 0:1], None, ALU.add).then_inc(k_evac, 1)

        def v_copy(s, half):
            dve.wait_ge(v_filled, s + 1)
            wait(dve, av_done, s - 1)
            v.tensor_copy(vv[:, half], bank[6][:]).then_inc(v_evac, 1)

        def add_scores(s, half, j):
            ls.at(s)
            for r in range(RT):
                dve.wait_ge(c_filled, 4 * s + r + 1)
                if r == 0:
                    dve.wait_ge(shift_in[half], 32 * j)
                    wait(dve, exp_done, s)
                view = lambda b: b.rearrange("p (a r k) -> p a r k", r=RT, k=TOK)[:, :, r]
                v.tensor_tensor(view(sc[:]), bank[r][:].rearrange("p (a k) -> p a k", k=TOK), view(shifted[:, half]),
                                ALU.add).then_inc(s_added, 1)
            dve.wait_ge(s_added, 4 * s + 4)
            ls(v.tensor_reduce(smax[:], sc[:].rearrange("p (a k) -> p a k", k=TOK), AX_X, ALU.max))
            v.tensor_scalar(nbias[:], smax[:], -HSCALE, None, ALU.mult).then_inc(nb_ready, 1)

        def o_norm(s):
            dve.wait_ge(av_done, s + 1)
            wait(dve, on_done, s)
            lo.at(s)(v.reciprocal(pinv[:], psums[:]))
            wait(dve, ot_filled, s)
            v.tensor_tensor(ob[:].rearrange("p (a b) -> p a b", b=HD), bank[7][:].rearrange("p (a b) -> p a b", b=HD),
                            bcast(pinv[:], HD, 2), ALU.mult).then_inc(on_done, 1)

        def residual(s):
            dve.wait_ge(wo_done, s + 1)
            wait(dve, hb_done, s)
            v.tensor_tensor(h1[:], bank[7][:], pair(s), ALU.add).then_inc(h1_done, 1)
            dve.wait_ge(h1_done, s + 1)
            lh.at(s)(v.memset(carrier[:], 0.0))
            stats(lh, h1, 2)

        def quantise(s):
            dve.wait_ge(rsr[2], s + 1)
            lt.at(s)
            wait(dve, yq_ready, s)
            lt(normalise(y, h1, 2))
            lt(v.tensor_scalar(y[:], y[:], scale_i[:, 0:1], QB, ALU.mult, ALU.min))
            lt(v.tensor_scalar(y[:], y[:], -QB, ROUND, ALU.max, ALU.add))
            wait(dve, yt_filled, s)
            lt(v.memset(carrier[:], 0.0))
            v.tensor_scalar(yq[:], y[:], ROUND, None, ALU.subtract).then_inc(yq_ready, 1)

        def finish(s, half, j):
            dve.wait_ge(f_done, s + 1)
            dve.wait_ge(hb_done, s + 1)
            wait(dve, out_sem[half], 16 * (j - 2))
            v.scalar_tensor_tensor(res[:, half], bank[7][:], scale_c[:, 0:1], hb[:, half], ALU.mult, ALU.add).then_inc(res_done, 1)

        def body(it, j, half, live):
            s1, s2, s3, s4, o = it - 1, it - 2, it - 3, it - 4, 1 - half
            if live(4): quantise(s4)
            if live(0): front_a(it)
            if live(3):
                pt_copy(s3, 1)
                pt_copy(s3, 3)
            if live(1): k_copy(s1, o)
            if live(0): front_b(it)
            if live(3): o_norm(s3)
            if live(2): v_copy(s2, half)
            if live(0): front_c(it)
            if live(4): finish(s4, half, j)
            if live(2): add_scores(s2, half, j)
            if live(3): residual(s3)
        pipeline(dve, PAIRS, 4, body)


def layout(inputs):
    import numpy as np

    def a(name):
        return np.asarray(inputs[name])

    def rows(w):
        return np.moveaxis(w.reshape(-1, P, *w.shape[1:]), 0, 1)
    freq = (np.float32(1.0) / np.float32(10000.0) ** (np.arange(0, AD, 2, dtype=np.float32) / np.float32(AD))).astype(np.float32)
    ang = np.arange(TOK, dtype=np.float32)[:, None] * freq
    cos, sin = np.cos(ang).astype(np.float32), np.sin(ang).astype(np.float32)
    div = np.exp(np.arange(0, D, 2, dtype=np.float32) * np.float32(-np.log(10000.0) / D)).astype(np.float32)
    pe = np.zeros((TOK, D), np.float32)
    pe[:, 0::2] = np.sin(np.arange(TOK, dtype=np.float32)[:, None] * div)
    pe[:, 1::2] = np.cos(np.arange(TOK, dtype=np.float32)[:, None] * div)
    arrays = {
        "idm": np.stack([a("x"), a("mask_BS_i1_0")], 1),
        "ident": np.eye(P, dtype=np.float32),
        "vocab_id": np.tile(np.arange(32, dtype=np.float32), 2)[:, None],
        "causal": np.where(np.tril(np.ones((TOK, TOK), bool)), 0.0, -1e30).astype(np.float32),
        "rope": np.stack([np.concatenate([cos, cos], 1), np.concatenate([-sin, sin], 1)], 1),
        "emb_t": a("L0_tok_emb").T, "pca_t": a("L0_tok_pca_lookup").T, "proj_w": a("L0_tok_proj_w"),
        "proj_b": a("L0_tok_proj_b").reshape(DC, P).T, "fus_w": a("L0_tok_fus_w"), "fus_b": a("L0_tok_fus_b")[None],
        "ln_g": a("L0_tok_ln_g"), "ln_b": a("L0_tok_ln_b"),
        "qk_norm": np.stack([a("L0_attn_q_norm_w"), a("L0_attn_k_norm_w")]),
        "l_wq": rows(a("L0_ffn_Wq").T), "l_wk": rows(a("L0_ffn_Wkc").T), "l_wv": rows(a("L0_ffn_Wvc").T),
        "l_wo": rows(a("L0_ffn_Wo").T), "l_wr": rows(a("L0_ffn_Wr").T),
        "l_g1": a("L0_ffn_g1").reshape(DC, P).T, "l_g2": a("L0_ffn_g2").reshape(DC, P).T,
        "l_rbias": a("L0_ffn_expert_bias"), "iota8": np.arange(EXPERTS, dtype=np.float32),
        "l_sw1": rows(a("L0_ffn_sW1").T), "l_sw3": rows(a("L0_ffn_sW3").T), "l_sw2": rows(a("L0_ffn_sW2").T),
        "l_ew1": rows(a("L0_ffn_eW1").reshape(-1, D).T), "l_ew3": rows(a("L0_ffn_eW3").reshape(-1, D).T),
        "l_ew2": rows(a("L0_ffn_eW2").transpose(2, 0, 1)),
        "c_wq": a("L1_attn_Wq"), "c_wk": a("L1_attn_Wk"), "c_wv": a("L1_attn_Wv"), "c_wp": a("L1_attn_Wp"),
        "c_wo": rows(a("L1_attn_Wo")), "c_pe": rows(np.ascontiguousarray(pe.T)),
        "c_bq": np.tile(a("L1_attn_bq"), RT)[:, None], "c_bk": np.tile(a("L1_attn_bk"), RT)[:, None],
        "c_bv": np.tile(a("L1_attn_bv"), RT)[:, None],
        "c_u": a("L1_attn_u_bias").reshape(DC, P).T, "c_v": a("L1_attn_v_bias").reshape(DC, P).T,
        "c_bo": a("L1_attn_bo")[None], "c_gamma": a("L1_attn_ln_gamma").reshape(DC, P).T,
        "c_beta": a("L1_attn_ln_beta").reshape(DC, P).T, "c_tern": rows(a("L1_ffn_ternary_weight").T),
        "c_fbias": a("L1_ffn_bias"), "c_scale": a("L1_ffn_act_scale").reshape(1),
        "wqkv_t": a("L0_attn_wqkv").T, "wo_t": a("L0_attn_wo").T,
    }
    return {k: np.ascontiguousarray(v) for k, v in arrays.items()}


def kernel(**inputs):
    import numpy as _np
    import concourse.bacc as _bacc
    from concourse import mybir as _mybir
    from concourse.bass_utils import run_bass_kernel_spmd as _run

    nc = _bacc.Bacc("TRN2", target_bir_lowering=False, num_devices=1)
    arrays = layout(inputs)
    dram = {k: nc.dram_tensor("in_" + k, v.shape, _mybir.dt.from_np(v.dtype), kind="ExternalInput").ap() for k, v in arrays.items()}
    out = nc.dram_tensor("out", (SEQS, TOK, D), F32, kind="ExternalOutput").ap()
    program(nc, dram, out)
    r = _run(nc, [{"in_" + k: v for k, v in arrays.items()}], core_ids=[0])
    return r.results[0]["out"]
```

```python
from contextlib import ExitStack

import concourse.bass as bass
from concourse import mybir

P = 128
ALU = mybir.AluOpType
ACT = mybir.ActivationFunctionType
AX_X = mybir.AxisListType.X
F32 = mybir.dt.float32
BF16 = mybir.dt.bfloat16
I32 = mybir.dt.int32
U32 = mybir.dt.uint32

SEQS = 64
TOK = 128
D = 256
DC = D // P
VOCAB = 28
PCA = 20
AH, AD = 16, 64
ATTN_GROUPS = 4
QKV_CHUNKS = 6
BANK = 512


def pipeline(eng, steps, skew, body, peel=2):
    first = max(skew + skew % 2, peel)
    last = steps - steps % 2
    for it in range(first):
        body(it, it // 2, it % 2, lambda off, it=it: 0 <= it - off < steps)
    with eng.Fori(first // 2, last // 2) as j:
        for half in range(2):
            body(2 * j + half, j, half, lambda off: True)
    for it in range(last, steps + skew):
        body(it, it // 2, it % 2, lambda off, it=it: 0 <= it - off < steps)


def wait(eng, sem, value, most=None):
    if isinstance(value, int):
        if most is not None:
            value = min(value, most)
        if value <= 0:
            return
    eng.wait_ge(sem, value)


class Chain:

    def __init__(self, sem):
        self.sem, self.used = sem, 0


class Links:

    def __init__(self, eng, chain, per_step, steps):
        self.eng, self.sem, self.per_step, self.k = eng, chain.sem, per_step, 0
        self.base = chain.used
        chain.used += per_step * steps

    def at(self, step):
        assert self.k in (0, self.per_step), (self.k, self.per_step)
        self.step, self.k = step, 0
        return self

    def __call__(self, ins):
        self.k += 1
        ins.then_inc(self.sem, 1)
        self.eng.wait_ge(self.sem, self.base + self.step * self.per_step + self.k)


def bcast(ap, n, axis):
    return ap.unsqueeze(axis).broadcast_to([*ap.shape[:axis], n, *ap.shape[axis:]])


def program(nc, dram, out):
    with ExitStack() as ctx:
        h = ctx.enter_context(nc.sbuf_tensor("h", [P, SEQS * D], F32))
        ident = ctx.enter_context(nc.sbuf_tensor("ident", [P, P], F32))
        ident16 = ctx.enter_context(nc.sbuf_tensor("ident16", [P, P], BF16))
        bank = [ctx.enter_context(nc.psum_tensor(f"bank{i}", [P, BANK], F32)) for i in range(8)]
        eps5 = ctx.enter_context(nc.sbuf_tensor("eps5", [P, AH], F32))
        eps6 = ctx.enter_context(nc.sbuf_tensor("eps6", [P, AH], F32))
        neghalf = ctx.enter_context(nc.sbuf_tensor("neghalf", [P, AH], F32))
        pos_all = ctx.enter_context(nc.sbuf_tensor("pos_all", [P, (GROUPS + 1) * 2 * G4], U32))
        tw_all = ctx.enter_context(nc.sbuf_tensor("tw_all", [P, GROUPS * 2 * G4], F32))
        sorted_y = nc.dram_tensor("sorted_y", (TILES * P, D), F32, kind="Internal").ap()
        carried = ctx.enter_context(nc.semaphore("carried"))
        dve_chain = [Chain(ctx.enter_context(nc.semaphore(f"dve_chain{i}"))) for i in range(6)]
        pool_chain = [Chain(ctx.enter_context(nc.semaphore(f"pool_chain{i}"))) for i in range(3)]
        shared = dict(dve_chain=dve_chain, pool_chain=pool_chain, carried=carried, pos_all=pos_all, tw_all=tw_all, sorted_y=sorted_y, ident16=ident16, nc=nc, dram=dram, h=h, ident=ident, bank=bank, eps5=eps5, eps6=eps6, neghalf=neghalf)
        block = ctx.enter_context(nc.Block())
        with ExitStack() as local:
            done = first_attention(ctx, block, shared, local)
        with ExitStack() as local:
            done = experts(ctx, block, shared, local, done)
        with ExitStack() as local:
            second_attention(ctx, block, shared, local, done, out)


def first_attention(ctx, block, shared, local):
    nc, dram, h, ident, bank = (shared[k] for k in ("nc", "dram", "h", "ident", "bank"))
    eps5, eps6, neghalf = (shared[k] for k in ("eps5", "eps6", "neghalf"))

    def sb(name, shape, dt=F32):
        return local.enter_context(nc.sbuf_tensor(name, shape, dt))

    def sem(name):
        return ctx.enter_context(nc.semaphore(name))

    wqkv = sb("wqkv", [P, DC, 3 * AH * AD])
    wo = sb("wo", [P, AH * AD // P, D])
    table = sb("table", [64, D])
    gain, shift = sb("tok_gain", [P, D]), sb("tok_shift", [P, D])
    rope_cs = sb("rope_cs", [P, 2, AD])
    norm_w = sb("norm_w", [P, 2, AD])
    rope_c = sb("rope_c", [P, 2, AD])
    rope_s = sb("rope_s", [P, 2, AD])
    causal = sb("causal", [P, BANK], BF16)
    causal_f = sb("causal_f", [P, TOK])
    ident16 = shared["ident16"]
    emb_t = sb("emb_t", [P, DC, VOCAB])
    pca_t = sb("pca_t", [PCA, VOCAB])
    proj_w = sb("proj_w", [PCA, D])
    proj_b = sb("proj_b", [P, DC])
    fus = sb("fus", [P, 2 * DC, D])
    fus_b = sb("fus_b", [1, D])
    cont_t = sb("cont_t", [P, DC, VOCAB])
    proj_bv = sb("proj_bv", [P, DC, VOCAB])
    onesv = sb("onesv", [P, P])
    idm = sb("idm", [64, 2, 2, TOK], I32)
    vocab_id = sb("vocab_id", [64, 1])
    hot = sb("hot", [64, TOK])
    mlen = sb("mlen", [64, TOK])
    mpad = sb("mpad", [64, TOK + 2])
    hpad = sb("hpad", [64, TOK + 2])
    wsum = sb("wsum", [64, TOK])
    msum = sb("msum", [64, TOK])
    minv = sb("minv", [64, TOK])
    ohw = sb("ohw", [64, 2, TOK])
    st6, mv0, mv1 = sb("st6", [P, 2, 6]), sb("mv0", [P, 2]), sb("mv1", [P, 2])
    carrier = sb("carrier", [P, 1])
    rstd = sb("rstd", [P, 4])
    hx = sb("hx", [P, 2, D])
    xin = sb("xin", [P, D])
    xt = sb("xt", [P, 2, DC, TOK])
    sq = sb("sq", [P, 2, BANK])
    ssq = sb("ssq", [P, 4, 8])
    rsh = sb("rsh", [P, 4, 8])
    rtmp = sb("rtmp", [P, 16])
    t1, t2 = sb("t1", [P, BANK]), sb("t2", [P, BANK])
    roped = sb("roped", [P, 2, 4, BANK])
    vbuf = sb("vbuf", [P, 2, 2, BANK])
    qscale = sb("qscale", [P, 2, AH])
    qkt = sb("qkt", [P, 4, BANK])
    smax, nbias = sb("smax", [P, 4]), sb("nbias", [P, 2, 4])
    probs = sb("probs", [P, 2, 4, TOK])
    probs_t = sb("probs_t", [P, 2, 4, TOK])
    psums = sb("psums", [P, 2, AH])
    pinv = sb("pinv", [P, 8])
    obuf = sb("obuf", [P, AH * AD])
    ot = sb("ot", [P, AH * AD // P, TOK])

    s_w = sem("a_weights")
    s_const = sem("a_const")
    s_tab = sem("a_table")
    s_ropetab = sem("a_rope_tables")
    s_idm = [sem(f"a_idm{i}") for i in range(2)]
    hot_pre, len_clipped = sem("a_hot_pre"), sem("a_len_clipped")
    hot_ready, hot_link = sem("a_hot_ready"), sem("a_hot_link")
    f_done, ln0_read = sem("a_fused"), sem("a_fused_read")
    ln_stat, pool_link = sem("a_ln_stat"), sem("a_pool_link")
    xin_ready, xt_filled, xt_evac = sem("a_xin"), sem("a_xt_filled"), sem("a_xt_evac")
    qkv_filled, sq_done, ssq_done, rs_ready = sem("a_qkv"), sem("a_sq"), sem("a_ssq"), sem("a_rs")
    rope_read, roped_done, v_evac = sem("a_rope_read"), sem("a_roped"), sem("a_v")
    qkt_filled, qkt_evac = sem("a_qkt_filled"), sem("a_qkt_evac")
    s_done, nb_ready, exp_done = sem("a_scores"), sem("a_nbias"), sem("a_exp")
    pt_filled, pt_evac, av_done = sem("a_pt_filled"), sem("a_pt_evac"), sem("a_av")
    on_done = sem("a_on")
    ot_filled, ot_evac, wo_done, stored = sem("a_ot_filled"), sem("a_ot_evac"), sem("a_wo"), sem("a_stored")

    LOADS = [
        (ident[:], dram["ident"]), (vocab_id[:], dram["vocab_id"]), (emb_t[:], dram["emb_t"].rearrange("(c p) v -> p c v", p=P)),
        (pca_t[:], dram["pca_t"]), (proj_w[:], dram["proj_w"]), (proj_b[:], dram["proj_b"]),
        (fus[:], dram["fus_w"].rearrange("(c p) n -> p c n", p=P)), (fus_b[:], dram["fus_b"]),
        (gain[:], dram["ln_g"].partition_broadcast(P)), (shift[:], dram["ln_b"].partition_broadcast(P)),
        (rope_cs[:], dram["rope"]), (norm_w[:], dram["qk_norm"].partition_broadcast(P)),
        (causal_f[:], dram["causal"]),
        (wqkv[:], dram["wqkv_t"].rearrange("(c p) n -> p c n", p=P)),
        (wo[:], dram["wo_t"].rearrange("(c p) n -> p c n", p=P)),
    ]
    NL = 16 * len(LOADS)

    @block.sync
    def _(sp):
        for dst, src in LOADS:
            sp.dma_start(dst, src).then_inc(s_w, 16)

        def body(it, j, half, live):
            if live(0):
                wait(sp, hot_pre, it - 1)
                sp.dma_start(idm[:, half], dram["idm"][it].partition_broadcast(64)).then_inc(s_idm[half], 16)
        pipeline(sp, SEQS, 0, body)

    @block.gpsimd
    def _(pool):
        g = nc.gpsimd
        for t, v in ((eps5, 1e-5), (eps6, 1e-6), (neghalf, -0.5), (onesv, 1.0), (mpad, 0.0), (hpad, 0.0)):
            g.memset(t[:], v).then_inc(s_const, 1)
        pool.wait_ge(s_const, 6)
        link = Links(pool, Chain(hot_link), 4, SEQS)
        plink = Links(pool, Chain(pool_link), 2, 2 * SEQS)
        rlink = Links(pool, shared["pool_chain"][0], 4, SEQS)

        def hot_sums(s):
            lk = link.at(s)
            pool.wait_ge(hot_pre, s + 1)
            lk(g.tensor_tensor(out=hpad[:, 1:TOK + 1], in0=hot[:], in1=mpad[:, 1:TOK + 1], op=ALU.mult))
            g.tensor_tensor(out=wsum[:], in0=hpad[:, 0:TOK], in1=hpad[:, 1:TOK + 1], op=ALU.add)
            lk(g.tensor_tensor(out=msum[:], in0=mpad[:, 0:TOK], in1=mpad[:, 1:TOK + 1], op=ALU.add))
            g.tensor_tensor(out=wsum[:], in0=wsum[:], in1=hpad[:, 2:TOK + 2], op=ALU.add)
            lk(g.tensor_tensor(out=msum[:], in0=msum[:], in1=mpad[:, 2:TOK + 2], op=ALU.add))

        def hot_mean(s, half):
            pool.wait_ge(len_clipped, s + 1)
            wait(pool, f_done, s - 1)
            link(g.tensor_tensor(out=ohw[:, half], in0=wsum[:], in1=minv[:], op=ALU.mult))
            g.tensor_tensor(out=ohw[0:32, half], in0=hot[0:32], in1=onesv[0:32, :], op=ALU.mult).then_inc(hot_ready, 1)

        def ln_rsqrt(n, src, dst):
            lk = plink.at(n)
            pool.wait_ge(ln_stat, n + 1)
            lk(g.tensor_tensor(out=rstd[:, dst + 2:dst + 3], in0=src, in1=eps5[:, 0:1], op=ALU.add))
            lk(g.tensor_tensor(out=rstd[:, dst:dst + 1], in0=rstd[:, dst + 2:dst + 3], in1=neghalf[:, 0:1], op=ALU.pow))

        def head_rsqrt(s, c):
            pool.wait_ge(ssq_done, 4 * s + c + 1)
            wait(pool, rs_ready, 4 * s + c)
            rlink_(g.tensor_tensor(out=rtmp[:, 0:8], in0=ssq[:, c], in1=eps6[:, 0:8], op=ALU.add))
            g.tensor_tensor(out=rsh[:, c], in0=rtmp[:, 0:8], in1=neghalf[:, 0:8], op=ALU.pow).then_inc(rs_ready, 1)

        def body(it, j, half, live):
            nonlocal rlink_
            if live(2):
                rlink_ = rlink.at(it - 2)
            for c in range(4):
                if live(2):
                    head_rsqrt(it - 2, c)
                if c == 1 and live(1):
                    ln_rsqrt(2 * (it - 1), mv0[:, 1:2], 0)
                if c == 3 and live(1):
                    ln_rsqrt(2 * (it - 1) + 1, mv1[:, 1:2], 1)
                if c == 0 and live(0):
                    hot_sums(it)
            if live(0):
                hot_mean(it, half)
        rlink_ = None
        pipeline(pool, SEQS, 3, body)

    @block.tensor
    def _(pe):
        t = nc.tensor
        pe.wait_ge(s_w, NL)
        for c in range(DC):
            ins = t.matmul(bank[c][:, 0:VOCAB], proj_w[:, c * P:(c + 1) * P], pca_t[:], start=True, stop=True)
        ins.then_inc(s_tab, 1)
        pe.wait_ge(s_const, 6)
        pe.wait_ge(s_tab, 4)
        for c in range(DC):
            t.matmul(bank[2][0:VOCAB, 0:D], emb_t[:, c], fus[:, c], start=(c == 0), stop=False)
            t.matmul(bank[2][0:VOCAB, 0:D], proj_bv[:, c], fus[:, DC + c], start=False, stop=False)
        t.matmul(bank[2][0:VOCAB, 0:D], onesv[0:1, 0:VOCAB], fus_b[:], start=False, stop=True).then_inc(s_tab, 1)
        for c in range(DC):
            ins = t.matmul(bank[3][32:32 + VOCAB, 0:D], cont_t[:, c], fus[:, DC + c], start=(c == 0), stop=(c == DC - 1))
        ins.then_inc(s_tab, 1)
        pe.wait_ge(s_tab, 8)
        pe.wait_ge(s_ropetab, 4)

        def fused(s, half):
            pe.wait_ge(hot_ready, s + 1)
            wait(pe, stored, s - 2)
            t.matmul(bank[7][:, 0:D], ohw[:, half], table[:], start=True, stop=True).then_inc(f_done, 1)

        def qkv(s, half, c):
            if c == 0:
                pe.wait_ge(xt_evac, s + 1)
            if c < 2:
                wait(pe, v_evac, 2 * s - 1 + c)
            else:
                pe.wait_ge(rope_read, 4 * s + c - 1)
            for d in range(DC):
                ins = t.matmul(bank[c % 2][:], xt[:, half, d], wqkv[:, d, c * BANK:(c + 1) * BANK],
                               start=(d == 0), stop=(d == DC - 1))
            ins.then_inc(qkv_filled, 1)

        def qk_transposes(s, half, g):
            if g == 0:
                wait(pe, xt_evac, s + 2, SEQS)
                wait(pe, ot_evac, 2 * s - 1)
                pe.wait_ge(roped_done, 4 * s + 4)
            elif g == 1:
                wait(pe, ot_evac, 2 * s)
            else:
                pe.wait_ge(qkt_evac, 4 * s + g - 1)
            for j in range(4):
                src = roped[:, half, 2 * (g % 2) + g // 2, j * P:(j + 1) * P]
                ins = t.transpose(bank[2 + g % 2][:, j * P:(j + 1) * P], src, ident[:])
            ins.then_inc(qkt_filled, 1)

        def scores(s, u):
            pe.wait_ge(qkt_evac, 4 * s + 2 * u + 2)
            wait(pe, exp_done, 4 * s + 2 * u)
            for par in range(2):
                t.matmul(bank[4 + par][:], ident16[:], causal[:], start=True, stop=False, skip_group_check=True)
            for j in range(4):
                for par in range(2):
                    rows, cols = slice(64 * par, 64 * par + 64), slice(j * P, (j + 1) * P)
                    ins = t.matmul(bank[4 + par][:, j * TOK:(j + 1) * TOK], qkt[rows, 2 * u, cols],
                                   qkt[rows, 2 * u + 1, cols], start=False, stop=(j == 3), skip_group_check=True)
                    if j == 3:
                        ins.then_inc(s_done, 1)

        def p_transposes(s, g):
            pe.wait_ge(exp_done, 4 * s + g + 1)
            if g < 2:
                pe.wait_ge(qkt_evac, 4 * s + 3 + g)
            else:
                pe.wait_ge(pt_evac, 4 * s + g - 1)
            for j in range(4):
                ins = t.transpose(bank[2 + g % 2][:, j * P:(j + 1) * P], probs[:, g % 2, j], ident[:])
            ins.then_inc(pt_filled, 1)

        def values(s, half, g):
            pe.wait_ge(pt_evac, 4 * s + g + 1)
            if g % 2 == 0:
                wait(pe, on_done, 2 * s + g // 2)
            if g == 0:
                pe.wait_ge(v_evac, 2 * s + 2)
            for j in range(4):
                hd = 8 * (g // 2) + 2 * j + g % 2
                ins = t.matmul(bank[6][:, (hd % 8) * AD:(hd % 8 + 1) * AD], probs_t[:, g % 2, j],
                               vbuf[:, half, hd // 8, (hd % 8) * AD:(hd % 8 + 1) * AD],
                               start=True, stop=True, skip_group_check=True)
            ins.then_inc(av_done, 1)

        def x_transposes(s):
            pe.wait_ge(xin_ready, s + 1)
            if isinstance(s, int) and s < 2:
                wait(pe, xt_evac, s)
            wait(pe, ot_evac, 2 * (s - 2) + 1)
            for d in range(DC):
                ins = t.transpose(bank[2][:, d * P:(d + 1) * P], xin[:, d * P:(d + 1) * P], ident[:])
            ins.then_inc(xt_filled, 1)

        def o_transposes(s, u):
            pe.wait_ge(on_done, 2 * s + u + 1)
            if u == 0:
                pe.wait_ge(pt_evac, 4 * s + 3)
            else:
                pe.wait_ge(pt_evac, 4 * s + 4)
            for j in range(4):
                ins = t.transpose(bank[2 + u][:, j * P:(j + 1) * P], obuf[:, (4 * u + j) * P:(4 * u + j + 1) * P], ident[:])
            ins.then_inc(ot_filled, 1)

        def out_proj(s):
            wait(pe, ln0_read, s + 3, SEQS)
            for u in range(8):
                if u % 4 == 0:
                    pe.wait_ge(ot_evac, 2 * s + u // 4 + 1)
                ins = t.matmul(bank[7][:, D:2 * D], ot[:, u], wo[:, u], start=(u == 0), stop=(u == 7))
            ins.then_inc(wo_done, 1)

        def body(it, j, half, live):
            s1, s2, s3 = it - 1, it - 2, it - 3
            other = 1 - half
            A, Q, F = live(3), live(2), live(1)
            if A:
                qk_transposes(s3, other, 0)
                qk_transposes(s3, other, 1)
            if Q: qkv(s2, half, 0)
            if A:
                scores(s3, 0)
                qk_transposes(s3, other, 2)
                qk_transposes(s3, other, 3)
            if Q: qkv(s2, half, 1)
            if F: fused(s1, other)
            if A: p_transposes(s3, 0)
            if Q: qkv(s2, half, 2)
            if A:
                p_transposes(s3, 1)
                scores(s3, 1)
                values(s3, other, 0)
                values(s3, other, 1)
            if Q: qkv(s2, half, 3)
            if A:
                p_transposes(s3, 2)
            if Q: qkv(s2, half, 4)
            if A:
                p_transposes(s3, 3)
                values(s3, other, 2)
                values(s3, other, 3)
            if Q: qkv(s2, half, 5)
            if A:
                o_transposes(s3, 0)
                o_transposes(s3, 1)
                out_proj(s3)
            if F: x_transposes(s1)
        pipeline(pe, SEQS, 3, body)

    @block.scalar
    def _(act):
        a = nc.scalar

        def qkt_copy(s, g):
            act.wait_ge(qkt_filled, 4 * s + g + 1)
            wait(act, s_done, 4 * (s - 1) + 2 * (g // 2) + 2)
            a.activation(qkt[:, g], bank[2 + g % 2][:], ACT.Copy).then_inc(qkt_evac, 1)

        def square(s, c):
            act.wait_ge(qkv_filled, 6 * s + c + 1)
            wait(act, ssq_done, 4 * s + c - 1)
            a.activation(sq[:, c % 2], bank[c % 2][:], ACT.Square, scale=AD ** -0.5).then_inc(sq_done, 1)

        def v_copy(s, half, c):
            act.wait_ge(qkv_filled, 6 * s + 5 + c)
            wait(act, av_done, 4 * (s - 1))
            a.activation(vbuf[:, half, c], bank[c % 2][:], ACT.Copy).then_inc(v_evac, 1)

        def exps(s, half, g):
            act.wait_ge(nb_ready, 4 * s + g + 1)
            wait(act, pt_filled, 4 * s + g - 1)
            for j in range(4):
                hd = 8 * (g // 2) + 2 * j + g % 2
                ins = a.activation(probs[:, g % 2, j], bank[4 + g % 2][:, j * TOK:(j + 1) * TOK], ACT.Exp,
                                   bias=nbias[:, g % 2, j:j + 1], scale=qscale[:, half, hd:hd + 1],
                                   accum_out=psums[:, half, hd:hd + 1])
            ins.then_inc(exp_done, 1)

        def pt_copy(s, g):
            act.wait_ge(pt_filled, 4 * s + g + 1)
            wait(act, av_done, 4 * s + g - 1)
            a.activation(probs_t[:, g % 2].rearrange("p a b -> p (a b)"), bank[2 + g % 2][:], ACT.Copy).then_inc(pt_evac, 1)

        def xt_copy(s, half):
            act.wait_ge(xt_filled, s + 1)
            wait(act, qkv_filled, 6 * (s - 1))
            a.activation(xt[:, half].rearrange("p a b -> p (a b)"), bank[2][:, 0:D], ACT.Copy).then_inc(xt_evac, 1)

        def ot_copy(s, u):
            act.wait_ge(ot_filled, 2 * s + u + 1)
            wait(act, wo_done, s)
            a.activation(ot[:, 4 * u:4 * u + 4].rearrange("p a b -> p (a b)"), bank[2 + u][:], ACT.Copy).then_inc(ot_evac, 1)

        def body(it, j, half, live):
            s1, s2, s3 = it - 1, it - 2, it - 3
            other = 1 - half
            A, Q, F = live(3), live(2), live(1)
            if A:
                qkt_copy(s3, 0)
                qkt_copy(s3, 1)
            if Q: square(s2, 0)
            if A:
                qkt_copy(s3, 2)
                qkt_copy(s3, 3)
                exps(s3, other, 0)
            if Q: square(s2, 1)
            if A:
                exps(s3, other, 1)
                pt_copy(s3, 0)
            if Q: square(s2, 2)
            if A:
                pt_copy(s3, 1)
                exps(s3, other, 2)
            if Q: square(s2, 3)
            if A:
                exps(s3, other, 3)
                pt_copy(s3, 2)
                pt_copy(s3, 3)
            if Q: v_copy(s2, half, 0)
            if Q: v_copy(s2, half, 1)
            if A:
                ot_copy(s3, 0)
                ot_copy(s3, 1)
            if F: xt_copy(s1, other)
        pipeline(act, SEQS, 3, body)

    @block.vector
    def _(dve):
        v = nc.vector
        dve.wait_ge(s_w, NL)
        dve.wait_ge(s_const, 6)
        v.memset(table[:], 0.0).then_inc(s_ropetab, 1)
        dve.wait_ge(s_tab, 1)
        for c in range(DC):
            v.tensor_copy(cont_t[:, c], bank[c][:, 0:VOCAB]).then_inc(s_tab, 1)
        v.tensor_copy(proj_bv[:], bcast(proj_b[:], VOCAB, 2)).then_inc(s_tab, 1)
        v.tensor_copy(causal[:].rearrange("p (a b) -> p a b", a=4), bcast(causal_f[:], 4, 1)).then_inc(s_ropetab, 1)
        v.tensor_copy(ident16[:], ident[:]).then_inc(s_ropetab, 1)
        for i in range(2):
            v.tensor_tensor(rope_c[:, i], rope_cs[:, 0], norm_w[:, i], ALU.mult)
            for u in range(2):
                ins = v.tensor_tensor(rope_s[:, i, 32 * u:32 * u + 32], rope_cs[:, 1, 32 * u:32 * u + 32],
                                      norm_w[:, i, 32 - 32 * u:64 - 32 * u], ALU.mult)
        ins.then_inc(s_ropetab, 1)
        dve.wait_ge(s_tab, 6)
        dve.wait_ge(s_ropetab, 4)
        v.tensor_copy(table[0:VOCAB], bank[2][0:VOCAB, 0:D]).then_inc(s_tab, 1)
        v.tensor_copy(table[32:32 + VOCAB], bank[3][32:32 + VOCAB, 0:D]).then_inc(s_tab, 1)
        dve.wait_ge(s_ropetab, 4)

        chain = shared["dve_chain"]
        lenl = Links(dve, chain[0], 1, SEQS)
        lnl = Links(dve, chain[1], 5, SEQS)
        ropel = Links(dve, chain[2], 4, SEQS)
        nbl = Links(dve, chain[3], 4, SEQS)
        onl = Links(dve, chain[4], 2, SEQS)

        def hot_prep(s, half, j):
            dve.wait_ge(s_idm[half], 16 * j + 16)
            wait(dve, hot_ready, s)
            v.tensor_scalar(hot[:], idm[:, half, 0], vocab_id[:], None, ALU.is_equal)
            v.tensor_copy(mpad[:, 1:TOK + 1], idm[:, half, 1]).then_inc(hot_pre, 1)

        def len_clip(s):
            dve.wait_ge(hot_link, 4 * s + 3)
            lenl.at(s)(v.tensor_scalar(mlen[:], msum[:], 1.0, None, ALU.max))
            v.reciprocal(minv[:], mlen[:]).then_inc(len_clipped, 1)

        def ln_stats(s):
            dve.wait_ge(f_done, s + 1)
            lnl.at(s)(v.bn_stats(st6[:, 0], bank[7][:, 0:D]))
            v.memset(carrier[:], 0.0)
            v.bn_aggr(mv0[:], st6[:, 0]).then_inc(ln_stat, 1)

        def ln_apply(s):
            dve.wait_ge(pool_link, 4 * s + 2)
            ins = v.tensor_scalar(hx[:, 0], bank[7][:, 0:D], mv0[:, 0:1], rstd[:, 0:1], ALU.subtract, ALU.mult)
            ins.then_inc(ln0_read, 1)
            dve.wait_ge(ln0_read, s + 1)
            wait(dve, xin_ready, s)
            lnl(v.tensor_tensor(hx[:, 0], hx[:, 0], gain[:], ALU.mult))
            lnl(v.tensor_tensor(hx[:, 1], hx[:, 0], shift[:], ALU.add))
            lnl(v.bn_stats(st6[:, 1], hx[:, 1]))
            v.memset(carrier[:], 0.0)
            v.bn_aggr(mv1[:], st6[:, 1]).then_inc(ln_stat, 1)
            lnl(v.tensor_copy(h[:, bass.ds(s * D, D)], hx[:, 1]))

        def ln_xin(s):
            dve.wait_ge(pool_link, 4 * s + 4)
            wait(dve, xt_filled, s)
            v.tensor_scalar(xin[:], hx[:, 1], mv1[:, 0:1], rstd[:, 1:2], ALU.subtract, ALU.mult).then_inc(xin_ready, 1)

        def rope(s, half, c):
            i = c // 2
            dve.wait_ge(sq_done, 4 * s + c + 1)
            if c == 0:
                ropel.at(s)
                wait(dve, qkt_filled, 4 * (s - 1))
            wait(dve, roped_done, 4 * s + c)
            v.tensor_reduce(ssq[:, c], sq[:, c % 2].rearrange("p (a b) -> p a b", b=AD), AX_X, ALU.add).then_inc(ssq_done, 1)
            x = bank[c % 2][:].rearrange("p (a b) -> p a b", b=AD)
            xs = bank[c % 2][:].rearrange("p (a u b) -> p a u b", u=2, b=32)
            y1 = t1[:].rearrange("p (a b) -> p a b", b=AD)
            y2 = t2[:].rearrange("p (a u b) -> p a u b", u=2, b=32)
            v.tensor_tensor(y1, x, bcast(rope_c[:, i], 8, 1), ALU.mult)
            for u in range(2):
                ins = v.tensor_tensor(y2[:, :, u], xs[:, :, 1 - u],
                                      bcast(rope_s[:, i, 32 * u:32 * u + 32], 8, 1), ALU.mult)
            ins.then_inc(rope_read, 1)
            dve.wait_ge(rope_read, 4 * s + c + 1)
            out = roped[:, half, c]
            if i == 0:
                v.tensor_tensor(out, t1[:], t2[:], ALU.add).then_inc(roped_done, 1)
            else:
                ropel(v.tensor_tensor(t1[:], t1[:], t2[:], ALU.add))
                dve.wait_ge(rs_ready, 4 * s + c + 1)
                v.tensor_tensor(out.rearrange("p (a b) -> p a b", b=AD), y1, bcast(rsh[:, c], AD, 2), ALU.mult).then_inc(roped_done, 1)
            if c == 3:
                for cc in range(2):
                    ropel(v.tensor_scalar(qscale[:, half, 8 * cc:8 * cc + 8], rsh[:, cc], AD ** -0.5, None, ALU.mult))

        def row_max(s, half, g):
            dve.wait_ge(s_done, 4 * s + g + 1)
            if g == 0:
                nbl.at(s)
            wait(dve, nb_ready, 4 * s + g)
            nbl(v.tensor_reduce(smax[:], bank[4 + g % 2][:].rearrange("p (a b) -> p a b", b=TOK), AX_X, ALU.max))
            wait(dve, exp_done, 4 * s + g - 1)
            v.scalar_tensor_tensor(nbias[:, g % 2], smax[:], -1.0, qscale[:, half, 8 * (g // 2) + g % 2:8 * (g // 2) + 8:2], ALU.mult, ALU.mult).then_inc(nb_ready, 1)

        def o_norm(s, half, u):
            if u == 0:
                onl.at(s)
            dve.wait_ge(av_done, 4 * s + 2 * u + 2)
            wait(dve, on_done, 2 * s + u)
            onl(v.reciprocal(pinv[:], psums[:, half, 8 * u:8 * u + 8]))
            wait(dve, ot_filled, 2 * s + u - 1)
            v.tensor_tensor(obuf[:, u * BANK:(u + 1) * BANK].rearrange("p (a b) -> p a b", b=AD),
                            bank[6][:].rearrange("p (a b) -> p a b", b=AD), bcast(pinv[:], AD, 2), ALU.mult).then_inc(on_done, 1)

        def residual(s):
            dve.wait_ge(wo_done, s + 1)
            hs = h[:, bass.ds(s * D, D)]
            v.tensor_tensor(hs, hs, bank[7][:, D:2 * D], ALU.add).then_inc(stored, 1)

        def body(it, j, half, live):
            s1, s2, s3 = it - 1, it - 2, it - 3
            other = 1 - half
            A, Q, F = live(3), live(2), live(1)
            if live(0): hot_prep(it, half, j)
            if A: row_max(s3, other, 0)
            if A: row_max(s3, other, 1)
            if Q: rope(s2, half, 0)
            if Q: rope(s2, half, 1)
            if live(0): len_clip(it)
            if F: ln_stats(s1)
            if A: row_max(s3, other, 2)
            if A: row_max(s3, other, 3)
            if Q: rope(s2, half, 2)
            if A: o_norm(s3, other, 0)
            if Q: rope(s2, half, 3)
            if A: o_norm(s3, other, 1)
            if F: ln_apply(s1)
            if F: ln_xin(s1)
            if A: residual(s3)
        pipeline(dve, SEQS, 3, body)

    return stored, SEQS


G4 = 4
GROUPS = SEQS // G4
GT = G4 * TOK
EXPERTS = 8
FF = 256
FC = FF // P
LH, LD = 4, 64
LSCALE = LD ** -0.5
TOP = 2
REGION = SEQS * TOK + P
TILES = SEQS * TOK * TOP // P + EXPERTS
SORTED_ROWS = (EXPERTS + 1) * REGION
ROUND_INT = 12582912.0


def experts(ctx, block, shared, local, a_done):
    nc, dram, h, ident, bank = (shared[k] for k in ("nc", "dram", "h", "ident", "bank"))
    eps5, eps6, neghalf = (shared[k] for k in ("eps5", "eps6", "neghalf"))
    pos_all, tw_all, sorted_y = (shared[k] for k in ("pos_all", "tw_all", "sorted_y"))
    sorted_x = nc.dram_tensor("sorted_x", (SORTED_ROWS, D), F32, kind="Internal").ap()

    def sb(name, shape, dt=F32):
        return local.enter_context(nc.sbuf_tensor("b_" + name, shape, dt))

    def sem(name):
        return ctx.enter_context(nc.semaphore("b_" + name))

    sw1, sw3 = sb("sw1", [P, DC, FF]), sb("sw3", [P, DC, FF])
    sw2 = sb("sw2", [P, FC, D])
    w13 = sb("w13", [P, DC, EXPERTS * 2 * FF])
    w2 = sb("w2", [P, FC, EXPERTS * D])
    wq = sb("wq", [P, DC, D])
    wk = sb("wk", [P, DC, 2 * LD])
    wv = sb("wv", [P, DC, LD])
    wo = sb("wo", [P, DC, D])
    wr = sb("wr", [P, DC, EXPERTS])
    g1, g2 = sb("g1", [P, DC]), sb("g2", [P, DC])
    rbias = sb("rbias", [P, EXPERTS])
    iota8 = sb("iota8", [P, EXPERTS])
    iota_p = sb("iota_p", [P, 1])
    iota_tiles = sb("iota_tiles", [1, TILES])
    before = sb("before", [P, P])
    onesv = sb("onesv", [P, P])
    zeros = sb("zeros", [P, D])
    carrier = sb("carrier", [P, 1])
    dummy = sb("dummy", [P, 1])
    st_f, mv1, mvf = sb("st_f", [P, 2, G4, 6]), sb("mv1", [P, G4, 2]), sb("mvf", [P, G4, 2])
    ms_f, rtmp, rs_f = sb("ms_f", [P, G4]), sb("rtmp", [P, G4]), sb("rs_f", [P, 2, G4])
    mv_all, rs_all = sb("mv_all", [P, SEQS * 2]), sb("rs_all", [P, SEQS])
    x = sb("x", [P, G4 * D])
    nx = sb("nx", [P, G4 * D])
    nxt = sb("nxt", [P, DC, GT])
    qt = sb("qt", [P, DC, GT])
    kt = sb("kt", [P, GT])
    vb = sb("vb", [P, 2, G4 * LD])
    smax, nbias = sb("smax", [P, 4]), sb("nbias", [P, 4, 4])
    probs = sb("probs", [P, 4, LH * TOK])
    pt = sb("pt", [P, G4, LH * TOK])
    psums = sb("psums", [P, G4, LH])
    pinv = sb("pinv", [P, 2 * LH])
    ob = sb("ob", [P, G4 * D])
    otb = sb("otb", [P, DC, GT])
    mvo, rso = sb("mvo", [P, G4 * 2]), sb("rso", [P, G4])
    st_o, mv_o = sb("st_o", [P, G4, 6]), sb("mv_o", [P, G4, 2])
    ms_o, rtmp_o, rs_o = sb("ms_o", [P, G4]), sb("rtmp_o", [P, G4]), sb("rs_o", [P, G4])
    x2 = sb("x2", [P, G4 * D])
    nx2 = sb("nx2", [P, 2, G4 * D])
    xft = sb("xft", [P, DC, GT])
    lg, ex, rw = (sb(n, [P, G4, EXPERTS]) for n in ("lg", "ex", "rw"))
    r4a, r4b = sb("r4a", [P, G4]), sb("r4b", [P, G4])
    top = sb("top", [P, G4, 8])
    topi = sb("topi", [P, G4, 8], U32)
    topf = sb("topf", [P, G4, 8])
    diff, ediff = sb("diff", [P, G4]), sb("ediff", [P, G4])
    tw = sb("tw", [P, TOP, G4])
    chosen = sb("chosen", [P, TOP, G4, EXPERTS])
    both = sb("both", [P, G4 + 1, EXPERTS])
    cnt = sb("cnt", [P, EXPERTS])
    slot = sb("slot", [P, G4, EXPERTS])
    picked = sb("picked", [P, TOP, G4, EXPERTS])
    posf = sb("posf", [P, TOP * G4])
    posf_all, ids_all = sb("posf_all", [P, SEQS * TOP]), sb("ids_all", [P, SEQS * TOP])
    shift, moved = sb("shift", [P, EXPERTS]), sb("moved", [P, SEQS * TOP])
    posg = sb("posg", [P, 2, TOP * G4], U32)
    th, up = sb("th", [P, GT]), sb("up", [P, GT])
    hid = sb("hid", [P, FC, GT])
    padf, pad = sb("padf", [P, EXPERTS]), sb("pad", [P, EXPERTS], U32)
    ntile, tiles_end, step = sb("ntile", [P, EXPERTS]), sb("tiles_end", [P, EXPERTS]), sb("step", [P, EXPERTS])
    tile_f = sb("tile_f", [1, 2, TILES])
    tile_i = sb("tile_i", [1, 2, TILES], I32)

    s_w, s_w2, s_const = sem("weights"), sem("weights2"), sem("const")
    stat_f, rsf_ready = sem("stat_f"), sem("rs_f")
    stat_o, rso_ready = sem("stat_o"), sem("rs_o")
    nx_ready, t_filled, t_evac = sem("nx"), sem("t_filled"), sem("t_evac")
    q_filled, q_evac = sem("q_filled"), sem("q_evac")
    s_done, nb_ready, exp_done = sem("scores"), sem("nbias"), sem("exp")
    pt_filled, pt_evac, av_done, on_done = sem("pt_filled"), sem("pt_evac"), sem("av"), sem("on")
    ot_filled, ot_evac, wo_done, x2_done = sem("ot_filled"), sem("ot_evac"), sem("wo"), sem("x2")
    nx2_ready, t2_filled, t2_evac = sem("nx2"), sem("t2_filled"), sem("t2_evac")
    r_done, r_shift, r_exp, r_diff, r_ediff = (sem(n) for n in (
        "r_logits", "r_shift", "r_exp", "r_diff", "r_ediff"))
    chosen_ready, cnt_filled, pos_done = sem("chosen"), sem("counts"), sem("positions")
    scattered = [sem(f"scattered{i}") for i in range(2)]
    w13_done, tanh_done, up_done, hid_done, w2_half, acc_done = (sem(n) for n in (
        "w13", "tanh", "up", "hid", "w2_half", "acc"))
    carried = shared["carried"]
    pad_ready, padded, plan_ready = sem("pad"), sem("padded"), sem("plan")

    LOADS = [
        (wq[:], dram["l_wq"]), (wk[:, :, 0:LD], dram["l_wk"]), (wk[:, :, LD:2 * LD], dram["l_wk"]), (wv[:], dram["l_wv"]),
        (wo[:], dram["l_wo"]), (wr[:], dram["l_wr"]), (g1[:], dram["l_g1"]), (g2[:], dram["l_g2"]),
        (rbias[:], dram["l_rbias"].partition_broadcast(P)), (iota8[:], dram["iota8"].partition_broadcast(P)),
        (sw1[:], dram["l_sw1"]), (sw3[:], dram["l_sw3"]), (sw2[:], dram["l_sw2"]),
        (iota_p[:], dram["iota_p"]), (iota_tiles[:], dram["iota_tiles"]), (before[:], dram["before"]),
    ]
    NL = 16 * len(LOADS)

    @block.sync
    def _(sp):
        sp.wait_ge(*a_done)
        for dst, src in LOADS:
            sp.dma_start(dst, src).then_inc(s_w, 16)
        sp.dma_start(w13[:], dram["l_ew13"]).then_inc(s_w2, 16)
        sp.dma_start(w2[:], dram["l_ew2"]).then_inc(s_w2, 16)
        sp.wait_ge(s_const, 5)
        for i in range(EXPERTS):
            rows = EXPERTS * REGION + i * P
            sp.dma_start(sorted_x[rows:rows + P], zeros[:]).then_inc(s_w2, 16)

    @block.gpsimd
    def _(pool):
        g = nc.gpsimd
        pool.wait_ge(*a_done)
        for t, val in ((onesv, 1.0), (both, 0.0), (zeros, 0.0), (pos_all, 0), (dummy, 0.0)):
            g.memset(t[:], val).then_inc(s_const, 1)
        pool.wait_ge(s_const, 5)
        chain = shared["pool_chain"]
        lf, lo = Links(pool, chain[0], 2, GROUPS), Links(pool, chain[1], 1, GROUPS)

        def rsqrt(link, ready, n, tmp, src, dst, eps, stat):
            pool.wait_ge(stat, n + 1)
            wait(pool, ready, n)
            link(g.tensor_tensor(out=tmp[:], in0=src, in1=eps[:, 0:G4], op=ALU.add))
            g.tensor_tensor(out=dst, in0=tmp[:], in1=neghalf[:, 0:G4], op=ALU.pow).then_inc(ready, 1)

        def scatter(s, o):
            pool.wait_ge(pos_done, s + 1)
            wait(pool, carried, s)
            g.tensor_tensor(out=dummy[:], in0=eps5[:, 0:1], in1=eps6[:, 0:1], op=ALU.add).then_inc(carried, 1)
            for k in range(TOP):
                for q in range(G4):
                    g.indirect_dma_start(sorted_x, bass.IndirectOffsetOnAxis(posg[:, o, k * G4 + q:k * G4 + q + 1], 0),
                                         nx2[:, o, q * D:(q + 1) * D], None).then_inc(scattered[o], 16)

        def body(it, j, half, live):
            if live(0):
                lf.at(it)
                rsqrt(lf, rsf_ready, 2 * it, rtmp, mv1[:, :, 1], rs_f[:, 0], eps5, stat_f)
            if live(4):
                scatter(it - 4, half)
            if live(2):
                rsqrt(lo.at(it - 2), rso_ready, it - 2, rtmp_o, ms_o[:], rs_o[:], eps6, stat_o)
            if live(0):
                rsqrt(lf, rsf_ready, 2 * it + 1, rtmp, ms_f[:], rs_f[:, 1], eps6, stat_f)
        pipeline(pool, GROUPS, 4, body, peel=6)
        pool.wait_ge(pad_ready, 1)
        for e in range(EXPERTS):
            g.indirect_dma_start(sorted_x, bass.IndirectOffsetOnAxis(pad[:, e:e + 1], 0), zeros[:], None).then_inc(padded, 16)

    @block.tensor
    def _(pe):
        t = nc.tensor
        pe.wait_ge(*a_done)
        pe.wait_ge(s_w, NL)
        pe.wait_ge(s_const, 5)

        def transposes(src, b, dst_bank):
            for q in range(G4):
                ins = t.transpose(dst_bank[:, q * TOK:(q + 1) * TOK], src[:, q * D + b * P:q * D + (b + 1) * P], ident[:])
            return ins

        def t1(g):
            pe.wait_ge(nx_ready, g + 1)
            wait(pe, q_evac, 4 * g)
            wait(pe, x2_done, g - 1)
            for b in range(2):
                transposes(nx, b, bank[b]).then_inc(t_filled, 1)

        def q_proj(g):
            pe.wait_ge(t_evac, 2 * g + 2)
            for c in range(DC):
                for d in range(DC):
                    ins = t.matmul(bank[c][:], wq[:, d, c * P:(c + 1) * P], nxt[:, d], start=(d == 0), stop=(d == DC - 1))
                ins.then_inc(q_filled, 1)

        def kv_proj(g):
            pe.wait_ge(q_evac, 4 * g + 1)
            for d in range(DC):
                ins = t.matmul(bank[0][:], wk[:, d], nxt[:, d], start=(d == 0), stop=(d == DC - 1))
            ins.then_inc(q_filled, 1)
            pe.wait_ge(q_evac, 4 * g + 2)
            for q in range(G4):
                for d in range(DC):
                    ins = t.matmul(bank[1][:, q * LD:(q + 1) * LD], nxt[:, d, q * TOK:(q + 1) * TOK], wv[:, d],
                                   start=(d == 0), stop=(d == DC - 1), skip_group_check=True)
            ins.then_inc(q_filled, 1)

        def scores(g, u):
            if u == 0:
                pe.wait_ge(q_evac, 4 * g + 4)
                wait(pe, on_done, 2 * g)
            else:
                wait(pe, pt_evac, 4 * g)
                wait(pe, pos_done, g - 2)
            for q in range(2):
                for c in range(DC):
                    for par in range(2):
                        rows, seq = slice(64 * par, 64 * par + 64), 2 * u + q
                        cols = slice(seq * TOK, (seq + 1) * TOK)
                        ins = t.matmul(bank[2 + 2 * u + par][:, (2 * q + c) * TOK:(2 * q + c + 1) * TOK], qt[rows, c, cols],
                                       kt[rows, cols], start=True, stop=True, skip_group_check=True)
                        if q == 1 and c == 1:
                            ins.then_inc(s_done, 1)

        def p_transposes(g, u):
            pe.wait_ge(exp_done, 4 * g + 2 * u + 2)
            for q in range(2):
                for hd in range(LH):
                    col = (2 * q + hd // 2) * TOK
                    ins = t.transpose(bank[2 + 2 * u + q][:, hd * TOK:(hd + 1) * TOK], probs[:, 2 * u + hd % 2, col:col + TOK], ident[:])
                ins.then_inc(pt_filled, 1)

        def values(g, o):
            pe.wait_ge(pt_evac, 4 * g + 4)
            for u in range(2):
                for q in range(2):
                    for hd in range(LH):
                        seq = 2 * u + q
                        ins = t.matmul(bank[2 + u][:, q * D + hd * LD:q * D + (hd + 1) * LD], pt[:, seq, hd * TOK:(hd + 1) * TOK],
                                       vb[:, o, seq * LD:(seq + 1) * LD], start=True, stop=True, skip_group_check=True)
                ins.then_inc(av_done, 1)

        def o_transposes(g):
            pe.wait_ge(on_done, 2 * g + 2)
            wait(pe, q_evac, 4 * g + 8, 4 * GROUPS)
            for b in range(2):
                transposes(ob, b, bank[b]).then_inc(ot_filled, 1)

        def out_proj(g):
            pe.wait_ge(ot_evac, 2 * g + 2)
            for q in range(G4):
                for c in range(DC):
                    ins = t.matmul(bank[q // 2][:, (q % 2) * D:(q % 2 + 1) * D], otb[:, c, q * TOK:(q + 1) * TOK], wo[:, c],
                                   start=(c == 0), stop=(c == DC - 1), skip_group_check=True)
            ins.then_inc(wo_done, 1)

        def t2(g, o):
            pe.wait_ge(nx2_ready, g + 1)
            wait(pe, acc_done, G4 * g)
            for b in range(2):
                transposes(nx2[:, o], b, bank[6 + b]).then_inc(t2_filled, 1)

        def logits(g):
            pe.wait_ge(t2_evac, 2 * g + 2)
            for q in range(G4):
                for d in range(DC):
                    ins = t.matmul(bank[6][:, q * EXPERTS:(q + 1) * EXPERTS], xft[:, d, q * TOK:(q + 1) * TOK], wr[:, d],
                                   start=(d == 0), stop=(d == DC - 1), skip_group_check=True)
            ins.then_inc(r_done, 1)

        def up_gate(g, n):
            if n == 0:
                pe.wait_ge(r_shift, g + 1)
            else:
                pe.wait_ge(hid_done, 2 * g + 1)
            cols = slice(n * P, (n + 1) * P)
            for i, w in enumerate((sw1, sw3)):
                for d in range(DC):
                    ins = t.matmul(bank[6 + i][:], w[:, d, cols], xft[:, d], start=(d == 0), stop=(d == DC - 1))
            ins.then_inc(w13_done, 1)

        def down(g):
            pe.wait_ge(hid_done, 2 * g + 2)
            for q in range(G4):
                for c in range(FC):
                    ins = t.matmul(bank[6 + q // 2][:, (q % 2) * D:(q % 2 + 1) * D], hid[:, c, q * TOK:(q + 1) * TOK],
                                   sw2[:, c], start=(c == 0), stop=(c == FC - 1), skip_group_check=True)
                if q % 2:
                    ins.then_inc(w2_half, 1)

        def counts(g):
            pe.wait_ge(chosen_ready, 2 * g + 2)
            wait(pe, pt_evac, 4 * g + 12, 4 * GROUPS)
            n = G4 + 1
            t.matmul(bank[4][:, 0:n * EXPERTS], before[:], both[:].rearrange("p a b -> p (a b)"), start=True, stop=False,
                     skip_group_check=True)
            for q in range(G4):
                ins = t.matmul(bank[4][:, (q + 1) * EXPERTS:n * EXPERTS].rearrange("p (a b) -> p a b", b=EXPERTS), onesv[:],
                               bcast(both[:, q], G4 - q, 1), start=False, stop=(q == G4 - 1), skip_group_check=True)
            ins.then_inc(cnt_filled, 1)

        def body(it, j, half, live):
            g, g1_, g2_, g3_, o = it, it - 1, it - 2, it - 3, 1 - half
            if live(3): t2(g3_, o)
            if live(2): o_transposes(g2_)
            if live(1):
                scores(g1_, 0)
                scores(g1_, 1)
            if live(3): logits(g3_)
            if live(2): out_proj(g2_)
            if live(3): up_gate(g3_, 0)
            if live(1):
                p_transposes(g1_, 0)
                p_transposes(g1_, 1)
            if live(3): up_gate(g3_, 1)
            if live(1): values(g1_, o)
            if live(3): down(g3_)
            if live(0):
                t1(g)
                q_proj(g)
                kv_proj(g)
            if live(3): counts(g3_)
        pipeline(pe, GROUPS, 3, body)

    @block.scalar
    def _(act):
        a = nc.scalar
        act.wait_ge(*a_done)
        act.wait_ge(s_w, NL)

        def t_copy(g):
            for b in range(2):
                act.wait_ge(t_filled, 2 * g + b + 1)
                wait(act, q_filled, 4 * g)
                a.activation(nxt[:, b], bank[b][:], ACT.Copy, scale=g1[:, b:b + 1]).then_inc(t_evac, 1)

        def t2_copy(g):
            for b in range(2):
                act.wait_ge(t2_filled, 2 * g + b + 1)
                wait(act, w13_done, 2 * g)
                a.activation(xft[:, b], bank[6 + b][:], ACT.Copy, scale=g2[:, b:b + 1]).then_inc(t2_evac, 1)

        def q_copy(g):
            for c in range(2):
                act.wait_ge(q_filled, 4 * g + c + 1)
                wait(act, s_done, 4 * g)
                a.activation(qt[:, c], bank[c][:], ACT.Copy).then_inc(q_evac, 1)

        def kv_copy(g, half):
            act.wait_ge(q_filled, 4 * g + 3)
            a.activation(kt[:], bank[0][:], ACT.Copy).then_inc(q_evac, 1)
            act.wait_ge(q_filled, 4 * g + 4)
            wait(act, av_done, 2 * (g - 1))
            a.activation(vb[:, half], bank[1][:, 0:G4 * LD], ACT.Copy).then_inc(q_evac, 1)

        def exps(g, u):
            for par in range(2):
                act.wait_ge(nb_ready, 4 * g + 2 * u + par + 1)
                wait(act, pt_filled, 4 * (g - 1) + 2 * u + 2)
                if u == 0 and par == 0:
                    wait(act, on_done, 2 * g)
                for i in range(4):
                    ins = a.activation(probs[:, 2 * u + par, i * TOK:(i + 1) * TOK], bank[2 + 2 * u + par][:, i * TOK:(i + 1) * TOK], ACT.Exp,
                                       bias=nbias[:, 2 * u + par, i:i + 1], scale=LSCALE,
                                       accum_out=psums[:, 2 * u + i // 2, 2 * (i % 2) + par:2 * (i % 2) + par + 1])
                ins.then_inc(exp_done, 1)

        def pt_copy(g, u):
            for q in range(2):
                act.wait_ge(pt_filled, 4 * g + 2 * u + q + 1)
                wait(act, av_done, 2 * g)
                a.activation(pt[:, 2 * u + q], bank[2 + 2 * u + q][:], ACT.Copy).then_inc(pt_evac, 1)

        def ot_copy(g):
            for b in range(2):
                act.wait_ge(ot_filled, 2 * g + b + 1)
                wait(act, wo_done, g)
                a.activation(otb[:, b], bank[b][:], ACT.Copy).then_inc(ot_evac, 1)

        def gate_tanh(g, n):
            act.wait_ge(w13_done, 2 * g + n + 1)
            wait(act, up_done, 2 * g + n)
            a.activation(th[:], bank[6][:], ACT.Tanh, scale=0.5).then_inc(tanh_done, 1)

        def route_exp(g):
            act.wait_ge(r_shift, g + 1)
            wait(act, r_diff, g)
            a.activation(ex[:], lg[:], ACT.Exp).then_inc(r_exp, 1)

        def route_ediff(g):
            act.wait_ge(r_diff, g + 1)
            a.activation(ediff[:], diff[:], ACT.Exp).then_inc(r_ediff, 1)

        def body(it, j, half, live):
            g, g1_, g2_, g3_, o = it, it - 1, it - 2, it - 3, 1 - half
            if live(3): t2_copy(g3_)
            if live(2): ot_copy(g2_)
            if live(1): exps(g1_, 0)
            if live(3): route_exp(g3_)
            if live(1): exps(g1_, 1)
            if live(3): gate_tanh(g3_, 0)
            if live(1):
                pt_copy(g1_, 0)
                pt_copy(g1_, 1)
            if live(3):
                gate_tanh(g3_, 1)
                route_ediff(g3_)
            if live(0):
                t_copy(g)
                q_copy(g)
                kv_copy(g, half)
        pipeline(act, GROUPS, 3, body)

    @block.vector
    def _(dve):
        v = nc.vector
        dve.wait_ge(*a_done)
        dve.wait_ge(s_w, NL)
        dve.wait_ge(s_const, 5)
        v.tensor_scalar(cnt[:], iota8[:], float(REGION), None, ALU.mult).then_inc(s_const, 1)
        dve.wait_ge(s_const, 6)
        chain = shared["dve_chain"]
        lf, lo = Links(dve, chain[0], 6, GROUPS), Links(dve, chain[1], 6, GROUPS)
        nbl, onl = Links(dve, chain[2], 4, GROUPS), Links(dve, chain[3], 2, GROUPS)
        rl, pl = Links(dve, chain[4], 10, GROUPS), Links(dve, chain[5], 4, GROUPS)

        def tile_of(g, q):
            return h[:, bass.ds((G4 * g + q) * D, D)]

        def stats(link, src, st, mv):
            for q in range(G4):
                ins = v.bn_stats(st[:, q], src(q))
            link(ins)
            v.memset(carrier[:], 0.0)
            for q in range(G4):
                ins = v.bn_aggr(mv[:, q], st[:, q])
            return ins

        def mean_square(link, ms, mv, stat):
            link(v.tensor_tensor(ms[:], mv[:, :, 0], mv[:, :, 0], ALU.mult))
            v.tensor_tensor(ms[:], ms[:], mv[:, :, 1], ALU.add).then_inc(stat, 1)

        def ln_stats(g):
            lf.at(g)
            wait(dve, nx_ready, g)
            lf(v.memset(carrier[:], 0.0))
            v.memset(carrier[:], 0.0)
            stats(lf, lambda q: tile_of(g, q), st_f[:, 0], mv1).then_inc(stat_f, 1)

        def ln_apply(g):
            dve.wait_ge(rsf_ready, 2 * g + 1)
            v.memset(carrier[:], 0.0)
            v.tensor_copy(mv_all[:, bass.ds(g * 2 * G4, 2 * G4)], mv1[:].rearrange("p a b -> p (a b)"))
            v.tensor_copy(rs_all[:, bass.ds(g * G4, G4)], rs_f[:, 0])
            for q in range(G4):
                ins = v.tensor_scalar(x[:, q * D:(q + 1) * D], tile_of(g, q), mv1[:, q, 0:1], rs_f[:, 0, q:q + 1], ALU.subtract, ALU.mult)
            lf(ins)
            lf(stats(lf, lambda q: x[:, q * D:(q + 1) * D], st_f[:, 1], mvf))
            mean_square(lf, ms_f, mvf, stat_f)

        def scale_rows(g):
            dve.wait_ge(rsf_ready, 2 * g + 2)
            wait(dve, t_filled, 2 * g)
            for q in range(G4):
                ins = v.tensor_scalar(nx[:, q * D:(q + 1) * D], x[:, q * D:(q + 1) * D], rs_f[:, 1, q:q + 1], None, ALU.mult)
            ins.then_inc(nx_ready, 1)

        def row_max(g, u):
            for par in range(2):
                if u == 0 and par == 0:
                    nbl.at(g)
                dve.wait_ge(s_done, 4 * g + 2 * u + par + 1)
                wait(dve, nb_ready, 4 * g + 2 * u + par)
                nbl(v.tensor_reduce(smax[:], bank[2 + 2 * u + par][:].rearrange("p (a b) -> p a b", b=TOK), AX_X, ALU.max))
                wait(dve, exp_done, 4 * (g - 1) + 2 * u + par + 1)
                v.tensor_scalar(nbias[:, 2 * u + par], smax[:], -LSCALE, None, ALU.mult).then_inc(nb_ready, 1)

        def o_norm(g):
            for u in range(2):
                if u == 0:
                    onl.at(g)
                dve.wait_ge(av_done, 2 * g + u + 1)
                wait(dve, on_done, 2 * g + u)
                onl(v.reciprocal(pinv[:], psums[:, 2 * u:2 * u + 2].rearrange("p a b -> p (a b)")))
                wait(dve, ot_filled, 2 * g)
                v.tensor_tensor(ob[:, u * 2 * D:(u + 1) * 2 * D].rearrange("p (a b) -> p a b", b=LD),
                                bank[2 + u][:].rearrange("p (a b) -> p a b", b=LD), bcast(pinv[:], LD, 2), ALU.mult).then_inc(on_done, 1)

        def residual(g):
            lo.at(g)
            wait(dve, nx2_ready, g)
            v.memset(carrier[:], 0.0)
            v.tensor_copy(mvo[:], mv_all[:, bass.ds(g * 2 * G4, 2 * G4)])
            lo(v.tensor_copy(rso[:], rs_all[:, bass.ds(g * G4, G4)]))
            for q in range(G4):
                ins = v.tensor_scalar(x2[:, q * D:(q + 1) * D], tile_of(g, q), mvo[:, 2 * q:2 * q + 1], rso[:, q:q + 1], ALU.subtract, ALU.mult)
            lo(ins)
            dve.wait_ge(wo_done, g + 1)
            for u in range(2):
                xs = x2[:, u * 2 * D:(u + 1) * 2 * D]
                ins = v.tensor_tensor(xs, xs, bank[u][:], ALU.add)
            ins.then_inc(x2_done, 1)

        def residual_stats(g):
            dve.wait_ge(x2_done, g + 1)
            lo(stats(lo, lambda q: x2[:, q * D:(q + 1) * D], st_o, mv_o))
            mean_square(lo, ms_o, mv_o, stat_o)
            hs = h[:, bass.ds(g * G4 * D, G4 * D)]
            lo(v.tensor_tensor(hs, hs, x2[:], ALU.add))

        def scale_rows2(g, j, half):
            dve.wait_ge(rso_ready, g + 1)
            wait(dve, t2_filled, 2 * g - 2)
            wait(dve, scattered[half], 16 * TOP * G4 * j)
            for q in range(G4):
                ins = v.tensor_scalar(nx2[:, half, q * D:(q + 1) * D], x2[:, q * D:(q + 1) * D], rs_o[:, q:q + 1], None, ALU.mult)
            ins.then_inc(nx2_ready, 1)

        def route_shift(m):
            dve.wait_ge(r_done, m + 1)
            rl.at(m)
            rl(v.tensor_tensor(lg[:], bank[6][:, 0:G4 * EXPERTS].rearrange("p (a b) -> p a b", b=EXPERTS), bcast(rbias[:], G4, 1), ALU.add))
            rl(v.tensor_reduce(r4a[:], lg[:], AX_X, ALU.max))
            v.tensor_tensor(lg[:], lg[:], bcast(r4a[:], EXPERTS, 2), ALU.subtract).then_inc(r_shift, 1)

        def route_top(m):
            dve.wait_ge(r_exp, m + 1)
            rl(v.tensor_reduce(r4a[:], ex[:], AX_X, ALU.add))
            rl(v.reciprocal(r4b[:], r4a[:]))
            rl(v.tensor_tensor(rw[:], ex[:], bcast(r4b[:], EXPERTS, 2), ALU.mult))
            v.memset(carrier[:], 0.0)
            for q in range(G4):
                ins = v.max(top[:, q], rw[:, q])
            rl(ins)
            v.memset(carrier[:], 0.0)
            for q in range(G4):
                ins = v.max_index(topi[:, q], top[:, q], rw[:, q])
            rl(ins)
            v.tensor_tensor(diff[:], top[:, :, 1], top[:, :, 0], ALU.subtract).then_inc(r_diff, 1)

        def route_weights(m):
            dve.wait_ge(r_ediff, m + 1)
            v.tensor_copy(topf[:], topi[:])
            rl(v.tensor_scalar(r4a[:], ediff[:], 1.0, None, ALU.add))
            rl(v.reciprocal(r4b[:], r4a[:]))
            rl(v.tensor_scalar(tw[:, 0], r4b[:], 0.5, None, ALU.mult))
            v.tensor_tensor(tw[:, 1], tw[:, 0], ediff[:], ALU.mult)
            for k in range(TOP):
                ins = v.tensor_tensor(chosen[:, k], bcast(iota8[:], G4, 1), bcast(topf[:, :, k], EXPERTS, 2), ALU.is_equal)
            ins.then_inc(chosen_ready, 1)
            dve.wait_ge(chosen_ready, 2 * m + 1)
            v.tensor_copy(ids_all[:, bass.ds(m * TOP * G4, TOP * G4)].rearrange("p (k q) -> p k q", k=TOP),
                          topf[:, :, 0:TOP].rearrange("p q k -> p k q"))
            v.tensor_copy(tw_all[:, bass.ds(m * TOP * G4, TOP * G4)], tw[:].rearrange("p a b -> p (a b)"))
            v.tensor_tensor(both[:, 0:G4], chosen[:, 0], chosen[:, 1], ALU.add).then_inc(chosen_ready, 1)

        def positions(m, o, j_o):
            pl.at(m)
            dve.wait_ge(cnt_filled, m + 1)
            pl(v.tensor_tensor(slot[:], bank[4][:, 0:G4 * EXPERTS].rearrange("p (a b) -> p a b", b=EXPERTS), bcast(cnt[:], G4, 1), ALU.add))
            v.tensor_tensor(cnt[:], bank[4][:, G4 * EXPERTS:(G4 + 1) * EXPERTS], cnt[:], ALU.add)
            pl(v.tensor_tensor(picked[:].rearrange("p a b c -> p a (b c)"), chosen[:].rearrange("p a b c -> p a (b c)"),
                               bcast(slot[:].rearrange("p b c -> p (b c)"), TOP, 1), ALU.mult))
            pl(v.tensor_reduce(posf[:], picked[:].rearrange("p a b c -> p (a b) c"), AX_X, ALU.add))
            wait(dve, scattered[o], 16 * TOP * G4 * j_o)
            v.memset(carrier[:], 0.0)
            pl(v.tensor_copy(posf_all[:, bass.ds(m * TOP * G4, TOP * G4)], posf[:]))
            v.tensor_copy(posg[:, o], posf[:]).then_inc(pos_done, 1)

        def hidden(m, n):
            dve.wait_ge(tanh_done, 2 * m + n + 1)
            v.scalar_tensor_tensor(up[:], th[:], 1.0, bank[6][:], ALU.add, ALU.mult).then_inc(up_done, 1)
            dve.wait_ge(up_done, 2 * m + n + 1)
            wait(dve, w2_half, 2 * m)
            v.tensor_tensor(hid[:, n], up[:], bank[7][:], ALU.mult).then_inc(hid_done, 1)

        def accumulate(m):
            for q in range(G4):
                if q % 2 == 0:
                    dve.wait_ge(w2_half, 2 * m + q // 2 + 1)
                hs = tile_of(m, q)
                v.scalar_tensor_tensor(hs, bank[6 + q // 2][:, (q % 2) * D:(q % 2 + 1) * D], 0.5, hs, ALU.mult, ALU.add).then_inc(acc_done, 1)

        def body(it, j, half, live):
            g, g1_, g2_, g3_, o = it, it - 1, it - 2, it - 3, 1 - half
            if live(0): ln_stats(g)
            if live(1):
                row_max(g1_, 0)
                row_max(g1_, 1)
            if live(3): route_shift(g3_)
            if live(2):
                residual(g2_)
                residual_stats(g2_)
            if live(3): hidden(g3_, 0)
            if live(0): ln_apply(g)
            if live(3): hidden(g3_, 1)
            if live(0): scale_rows(g)
            if live(1): o_norm(g1_)
            if live(3): route_top(g3_)
            if live(2): scale_rows2(g2_, j - 1, half)
            if live(3):
                route_weights(g3_)
                accumulate(g3_)
            if live(3): positions(g3_, o, j - 2 + half)
        pipeline(dve, GROUPS, 3, body, peel=6)

        link = Links(dve, chain[0], 36, 1).at(0)
        dve.wait_ge(pos_done, GROUPS)
        link(v.tensor_scalar(padf[:], cnt[:], iota_p[:, 0:1], None, ALU.add))
        v.tensor_copy(pad[:], padf[:]).then_inc(pad_ready, 1)
        link(v.scalar_tensor_tensor(ntile[:], iota8[:], -float(REGION), cnt[:], ALU.mult, ALU.add))
        link(v.tensor_scalar(ntile[:], ntile[:], 1.0 / P, 0.5 - 0.5 / P, ALU.mult, ALU.add))
        link(v.tensor_scalar(ntile[:], ntile[:], ROUND_INT, None, ALU.add))
        link(v.tensor_scalar(ntile[:], ntile[:], ROUND_INT, None, ALU.subtract))
        v.tensor_copy(tiles_end[:, 0:1], ntile[:, 0:1])
        link(v.tensor_scalar(step[:], ntile[:], -float(P), float(REGION), ALU.mult, ALU.add))
        for e in range(1, EXPERTS):
            link(v.tensor_tensor(tiles_end[:, e:e + 1], tiles_end[:, e - 1:e], ntile[:, e:e + 1], ALU.add))
        passed = pt[0:1].rearrange("p a b -> p (a b)")[:, 0:TILES * EXPERTS].rearrange("p (a b) -> p a b", b=EXPERTS)
        steps = probs[0:1].rearrange("p a b -> p (a b)")[:, 0:TILES * EXPERTS].rearrange("p (a b) -> p a b", b=EXPERTS)
        link(v.tensor_tensor(passed, bcast(iota_tiles[:], EXPERTS, 2), bcast(tiles_end[0:1], TILES, 1), ALU.is_ge))
        v.tensor_tensor(steps, passed, bcast(step[0:1], TILES, 1), ALU.mult)
        link(v.tensor_reduce(tile_f[:, 0], passed, AX_X, ALU.add))
        link(v.tensor_reduce(tile_f[:, 1], steps, AX_X, ALU.add))
        v.tensor_scalar(tile_f[:, 0], tile_f[:, 0], float(EXPERTS - 1), None, ALU.min)
        link(v.scalar_tensor_tensor(tile_f[:, 1], iota_tiles[:], float(P), tile_f[:, 1], ALU.mult, ALU.add))
        v.tensor_copy(tile_i[:], tile_f[:]).then_inc(plan_ready, 1)
        link(v.tensor_tensor(shift[:], tiles_end[:], ntile[:], ALU.subtract))
        link(v.tensor_scalar(shift[:], shift[:], float(P), None, ALU.mult))
        link(v.scalar_tensor_tensor(shift[:], iota8[:], -float(REGION), shift[:], ALU.mult, ALU.add))
        for e in range(EXPERTS):
            link(v.tensor_scalar(moved[:], ids_all[:], float(e), shift[:, e:e + 1], ALU.is_equal, ALU.mult))
            link(v.tensor_tensor(posf_all[:], posf_all[:], moved[:], ALU.add))
        v.tensor_copy(pos_all[:, 0:SEQS * TOP], posf_all[:]).then_inc(plan_ready, 1)

    return specialists(ctx, block, shared, dict(
        x_rows=x, xt=nx, act_t=th, gated=up, hid=hid, hid_t=qt, y=nx2, w13=w13, w2=w2, g2=g2, tile_i=tile_i,
        sorted_x=sorted_x, sorted_y=sorted_y,
        ready=[(plan_ready, 2), (padded, 16 * EXPERTS), (scattered[0], 8 * 16 * GROUPS // 2), (scattered[1], 8 * 16 * GROUPS // 2),
               (acc_done, G4 * GROUPS), (s_w2, 16 * (2 + EXPERTS))]))


def specialists(ctx, block, shared, b):
    nc, ident, bank = (shared[k] for k in ("nc", "ident", "bank"))
    w13, w2, g2, tile_i, sorted_x, sorted_y = (b[k] for k in ("w13", "w2", "g2", "tile_i", "sorted_x", "sorted_y"))
    STEPS = TILES // 2
    x_rows = b["x_rows"][:].rearrange("p (s k d) -> p s k d", s=2, k=2)
    xt = b["xt"][:].rearrange("p (s c n) -> p s c n", s=2, c=DC)
    th = b["act_t"][:].rearrange("p (k n) -> p k n", k=2)
    gated = b["gated"][:].rearrange("p (k n) -> p k n", k=2)
    hid = b["hid"][:, 0].rearrange("p (k n) -> p k n", k=2)
    hid_t = b["hid_t"][:, 0].rearrange("p (c n) -> p c n", c=FC)
    y = b["y"][:, :, 0:2 * D].rearrange("p s (k d) -> p s k d", k=2)

    def sem(name):
        return ctx.enter_context(nc.semaphore("s_" + name))
    x_in, y_out = [sem(f"x_in{i}") for i in range(2)], [sem(f"y_out{i}") for i in range(2)]
    xt_filled, xt_evac, w13_done, tanh_done, gated_done, hid_done = (sem(n) for n in (
        "xt_filled", "xt_evac", "w13", "tanh", "gated", "hid"))
    ht_filled, ht_evac, w2_done, y_ready = sem("ht_filled"), sem("ht_evac"), sem("w2"), sem("y")

    def start(eng):
        for s, n in b["ready"]:
            eng.wait_ge(s, n)

    @block.sync
    def _(sp):
        start(sp)

        def rows(s, k):
            return sp.value_load(tile_i[0:1, 1, bass.ds(2 * s + k, 1)], min_val=0, max_val=SORTED_ROWS - P)

        def body(it, j, half, live):
            if live(0):
                first = [rows(it, k) for k in range(2)]
                wait(sp, xt_filled, it - 1)
                for k in range(2):
                    sp.dma_start(x_rows[:, half, k], sorted_x[bass.ds(first[k], P)]).then_inc(x_in[half], 16)
            if live(4):
                sp.wait_ge(y_ready, it - 3)
                for k in range(2):
                    sp.dma_start(sorted_y[bass.ds((2 * (it - 4) + k) * P, P)], y[:, half, k]).then_inc(y_out[half], 16)
        pipeline(sp, STEPS, 4, body)
        for i in range(2):
            sp.wait_ge(y_out[i], 32 * STEPS // 2)

    @block.gpsimd
    def _(pool):
        start(pool)

    @block.tensor
    def _(pe):
        t = nc.tensor
        start(pe)

        def expert(s, k):
            return pe.value_load(tile_i[0:1, 0, bass.ds(2 * s + k, 1)], min_val=0, max_val=EXPERTS - 1)

        def x_transposes(s, slot, n_in):
            pe.wait_ge(x_in[slot], 32 * n_in)
            wait(pe, xt_evac, 2 * s)
            for c in range(DC):
                for k in range(2):
                    ins = t.transpose(bank[0][:, (2 * c + k) * P:(2 * c + k + 1) * P], x_rows[:, slot, k, c * P:(c + 1) * P], ident[:])
            ins.then_inc(xt_filled, 1)

        def up_gate(s, slot, chosen):
            pe.wait_ge(xt_evac, 2 * s + 2)
            for k, e in enumerate(chosen):
                wait(pe, hid_done, 2 * (s - 1) + k + 1)
                for c in range(DC):
                    ins = t.matmul(bank[1 + k][:], xt[:, slot, c, k * P:(k + 1) * P], w13[:, c, bass.ds(e * 2 * FF, 2 * FF)],
                                   start=(c == 0), stop=(c == DC - 1))
                ins.then_inc(w13_done, 1)

        def h_transposes(s):
            for k in range(2):
                pe.wait_ge(hid_done, 2 * s + k + 1)
                wait(pe, ht_evac, s)
                for c in range(FC):
                    ins = t.transpose(bank[3][:, (2 * c + k) * P:(2 * c + k + 1) * P], hid[:, k, c * P:(c + 1) * P], ident[:])
            ins.then_inc(ht_filled, 1)

        def down(s, chosen):
            pe.wait_ge(ht_evac, s + 1)
            wait(pe, y_ready, s)
            for k, e in enumerate(chosen):
                for c in range(FC):
                    ins = t.matmul(bank[4][:, k * D:(k + 1) * D], hid_t[:, c, k * P:(k + 1) * P], w2[:, c, bass.ds(e * D, D)],
                                   start=(c == 0), stop=(c == FC - 1), skip_group_check=True)
            ins.then_inc(w2_done, 1)

        def body(it, j, half, live):
            if live(2): experts_up = [expert(it - 2, k) for k in range(2)]
            if live(3): experts_down = [expert(it - 3, k) for k in range(2)]
            if live(1): x_transposes(it - 1, 1 - half, j + half)
            if live(3): h_transposes(it - 3)
            if live(2): up_gate(it - 2, half, experts_up)
            if live(3): down(it - 3, experts_down)
        pipeline(pe, STEPS, 4, body)

    @block.scalar
    def _(act):
        a = nc.scalar
        start(act)

        def xt_copy(s, slot):
            act.wait_ge(xt_filled, s + 1)
            wait(act, w13_done, 2 * (s - 1))
            for c in range(DC):
                a.activation(xt[:, slot, c], bank[0][:, 2 * c * P:2 * (c + 1) * P], ACT.Copy, scale=g2[:, c:c + 1]).then_inc(xt_evac, 1)

        def gate_tanh(s):
            for k in range(2):
                act.wait_ge(w13_done, 2 * s + k + 1)
                wait(act, gated_done, 2 * (s - 1) + k + 1)
                a.activation(th[:, k], bank[1 + k][:, 0:FF], ACT.Tanh, scale=0.5).then_inc(tanh_done, 1)

        def y_copy(s, slot, n_out):
            act.wait_ge(w2_done, s + 1)
            wait(act, y_out[slot], 32 * n_out)
            a.activation(y[:, slot].rearrange("p k d -> p (k d)"), bank[4][:], ACT.Copy).then_inc(y_ready, 1)

        def body(it, j, half, live):
            if live(1): xt_copy(it - 1, 1 - half)
            if live(2): gate_tanh(it - 2)
            if live(3): y_copy(it - 3, 1 - half, j - 2 + half)
        pipeline(act, STEPS, 4, body, peel=6)

    @block.vector
    def _(dve):
        v = nc.vector
        start(dve)

        def ht_copy(s):
            dve.wait_ge(ht_filled, s + 1)
            wait(dve, w2_done, s)
            v.tensor_copy(hid_t.rearrange("p c n -> p (c n)"), bank[3][:]).then_inc(ht_evac, 1)

        def hidden(s):
            for k in range(2):
                dve.wait_ge(tanh_done, 2 * s + k + 1)
                wait(dve, hid_done, 2 * s + k)
                v.scalar_tensor_tensor(gated[:, k], th[:, k], 1.0, bank[1 + k][:, 0:FF], ALU.add, ALU.mult).then_inc(gated_done, 1)
                dve.wait_ge(gated_done, 2 * s + k + 1)
                wait(dve, ht_filled, s)
                v.tensor_tensor(hid[:, k], gated[:, k], bank[1 + k][:, FF:2 * FF], ALU.mult).then_inc(hid_done, 1)

        def body(it, j, half, live):
            if live(3): ht_copy(it - 3)
            if live(2): hidden(it - 2)
        pipeline(dve, STEPS, 4, body)

    return [(y_out[i], 32 * STEPS // 2) for i in range(2)]


PAIRS = SEQS // 2
HH, HD = 8, 32
RT = 4
H2 = 2 * HH
HSCALE = D ** -0.5
QB = 127.0
ROUND = 12582912.0
FLT_MAX = 3.4028235e38


def second_attention(ctx, block, shared, local, b_done, out):
    nc, dram, h, ident, bank = (shared[k] for k in ("nc", "dram", "h", "ident", "bank"))
    eps5, neghalf = shared["eps5"], shared["neghalf"]

    def sb(name, shape, dt=F32):
        return local.enter_context(nc.sbuf_tensor("c_" + name, shape, dt))

    def sem(name):
        return ctx.enter_context(nc.semaphore("c_" + name))

    W = 2 * D
    pos_all, tw_all, sorted_y = (shared[k] for k in ("pos_all", "tw_all", "sorted_y"))
    posc = sb("posc", [P, 2, 2, 2], U32)
    twc = sb("twc", [P, 2, 2])
    yg = sb("yg", [P, 2, 2, 2, D])
    pc_ready, gathered, added = sem("posc"), [sem(f"gathered{i}") for i in range(2)], sem("added")
    carried = shared["carried"]
    dummy = sb("dummy", [P, 1])
    wbd = sb("wbd", [P, 4, P])
    wo = sb("wo", [P, DC, D])
    pe_t = sb("pe_t", [P, DC, TOK])
    pp = sb("pp", [P, DC, TOK])
    bq, bk, bv = sb("bq", [P, 1]), sb("bk", [P, 1]), sb("bv", [P, 1])
    ub, vb_ = sb("ub", [P, DC]), sb("vb_", [P, DC])
    bqu, bqv = sb("bqu", [P, DC]), sb("bqv", [P, DC])
    bo, bo2 = sb("bo", [1, D]), sb("bo2", [1, D])
    ones = sb("ones", [1, P])
    gamma, beta = sb("gamma", [P, DC]), sb("beta", [P, DC])
    tern_i = sb("tern_i", [P, DC, D], I32)
    tern = sb("tern", [P, DC, D], BF16)
    fbias = sb("fbias", [P, D])
    scale, scale_c, scale_i = sb("scale", [P, 1]), sb("scale_c", [P, 1]), sb("scale_i", [P, 1])
    ident16 = shared["ident16"]
    carrier = sb("carrier", [P, 1])
    st = sb("st", [P, 3, 2, 6])
    mv = sb("mv", [P, 3, 2, 2])
    rtmp, rs = sb("rtmp", [P, 3, 2]), sb("rs", [P, 3, 2])
    x, xn = sb("x", [P, W]), sb("xn", [P, W])
    xnt = sb("xnt", [P, 2, DC, 2 * TOK])
    qu, kt = sb("qu", [P, 2, DC, 2 * TOK]), sb("kt", [P, 2, DC, 2 * TOK])
    qv = sb("qv", [P, DC, 2 * TOK])
    vv = sb("vv", [P, 2, W])
    posb = sb("posb", [P, H2, TOK + 1])
    shifted = sb("shifted", [P, 2, H2 * TOK])
    sc = sb("sc", [P, H2 * TOK])
    probs, pt = sb("probs", [P, H2 * TOK]), sb("pt", [P, H2 * TOK])
    smax, nbias, pinv = (sb(n, [P, H2]) for n in ("smax", "nbias", "pinv"))
    psums = sb("psums", [P, 2, H2])
    ob = sb("ob", [P, W])
    ot = sb("ot", [P, DC, 2 * TOK])
    h1 = sb("h1", [P, W])
    hb = sb("hb", [P, 2, W])
    y = sb("y", [P, W])
    yq, yt = sb("yq", [P, W], BF16), sb("yt", [P, DC, 2 * TOK], BF16)
    res = sb("res", [P, 2, W])
    scratch = nc.dram_tensor("scratch", (2, H2, TOK, TOK + 1), F32, kind="Internal").ap()

    s_w, s_z, s_pre, scale_bound = sem("weights"), sem("zero"), sem("pre"), sem("scale_bound")
    stat = [sem(f"stat{i}") for i in range(3)]
    rsr = [sem(f"rs{i}") for i in range(3)]
    xn_ready, xt_filled, xt_evac = sem("xn"), sem("xt_filled"), sem("xt_evac")
    q_filled, q_evac, k_filled, k_evac = sem("q_filled"), sem("q_evac"), sem("k_filled"), sem("k_evac")
    v_filled, v_evac = sem("v_filled"), sem("v_evac")
    pos_filled, pos_evac, c_filled, s_added = sem("pos_filled"), sem("pos_evac"), sem("c_filled"), sem("s_added")
    pos_out = [sem(f"pos_out{i}") for i in range(2)]
    shift_in = [sem(f"shift_in{i}") for i in range(2)]
    nb_ready, exp_done = sem("nb"), sem("exp")
    pt_filled, pt_evac_a, pt_evac_d, av_done, on_done = sem("pt_filled"), sem("pt_evac_act"), sem("pt_evac_dve"), sem("av"), sem("on")
    ot_filled, ot_evac, wo_done, h1_done, hb_done = sem("ot_filled"), sem("ot_evac"), sem("wo"), sem("h1"), sem("hb")
    yq_ready, yt_filled, yt_evac, f_done, res_done = sem("yq"), sem("yt_filled"), sem("yt_evac"), sem("ffn"), sem("res")
    out_sem = [sem(f"out{i}") for i in range(2)]

    LOADS = [(wbd[32 * r:32 * r + 32, i, 32 * r:32 * r + 32], dram[n])
             for i, n in enumerate(("c_wq", "c_wk", "c_wv", "c_wp")) for r in range(RT)] + [
        (wo[:], dram["c_wo"]), (pe_t[:], dram["c_pe"]), (bq[:], dram["c_bq"]), (bk[:], dram["c_bk"]), (bv[:], dram["c_bv"]),
        (ub[:], dram["c_u"]), (vb_[:], dram["c_v"]), (bo[:], dram["c_bo"]), (gamma[:], dram["c_gamma"]), (beta[:], dram["c_beta"]),
        (tern_i[:], dram["c_tern"]), (fbias[:], dram["c_fbias"].partition_broadcast(P)),
        (scale[:], dram["c_scale"].partition_broadcast(P)),
    ]
    NL = 16 * len(LOADS)

    @block.sync
    def _(sp):
        for s, n in b_done:
            sp.wait_ge(s, n)
        sp.wait_ge(s_z, 1)
        for dst, src in LOADS:
            sp.dma_start(dst, src).then_inc(s_w, 16)

        def body(it, j, half, live):
            s1, s4, o = it - 1, it - 4, 1 - half
            j1 = j if half else j - 1
            if live(1):
                sp.wait_ge(pos_evac, 4 * s1 + 4)
                sp.dma_start(scratch[o].rearrange("i q k -> q i k"), posb[:]).then_inc(pos_out[o], 16)
            if live(4):
                sp.wait_ge(res_done, s4 + 1)
                sp.dma_start(out[bass.ds(2 * s4, 2)].rearrange("s t d -> t s d"),
                             res[:, half].rearrange("p (s d) -> p s d", s=2)).then_inc(out_sem[half], 16)
            if live(1):
                sp.wait_ge(pos_out[o], 16 * (j1 + 1))
                wait(sp, s_added, 4 * (s1 - 1))
                src = scratch[o].rearrange("i q k -> i (q k)")[:, TOK:].rearrange("i (q k) -> q i k", k=TOK)
                dst = shifted[:, o].rearrange("p (i k) -> p i k", k=TOK)
                for q in range(2):
                    sp.dma_start(dst[:, q * HH:(q + 1) * HH], src[:, q * HH:(q + 1) * HH]).then_inc(shift_in[o], 16)
        pipeline(sp, PAIRS, 4, body)
        for i in range(2):
            sp.wait_ge(out_sem[i], 16 * PAIRS // 2)
        sp.wait_ge(gathered[0], 64 * (PAIRS // 2 + 1))

    @block.gpsimd
    def _(pool):
        g = nc.gpsimd
        for s, n in b_done:
            pool.wait_ge(s, n)
        g.memset(ones[:], 1.0)
        g.memset(posb[:, :, 0:1], 0.0)
        g.memset(wbd[:], 0.0).then_inc(s_z, 1)
        lks = [Links(pool, shared["pool_chain"][n], 1, PAIRS) for n in range(3)]

        def rsqrt(n, s):
            pool.wait_ge(stat[n], s + 1)
            wait(pool, rsr[n], s)
            lks[n].at(s)(g.tensor_tensor(out=rtmp[:, n], in0=mv[:, n, :, 1], in1=eps5[:, 0:2], op=ALU.add))
            g.tensor_tensor(out=rs[:, n], in0=rtmp[:, n], in1=neghalf[:, 0:2], op=ALU.pow).then_inc(rsr[n], 1)

        def gather(s, slot):
            pool.wait_ge(pc_ready, s + 1)
            wait(pool, carried, GROUPS + s)
            g.tensor_tensor(out=dummy[:], in0=eps5[:, 0:1], in1=neghalf[:, 0:1], op=ALU.add).then_inc(carried, 1)
            for k in range(2):
                for i in range(2):
                    g.indirect_dma_start(yg[:, slot, k, i], None, sorted_y,
                                         bass.IndirectOffsetOnAxis(posc[:, slot, k, i:i + 1], 0)).then_inc(gathered[slot], 16)
        gather(0, 0)

        def body(it, j, half, live):
            if live(0):
                gather(it + 1, 1 - half)
                rsqrt(0, it)
                rsqrt(1, it)
            if live(3):
                s3 = it - 3
                rsqrt(2, s3)
                wait(pool, res_done, s3 - 1)
                if isinstance(s3, int) and s3 == 0:
                    pool.wait_ge(s_w, NL)
                for q in range(2):
                    ins = g.tensor_tensor(out=hb[:, 1 - half, q * D:(q + 1) * D], in0=h1[:, q * D:(q + 1) * D], in1=fbias[:], op=ALU.add)
                ins.then_inc(hb_done, 1)
        pipeline(pool, PAIRS, 4, body, peel=6)

    @block.tensor
    def _(pe):
        t = nc.tensor
        for s, n in b_done:
            pe.wait_ge(s, n)
        pe.wait_ge(s_w, NL)
        for c in range(DC):
            t.matmul(bank[4][:, c * TOK:(c + 1) * TOK], wbd[:, 3], pe_t[:, c], start=True, stop=True, skip_group_check=True)
        for c in range(DC):
            t.matmul(bank[5][0:1, 0:D], bv[:], wo[:, c], start=(c == 0), stop=False)
        t.matmul(bank[5][0:1, 0:D], ones[0:1, 0:1], bo[:], start=False, stop=True).then_inc(s_pre, 1)
        pe.wait_ge(s_pre, 3)

        def col(q, c, n=P):
            return slice((2 * q + c) * TOK, (2 * q + c + 1) * TOK)

        def x_transposes(s):
            pe.wait_ge(xn_ready, s + 1)
            wait(pe, v_evac, s - 1)
            for c in range(DC):
                for q in range(2):
                    ins = t.transpose(bank[6][:, c * 2 * TOK + q * TOK:c * 2 * TOK + (q + 1) * TOK],
                                      xn[:, q * D + c * P:q * D + (c + 1) * P], ident[:])
            ins.then_inc(xt_filled, 1)

        def project(s, o, w, filled, waits):
            for sm, val in waits:
                pe.wait_ge(sm, val)
            t.matmul(bank[6][:], wbd[:, w], xnt[:, o].rearrange("p a b -> p (a b)"), start=True, stop=True).then_inc(filled, 1)

        def v_proj(s, half):
            wait(pe, k_evac, s + 2, PAIRS)
            for q in range(2):
                for c in range(DC):
                    ins = t.matmul(bank[6][:, q * D + c * P:q * D + (c + 1) * P], xnt[:, half, c, q * TOK:(q + 1) * TOK],
                                   wbd[:, 2], start=True, stop=True, skip_group_check=True)
            ins.then_inc(v_filled, 1)

        def position_scores(s, o):
            pe.wait_ge(q_evac, 4 * s + 4)
            wait(pe, s_added, 4 * s)
            for q in range(2):
                for c in range(DC):
                    for r in range(RT):
                        rows = slice(32 * r, 32 * r + 32)
                        ins = t.matmul(bank[r][:, col(q, c)], qv[rows, c, q * TOK:(q + 1) * TOK], pp[rows, c],
                                       start=True, stop=True, skip_group_check=True)
                        if q == 1 and c == 1:
                            ins.then_inc(pos_filled, 1)

        def content_scores(s, half, q):
            if q == 0:
                pe.wait_ge(pos_evac, 4 * s + 4)
                pe.wait_ge(k_evac, s + 1)
            for c in range(DC):
                for r in range(RT):
                    rows, cols = slice(32 * r, 32 * r + 32), slice(q * TOK, (q + 1) * TOK)
                    ins = t.matmul(bank[r][:, col(q, c)], qu[rows, half, c, cols], kt[rows, half, c, cols],
                                   start=True, stop=True, skip_group_check=True)
                    if q == 1 and c == 1:
                        ins.then_inc(c_filled, 1)

        def p_transposes(s, k):
            if k == 0:
                pe.wait_ge(exp_done, s + 1)
            if k < 2:
                wait(pe, (pt_evac_a, pt_evac_d)[k], 2 * s)
                wait(pe, (yt_evac, res_done)[k], s - 1)
            else:
                pe.wait_ge((pt_evac_a, pt_evac_d)[k - 2], 2 * s + 1)
            for i in range(4):
                hd = 4 * k + i
                ins = t.transpose(bank[4 + k % 2][:, i * TOK:(i + 1) * TOK], probs[:, hd * TOK:(hd + 1) * TOK], ident[:])
            ins.then_inc(pt_filled, 1)

        def values(s, o):
            pe.wait_ge(pt_evac_a, 2 * s + 2)
            pe.wait_ge(pt_evac_d, 2 * s + 2)
            pe.wait_ge(v_evac, s + 1)
            wait(pe, h1_done, s)
            for hd in range(H2):
                ins = t.matmul(bank[7][:, hd * HD:(hd + 1) * HD], pt[:, hd * TOK:(hd + 1) * TOK],
                               vv[:, o, hd * HD:(hd + 1) * HD], start=True, stop=True, skip_group_check=True)
            ins.then_inc(av_done, 1)

        def o_transposes(s):
            pe.wait_ge(on_done, s + 1)
            for c in range(DC):
                for q in range(2):
                    ins = t.transpose(bank[7][:, c * 2 * TOK + q * TOK:c * 2 * TOK + (q + 1) * TOK],
                                      ob[:, q * D + c * P:q * D + (c + 1) * P], ident[:])
            ins.then_inc(ot_filled, 1)

        def y_transposes(s):
            pe.wait_ge(yq_ready, s + 1)
            wait(pe, pt_evac_a, 2 * s + 4, 2 * PAIRS)
            b16 = bank[4][:].bitcast(BF16)
            for c in range(DC):
                for q in range(2):
                    ins = t.transpose(b16[:, c * 2 * TOK + q * TOK:c * 2 * TOK + (q + 1) * TOK],
                                      yq[:, q * D + c * P:q * D + (c + 1) * P], ident16[:])
            ins.then_inc(yt_filled, 1)

        def ffn(s):
            pe.wait_ge(yt_evac, s + 1)
            wait(pe, pt_evac_d, 2 * s + 4, 2 * PAIRS)
            for q in range(2):
                for c in range(DC):
                    ins = t.matmul(bank[5][:, q * D:(q + 1) * D], yt[:, c, q * TOK:(q + 1) * TOK], tern[:, c],
                                   start=(c == 0), stop=(c == DC - 1), skip_group_check=True)
            ins.then_inc(f_done, 1)

        def out_proj(s):
            pe.wait_ge(ot_evac, s + 1)
            for q in range(2):
                for c in range(DC):
                    t.matmul(bank[7][:, q * D:(q + 1) * D], ot[:, c, q * TOK:(q + 1) * TOK], wo[:, c],
                             start=(c == 0), stop=False, skip_group_check=True)
                ins = t.matmul(bank[7][:, q * D:(q + 1) * D], ones[:], bo2[:], start=False, stop=True, skip_group_check=True)
            ins.then_inc(wo_done, 1)

        def body(it, j, half, live):
            s1, s2, s3, s4, o = it - 1, it - 2, it - 3, it - 4, 1 - half
            if live(1): x_transposes(s1)
            if live(3):
                p_transposes(s3, 0)
                p_transposes(s3, 1)
            if live(1): project(s1, o, 0, q_filled, [(xt_evac, 2 * s1 + 2)])
            if live(3):
                p_transposes(s3, 2)
                p_transposes(s3, 3)
            if live(2): content_scores(s2, half, 0)
            if live(1): project(s1, o, 1, k_filled, [(q_evac, 4 * s1 + 4)])
            if live(2): content_scores(s2, half, 1)
            if live(3): values(s3, o)
            if live(2): v_proj(s2, half)
            if live(1): position_scores(s1, o)
            if live(4): y_transposes(s4)
            if live(3): o_transposes(s3)
            if live(4): ffn(s4)
            if live(3): out_proj(s3)
        pipeline(pe, PAIRS, 4, body, peel=6)

    @block.scalar
    def _(act):
        a = nc.scalar
        for s, n in b_done:
            act.wait_ge(s, n)
        act.wait_ge(s_w, NL)
        act.wait_ge(s_pre, 4)

        def xt_copy(s, o):
            for c in range(DC):
                act.wait_ge(xt_filled, s + 1)
                wait(act, v_filled, s - 1)
                a.activation(xnt[:, o, c], bank[6][:, c * 2 * TOK:(c + 1) * 2 * TOK], ACT.Identity,
                             scale=gamma[:, c:c + 1], bias=beta[:, c:c + 1]).then_inc(xt_evac, 1)

        def q_copy(s, o):
            act.wait_ge(q_filled, s + 1)
            wait(act, pos_filled, 4 * s)
            wait(act, c_filled, 4 * (s - 1))
            for dst, bias in ((qu[:, o], bqu), (qv, bqv)):
                for c in range(DC):
                    a.activation(dst[:, c], bank[6][:, c * 2 * TOK:(c + 1) * 2 * TOK], ACT.Identity,
                                 bias=bias[:, c:c + 1]).then_inc(q_evac, 1)

        def pt_copy(s, k):
            act.wait_ge(pt_filled, 4 * s + k + 1)
            wait(act, av_done, s)
            a.activation(pt[:, 4 * k * TOK:4 * (k + 1) * TOK], bank[4 + k % 2][:], ACT.Copy).then_inc(pt_evac_a, 1)

        def pos_copy(s, r):
            act.wait_ge(pos_filled, 4 * s + r + 1)
            if r == 0:
                if isinstance(s, int):
                    for i in range(2):
                        wait(act, pos_out[i], 16 * ((s + 1 - i) // 2))
                else:
                    act.wait_ge(pos_out[pos_copy.other], 16 * pos_copy.count)
            dst = posb[:].rearrange("p (a r) k -> p a r k", r=RT)[:, :, r, 1:TOK + 1]
            a.activation(dst, bank[r][:].rearrange("p (a k) -> p a k", k=TOK), ACT.Copy).then_inc(pos_evac, 1)

        def ot_copy(s):
            act.wait_ge(ot_filled, s + 1)
            wait(act, wo_done, s)
            a.activation(ot[:].rearrange("p a b -> p (a b)"), bank[7][:], ACT.Copy).then_inc(ot_evac, 1)

        def yt_copy(s):
            act.wait_ge(yt_filled, s + 1)
            wait(act, f_done, s)
            a.activation(yt[:].rearrange("p a b -> p (a b)"), bank[4][:].bitcast(BF16)[:, 0:W], ACT.Copy).then_inc(yt_evac, 1)

        def exps(s, half):
            act.wait_ge(nb_ready, s + 1)
            wait(act, on_done, s - 1)
            wait(act, pt_filled, 4 * s)
            for i in range(H2):
                ins = a.activation(probs[:, i * TOK:(i + 1) * TOK], sc[:, i * TOK:(i + 1) * TOK], ACT.Exp,
                                   bias=nbias[:, i:i + 1], scale=HSCALE, accum_out=psums[:, half, i:i + 1])
            ins.then_inc(exp_done, 1)

        def body(it, j, half, live):
            s1, s2, s3, s4, o = it - 1, it - 2, it - 3, it - 4, 1 - half
            if live(1): xt_copy(s1, o)
            if live(3): pt_copy(s3, 0)
            if live(1): q_copy(s1, o)
            if live(3): pt_copy(s3, 2)
            if live(2): exps(s2, half)
            if live(1):
                pos_copy.other, pos_copy.count = half, j
                for r in range(RT):
                    pos_copy(s1, r)
            if live(4): yt_copy(s4)
            if live(3): ot_copy(s3)
        pipeline(act, PAIRS, 4, body, peel=6)

    @block.vector
    def _(dve):
        v = nc.vector
        for s, n in b_done:
            dve.wait_ge(s, n)
        dve.wait_ge(s_w, NL)
        v.tensor_tensor(bqu[:], ub[:], bcast(bq[:, 0], DC, 1), ALU.add)
        v.tensor_tensor(bqv[:], vb_[:], bcast(bq[:, 0], DC, 1), ALU.add)
        v.tensor_scalar(tern[:].rearrange("p a b -> p (a b)"), tern_i[:].rearrange("p a b -> p (a b)"), -1.0, None, ALU.add)
        v.tensor_scalar(scale_c[:], scale[:], 1e-5, FLT_MAX, ALU.max, ALU.min).then_inc(scale_bound, 1)
        dve.wait_ge(scale_bound, 1)
        v.reciprocal(scale_i[:], scale_c[:])
        dve.wait_ge(s_pre, 1)
        v.tensor_copy(pp[:].rearrange("p a b -> p (a b)"), bank[4][:, 0:DC * TOK]).then_inc(s_pre, 1)
        v.tensor_copy(bo2[:], bank[5][0:1, 0:D]).then_inc(s_pre, 1)
        v.memset(carrier[:], 0.0).then_inc(s_pre, 1)
        dve.wait_ge(s_pre, 4)

        chain = shared["dve_chain"]
        lf, lh, lt = Links(dve, chain[0], 6, PAIRS), Links(dve, chain[1], 2, PAIRS), Links(dve, chain[2], 4, PAIRS)
        ls, lo, lc = Links(dve, chain[3], 1, PAIRS), Links(dve, chain[4], 1, PAIRS), Links(dve, chain[5], 2, PAIRS)

        def pair(s):
            return h[:, bass.ds(s * W, W)]

        def stats(link, src, n):
            for q in range(2):
                ins = v.bn_stats(st[:, n, q], src[:, q * D:(q + 1) * D])
            link(ins)
            v.memset(carrier[:], 0.0)
            for q in range(2):
                ins = v.bn_aggr(mv[:, n, q], st[:, n, q])
            ins.then_inc(stat[n], 1)

        def normalise(dst, src, n):
            for q in range(2):
                ins = v.tensor_scalar(dst[:, q * D:(q + 1) * D], src[:, q * D:(q + 1) * D], mv[:, n, q, 0:1], rs[:, n, q:q + 1],
                                      ALU.subtract, ALU.mult)
            return ins

        def positions(s, j, half):
            wait(dve, added, s - 1)
            src = pos_all[:, bass.ds(j * 2 * G4, 2 * G4)].rearrange("p (k q) -> p k q", k=2)[:, :, 2 * half:2 * half + 2]
            v.tensor_copy(posc[:, half], src).then_inc(pc_ready, 1)
        positions(0, 0, 0)

        def combine(s, j, half):
            dve.wait_ge(gathered[half], 64 * (j + 1))
            src = tw_all[:, bass.ds(j * 2 * G4, 2 * G4)].rearrange("p (k q) -> p k q", k=2)[:, :, 2 * half:2 * half + 2]
            wait(dve, added, s)
            lc.at(s)(v.tensor_copy(twc[:], src))
            hs = pair(s)
            for k in range(2):
                for i in range(2):
                    hq = hs[:, i * D:(i + 1) * D]
                    ins = v.scalar_tensor_tensor(hq, yg[:, half, k, i], twc[:, k, i:i + 1], hq, ALU.mult, ALU.add)
                if k == 0:
                    lc(ins)
            ins.then_inc(added, 1)
            dve.wait_ge(added, s + 1)

        def front_a(s):
            lf.at(s)
            wait(dve, xn_ready, s)
            lf(v.memset(carrier[:], 0.0))
            lf(v.memset(carrier[:], 0.0))
            v.memset(carrier[:], 0.0)
            stats(lf, pair(s), 0)

        def front_b(s):
            dve.wait_ge(rsr[0], s + 1)
            lf(normalise(x, pair(s), 0))
            stats(lf, x, 1)

        def front_c(s):
            dve.wait_ge(rsr[1], s + 1)
            wait(dve, xt_filled, s)
            lf(v.memset(carrier[:], 0.0))
            normalise(xn, x, 1).then_inc(xn_ready, 1)

        def pt_copy(s, k):
            dve.wait_ge(pt_filled, 4 * s + k + 1)
            wait(dve, av_done, s)
            v.tensor_copy(pt[:, 4 * k * TOK:4 * (k + 1) * TOK], bank[4 + k % 2][:]).then_inc(pt_evac_d, 1)

        def k_copy(s, o):
            dve.wait_ge(k_filled, s + 1)
            wait(dve, c_filled, 4 * (s - 1))
            v.tensor_scalar(kt[:, o].rearrange("p a b -> p (a b)"), bank[6][:], bk[:, 0:1], None, ALU.add).then_inc(k_evac, 1)

        def v_copy(s, half):
            dve.wait_ge(v_filled, s + 1)
            wait(dve, av_done, s - 1)
            v.tensor_copy(vv[:, half], bank[6][:]).then_inc(v_evac, 1)

        def add_scores(s, half, j):
            ls.at(s)
            for r in range(RT):
                dve.wait_ge(c_filled, 4 * s + r + 1)
                if r == 0:
                    dve.wait_ge(shift_in[half], 32 * j)
                    wait(dve, exp_done, s)
                view = lambda b: b.rearrange("p (a r k) -> p a r k", r=RT, k=TOK)[:, :, r]
                v.tensor_tensor(view(sc[:]), bank[r][:].rearrange("p (a k) -> p a k", k=TOK), view(shifted[:, half]),
                                ALU.add).then_inc(s_added, 1)
            dve.wait_ge(s_added, 4 * s + 4)
            ls(v.tensor_reduce(smax[:], sc[:].rearrange("p (a k) -> p a k", k=TOK), AX_X, ALU.max))
            v.tensor_scalar(nbias[:], smax[:], -HSCALE, None, ALU.mult).then_inc(nb_ready, 1)

        def o_norm(s, o):
            dve.wait_ge(av_done, s + 1)
            wait(dve, on_done, s)
            lo.at(s)(v.reciprocal(pinv[:], psums[:, o]))
            wait(dve, ot_filled, s)
            v.tensor_tensor(ob[:].rearrange("p (a b) -> p a b", b=HD), bank[7][:].rearrange("p (a b) -> p a b", b=HD),
                            bcast(pinv[:], HD, 2), ALU.mult).then_inc(on_done, 1)

        def residual(s):
            dve.wait_ge(wo_done, s + 1)
            wait(dve, hb_done, s)
            v.tensor_tensor(h1[:], bank[7][:], pair(s), ALU.add).then_inc(h1_done, 1)
            dve.wait_ge(h1_done, s + 1)
            lh.at(s)(v.memset(carrier[:], 0.0))
            stats(lh, h1, 2)

        def quantise(s):
            dve.wait_ge(rsr[2], s + 1)
            lt.at(s)
            wait(dve, yq_ready, s)
            lt(normalise(y, h1, 2))
            lt(v.tensor_scalar(y[:], y[:], scale_i[:, 0:1], QB, ALU.mult, ALU.min))
            lt(v.tensor_scalar(y[:], y[:], -QB, ROUND, ALU.max, ALU.add))
            wait(dve, yt_filled, s)
            lt(v.memset(carrier[:], 0.0))
            v.tensor_scalar(yq[:], y[:], ROUND, None, ALU.subtract).then_inc(yq_ready, 1)

        def finish(s, half, j):
            dve.wait_ge(f_done, s + 1)
            dve.wait_ge(hb_done, s + 1)
            wait(dve, out_sem[half], 16 * (j - 2))
            v.scalar_tensor_tensor(res[:, half], bank[5][:], scale_c[:, 0:1], hb[:, half], ALU.mult, ALU.add).then_inc(res_done, 1)

        def body(it, j, half, live):
            s1, s2, s3, s4, o = it - 1, it - 2, it - 3, it - 4, 1 - half
            if live(3): pt_copy(s3, 1)
            if live(0):
                positions(it + 1, j + half, 1 - half)
                combine(it, j, half)
            if live(3): pt_copy(s3, 3)
            if live(0): front_a(it)
            if live(1): k_copy(s1, o)
            if live(4): quantise(s4)
            if live(2): add_scores(s2, half, j)
            if live(0): front_b(it)
            if live(3): o_norm(s3, o)
            if live(2): v_copy(s2, half)
            if live(0): front_c(it)
            if live(4): finish(s4, half, j)
            if live(3): residual(s3)
        pipeline(dve, PAIRS, 4, body, peel=6)


def layout(inputs):
    import numpy as np

    def a(name):
        return np.asarray(inputs[name])

    def rows(w):
        return np.moveaxis(w.reshape(-1, P, *w.shape[1:]), 0, 1)
    freq = (np.float32(1.0) / np.float32(10000.0) ** (np.arange(0, AD, 2, dtype=np.float32) / np.float32(AD))).astype(np.float32)
    ang = np.arange(TOK, dtype=np.float32)[:, None] * freq
    cos, sin = np.cos(ang).astype(np.float32), np.sin(ang).astype(np.float32)
    div = np.exp(np.arange(0, D, 2, dtype=np.float32) * np.float32(-np.log(10000.0) / D)).astype(np.float32)
    pe = np.zeros((TOK, D), np.float32)
    pe[:, 0::2] = np.sin(np.arange(TOK, dtype=np.float32)[:, None] * div)
    pe[:, 1::2] = np.cos(np.arange(TOK, dtype=np.float32)[:, None] * div)
    arrays = {
        "idm": np.stack([a("x"), a("mask_BS_i1_0")], 1),
        "ident": np.eye(P, dtype=np.float32),
        "vocab_id": np.tile(np.arange(32, dtype=np.float32), 2)[:, None],
        "causal": np.where(np.tril(np.ones((TOK, TOK), bool)), 0.0, -1e30).astype(np.float32),
        "rope": np.stack([np.concatenate([cos, cos], 1), np.concatenate([-sin, sin], 1)], 1),
        "emb_t": a("L0_tok_emb").T, "pca_t": a("L0_tok_pca_lookup").T, "proj_w": a("L0_tok_proj_w"),
        "proj_b": a("L0_tok_proj_b").reshape(DC, P).T, "fus_w": a("L0_tok_fus_w"), "fus_b": a("L0_tok_fus_b")[None],
        "ln_g": a("L0_tok_ln_g"), "ln_b": a("L0_tok_ln_b"),
        "qk_norm": np.stack([a("L0_attn_q_norm_w"), a("L0_attn_k_norm_w")]),
        "l_wq": rows(a("L0_ffn_Wq").T), "l_wk": rows(a("L0_ffn_Wkc").T), "l_wv": rows(a("L0_ffn_Wvc").T),
        "l_wo": rows(a("L0_ffn_Wo").T), "l_wr": rows(a("L0_ffn_Wr").T),
        "l_g1": a("L0_ffn_g1").reshape(DC, P).T, "l_g2": a("L0_ffn_g2").reshape(DC, P).T,
        "l_rbias": a("L0_ffn_expert_bias"), "iota8": np.arange(EXPERTS, dtype=np.float32),
        "l_sw1": rows(a("L0_ffn_sW1").T), "l_sw3": rows(a("L0_ffn_sW3").T), "l_sw2": rows(a("L0_ffn_sW2").T),
        "l_ew13": rows(np.concatenate([a("L0_ffn_eW1"), a("L0_ffn_eW3")], 1).reshape(-1, D).T),
        "iota_p": np.arange(P, dtype=np.float32)[:, None], "iota_tiles": np.arange(TILES, dtype=np.float32)[None],
        "before": np.triu(np.ones((P, P), np.float32), 1),
        "l_ew2": rows(a("L0_ffn_eW2").transpose(2, 0, 1)),
        "c_wq": a("L1_attn_Wq"), "c_wk": a("L1_attn_Wk"), "c_wv": a("L1_attn_Wv"), "c_wp": a("L1_attn_Wp"),
        "c_wo": rows(a("L1_attn_Wo")), "c_pe": rows(np.ascontiguousarray(pe.T)),
        "c_bq": np.tile(a("L1_attn_bq"), RT)[:, None], "c_bk": np.tile(a("L1_attn_bk"), RT)[:, None],
        "c_bv": np.tile(a("L1_attn_bv"), RT)[:, None],
        "c_u": a("L1_attn_u_bias").reshape(DC, P).T, "c_v": a("L1_attn_v_bias").reshape(DC, P).T,
        "c_bo": a("L1_attn_bo")[None], "c_gamma": a("L1_attn_ln_gamma").reshape(DC, P).T,
        "c_beta": a("L1_attn_ln_beta").reshape(DC, P).T, "c_tern": rows(a("L1_ffn_ternary_weight").T),
        "c_fbias": a("L1_ffn_bias"), "c_scale": a("L1_ffn_act_scale").reshape(1),
        "wqkv_t": a("L0_attn_wqkv").T, "wo_t": a("L0_attn_wo").T,
    }
    return {k: np.ascontiguousarray(v) for k, v in arrays.items()}


def kernel(**inputs):
    import numpy as _np
    import concourse.bacc as _bacc
    from concourse import mybir as _mybir
    from concourse.bass_utils import run_bass_kernel_spmd as _run

    nc = _bacc.Bacc("TRN2", target_bir_lowering=False, num_devices=1)
    arrays = layout(inputs)
    dram = {k: nc.dram_tensor("in_" + k, v.shape, _mybir.dt.from_np(v.dtype), kind="ExternalInput").ap() for k, v in arrays.items()}
    out = nc.dram_tensor("out", (SEQS, TOK, D), F32, kind="ExternalOutput").ap()
    program(nc, dram, out)
    r = _run(nc, [{"in_" + k: v for k, v in arrays.items()}], core_ids=[0])
    return r.results[0]["out"]
```
